# Optimizing a Trainium2 kernel written in Bass

```python
import numpy as np
import jax
import jax.numpy as jnp

def _softmax(x, axis=-1):
    return jax.nn.softmax(x, axis=axis)

def _gelu(x):
    return jax.nn.gelu(x, approximate=True)

def _silu(x):
    return jax.nn.silu(x)

def _sigmoid(x):
    return jax.nn.sigmoid(x)

def _layernorm(x, axis=-1, eps=1e-05):
    m = jnp.mean(x, axis=axis, keepdims=True)
    v = jnp.var(x, axis=axis, keepdims=True)
    return (x - m) / jnp.sqrt(v + eps)

def _scatter_add(tgt, idx, src, axis=0):
    return tgt.at[idx].add(src)

def _segment_sum(src, seg, n):
    return jax.ops.segment_sum(src, seg, n)
kernel_name = 'mk_gnn_resnorm_d4_gnn_r32_d3034b'

def setup_inputs(seed: int=0):
    np.random.seed(seed)
    _w = jnp.asarray

    def _rec_inputs():
        import jax
        import jax.numpy as jnp
        _gk = jax.random.key(seed)
        x = -0.000202 + 1 * jax.random.normal(jax.random.fold_in(_gk, 1), (3125, 128), jnp.float32)
        src = jax.random.randint(jax.random.fold_in(_gk, 2), (100000,), 0, 3125, jnp.int32)
        dst = jax.random.randint(jax.random.fold_in(_gk, 3), (100000,), 0, 3125, jnp.int32)
        _o = jnp.argsort(dst, stable=True)
        src = src[_o]
        dst = dst[_o]
        edge_weight = jax.random.uniform(jax.random.fold_in(_gk, 12), (100000,), jnp.float32, 0.0, 0.999998)
        return (x, src, dst, edge_weight)
    x, src, dst, edge_weight = _rec_inputs()

    def _L0_gnn_setup():
        import jax, jax.numpy as jnp
        import numpy as np
        N_NODES = 50000
        N_EDGES = 18750
        DIM = 128
        N_LAYERS = 3
        BN_EPS = 1e-05
        key = jax.random.key(seed)
        ks = jax.random.split(key, 8)
        x = jax.random.normal(ks[0], (N_NODES, DIM), dtype=jnp.float32)
        edge_index = jax.random.randint(ks[1], (2, N_EDGES), 0, N_NODES, dtype=jnp.int64)
        s = 1.0 / np.sqrt(DIM)
        W1 = jax.random.normal(ks[2], (N_LAYERS, DIM, DIM), dtype=jnp.float32) * s
        b1 = jax.random.normal(ks[3], (N_LAYERS, DIM), dtype=jnp.float32) * s
        W2 = jax.random.normal(ks[4], (N_LAYERS, DIM, DIM), dtype=jnp.float32) * s
        b2 = jax.random.normal(ks[5], (N_LAYERS, DIM), dtype=jnp.float32) * s
        gamma = jnp.ones((N_LAYERS, DIM), dtype=jnp.float32)
        beta = jnp.zeros((N_LAYERS, DIM), dtype=jnp.float32)
        return {'x': x, 'edge_index': edge_index, 'W1': W1, 'b1': b1, 'W2': W2, 'b2': b2, 'gamma': gamma, 'beta': beta}
    _L0_gnn_all = _L0_gnn_setup()
    _L0_gnn_in = {k: v for k, v in _L0_gnn_all.items() if k in ('W1', 'b1', 'W2', 'b2', 'gamma', 'beta')}
    del _L0_gnn_all

    def _L1_gnn_setup():
        import jax, jax.numpy as jnp
        import numpy as np
        N = 50000
        E = 25000
        IN = 128
        HID = 32
        HEADS = 4
        EMB = 128
        LAYERS = 3
        NEG_SLOPE = 0.2

        def _layer_norm(x, g, b):
            mu = jnp.mean(x, axis=-1, keepdims=True)
            var = jnp.var(x, axis=-1, keepdims=True)
            return g * (x - mu) / jnp.sqrt(var + 1e-05) + b

        def _gatv2(h, src, dst, n, Wl, bl, Wr, br, att, bias):
            H, C = att.shape
            xl = (h @ Wl + bl).reshape(n, H, C)
            xr = (h @ Wr + br).reshape(n, H, C)
            x_i = xl[dst]
            x_j = xr[src]
            e = jax.nn.leaky_relu(x_i + x_j, NEG_SLOPE)
            logit = jnp.einsum('ehc,hc->eh', e, att)
            m = jax.ops.segment_max(logit, dst, num_segments=n)
            ex = jnp.exp(logit - m[dst])
            den = jax.ops.segment_sum(ex, dst, num_segments=n)
            alpha = ex / (den[dst] + 1e-16)
            out = jax.ops.segment_sum(alpha[..., None] * x_j, dst, num_segments=n)
            return out.reshape(n, H * C) + bias
        key = jax.random.key(seed)
        ks = iter(jax.random.split(key, 64))
        d = {}
        d['x'] = jax.random.normal(next(ks), (N, IN), jnp.float32)
        d['edge_index'] = jax.random.randint(next(ks), (2, E), 0, N, dtype=jnp.int64)

        def w(shape, fan):
            return jax.random.normal(next(ks), shape, jnp.float32) / np.float32(np.sqrt(fan))
        HC = HID * HEADS
        d['W_in'] = w((IN, HID), IN)
        d['b_in'] = jnp.zeros((HID,), jnp.float32)
        for i in range(LAYERS):
            ic = HID if i == 0 else HC
            d[f'Wl{i}'] = w((ic, HC), ic)
            d[f'bl{i}'] = jnp.zeros((HC,), jnp.float32)
            d[f'Wr{i}'] = w((ic, HC), ic)
            d[f'br{i}'] = jnp.zeros((HC,), jnp.float32)
            d[f'att{i}'] = w((HEADS, HID), HID)
            d[f'bo{i}'] = jnp.zeros((HC,), jnp.float32)
            d[f'g{i}'] = jnp.ones((HC,), jnp.float32)
            d[f'be{i}'] = jnp.zeros((HC,), jnp.float32)
        d['W_out'] = w((HC, EMB), HC)
        d['b_out'] = jnp.zeros((EMB,), jnp.float32)
        return d
    _L1_gnn_all = _L1_gnn_setup()
    _L1_gnn_in = {k: v for k, v in _L1_gnn_all.items() if k in ('W_in', 'b_in', 'Wl0', 'bl0', 'Wr0', 'br0', 'att0', 'bo0', 'g0', 'be0', 'Wl1', 'bl1', 'Wr1', 'br1', 'att1', 'bo1', 'g1', 'be1', 'Wl2', 'bl2', 'Wr2', 'br2', 'att2', 'bo2', 'g2', 'be2', 'W_out', 'b_out')}
    del _L1_gnn_all

    def _L2_gnn_setup():
        import jax, jax.numpy as jnp
        import numpy as np
        from jax.ops import segment_sum
        N = 3125
        M = 625
        E = 50000
        D_IN = 128
        D_OUT = 128
        key = jax.random.key(seed)
        k1, k2, k3, k4, k5, k6 = jax.random.split(key, 6)
        x = jax.random.normal(k1, (N, D_IN), dtype=jnp.float32)
        node_idx = jax.random.randint(k2, (E,), 0, N)
        he_idx = jax.random.randint(k3, (E,), 0, M)
        hyperedge_index = jnp.stack([node_idx, he_idx], axis=0)
        hyperedge_weight = jax.random.uniform(k4, (M,), dtype=jnp.float32)
        W = jax.random.normal(k5, (D_OUT, D_IN), dtype=jnp.float32) / np.sqrt(D_IN)
        b = jax.random.normal(k6, (D_OUT,), dtype=jnp.float32) * 0.01
        return {'x': x, 'hyperedge_index': hyperedge_index, 'hyperedge_weight': hyperedge_weight, 'W': W, 'b': b}
    _L2_gnn_all = _L2_gnn_setup()
    _L2_gnn_in = {k: v for k, v in _L2_gnn_all.items() if k in ('hyperedge_weight', 'W', 'b')}
    del _L2_gnn_all

    def _L3_gnn_setup():
        import jax, jax.numpy as jnp
        import numpy as np
        HIDDEN = 128
        N_NODES = 10000
        N_EDGES = 20000

        def _layer_norm(h, g, b, eps=1e-05):
            mu = jnp.mean(h, axis=-1, keepdims=True)
            var = jnp.var(h, axis=-1, keepdims=True)
            return (h - mu) * jax.lax.rsqrt(var + eps) * g + b
        key = jax.random.key(seed)
        ks = jax.random.split(key, 12)
        s = 0.05
        inp = {'x': jax.random.normal(ks[0], (N_NODES, HIDDEN), dtype=jnp.float32), 'edge_index': jax.random.randint(ks[1], (2, N_EDGES), 0, N_NODES, dtype=jnp.int32), 'edge_weight': jax.random.uniform(ks[2], (N_EDGES,), dtype=jnp.float32), 'mW1': jax.random.normal(ks[3], (2 * HIDDEN + 1, HIDDEN), dtype=jnp.float32) * s, 'mb1': jnp.zeros((HIDDEN,), dtype=jnp.float32), 'mW2': jax.random.normal(ks[4], (HIDDEN, HIDDEN), dtype=jnp.float32) * s, 'mb2': jnp.zeros((HIDDEN,), dtype=jnp.float32), 'uW1': jax.random.normal(ks[5], (2 * HIDDEN, HIDDEN), dtype=jnp.float32) * s, 'ub1': jnp.zeros((HIDDEN,), dtype=jnp.float32), 'ln_g': jnp.ones((HIDDEN,), dtype=jnp.float32), 'ln_b': jnp.zeros((HIDDEN,), dtype=jnp.float32), 'uW2': jax.random.normal(ks[6], (HIDDEN, HIDDEN), dtype=jnp.float32) * s, 'ub2': jnp.zeros((HIDDEN,), dtype=jnp.float32)}
        return inp
    _L3_gnn_all = _L3_gnn_setup()
    _L3_gnn_in = {k: v for k, v in _L3_gnn_all.items() if k in ('mW1', 'mb1', 'mW2', 'mb2', 'uW1', 'ub1', 'ln_g', 'ln_b', 'uW2', 'ub2')}
    del _L3_gnn_all
    return {'x': x, 'src': src, 'dst': dst, 'edge_weight': edge_weight, 'L0_gnn_W1': _L0_gnn_in['W1'], 'L0_gnn_b1': _L0_gnn_in['b1'], 'L0_gnn_W2': _L0_gnn_in['W2'], 'L0_gnn_b2': _L0_gnn_in['b2'], 'L0_gnn_gamma': _L0_gnn_in['gamma'], 'L0_gnn_beta': _L0_gnn_in['beta'], 'L1_gnn_W_in': _L1_gnn_in['W_in'], 'L1_gnn_b_in': _L1_gnn_in['b_in'], 'L1_gnn_Wl0': _L1_gnn_in['Wl0'], 'L1_gnn_bl0': _L1_gnn_in['bl0'], 'L1_gnn_Wr0': _L1_gnn_in['Wr0'], 'L1_gnn_br0': _L1_gnn_in['br0'], 'L1_gnn_att0': _L1_gnn_in['att0'], 'L1_gnn_bo0': _L1_gnn_in['bo0'], 'L1_gnn_g0': _L1_gnn_in['g0'], 'L1_gnn_be0': _L1_gnn_in['be0'], 'L1_gnn_Wl1': _L1_gnn_in['Wl1'], 'L1_gnn_bl1': _L1_gnn_in['bl1'], 'L1_gnn_Wr1': _L1_gnn_in['Wr1'], 'L1_gnn_br1': _L1_gnn_in['br1'], 'L1_gnn_att1': _L1_gnn_in['att1'], 'L1_gnn_bo1': _L1_gnn_in['bo1'], 'L1_gnn_g1': _L1_gnn_in['g1'], 'L1_gnn_be1': _L1_gnn_in['be1'], 'L1_gnn_Wl2': _L1_gnn_in['Wl2'], 'L1_gnn_bl2': _L1_gnn_in['bl2'], 'L1_gnn_Wr2': _L1_gnn_in['Wr2'], 'L1_gnn_br2': _L1_gnn_in['br2'], 'L1_gnn_att2': _L1_gnn_in['att2'], 'L1_gnn_bo2': _L1_gnn_in['bo2'], 'L1_gnn_g2': _L1_gnn_in['g2'], 'L1_gnn_be2': _L1_gnn_in['be2'], 'L1_gnn_W_out': _L1_gnn_in['W_out'], 'L1_gnn_b_out': _L1_gnn_in['b_out'], 'L2_gnn_hyperedge_weight': _L2_gnn_in['hyperedge_weight'], 'L2_gnn_W': _L2_gnn_in['W'], 'L2_gnn_b': _L2_gnn_in['b'], 'L3_gnn_mW1': _L3_gnn_in['mW1'], 'L3_gnn_mb1': _L3_gnn_in['mb1'], 'L3_gnn_mW2': _L3_gnn_in['mW2'], 'L3_gnn_mb2': _L3_gnn_in['mb2'], 'L3_gnn_uW1': _L3_gnn_in['uW1'], 'L3_gnn_ub1': _L3_gnn_in['ub1'], 'L3_gnn_ln_g': _L3_gnn_in['ln_g'], 'L3_gnn_ln_b': _L3_gnn_in['ln_b'], 'L3_gnn_uW2': _L3_gnn_in['uW2'], 'L3_gnn_ub2': _L3_gnn_in['ub2']}

def reference(x, src, dst, edge_weight, L0_gnn_W1, L0_gnn_b1, L0_gnn_W2, L0_gnn_b2, L0_gnn_gamma, L0_gnn_beta, L1_gnn_W_in, L1_gnn_b_in, L1_gnn_Wl0, L1_gnn_bl0, L1_gnn_Wr0, L1_gnn_br0, L1_gnn_att0, L1_gnn_bo0, L1_gnn_g0, L1_gnn_be0, L1_gnn_Wl1, L1_gnn_bl1, L1_gnn_Wr1, L1_gnn_br1, L1_gnn_att1, L1_gnn_bo1, L1_gnn_g1, L1_gnn_be1, L1_gnn_Wl2, L1_gnn_bl2, L1_gnn_Wr2, L1_gnn_br2, L1_gnn_att2, L1_gnn_bo2, L1_gnn_g2, L1_gnn_be2, L1_gnn_W_out, L1_gnn_b_out, L2_gnn_hyperedge_weight, L2_gnn_W, L2_gnn_b, L3_gnn_mW1, L3_gnn_mb1, L3_gnn_mW2, L3_gnn_mb2, L3_gnn_uW1, L3_gnn_ub1, L3_gnn_ln_g, L3_gnn_ln_b, L3_gnn_uW2, L3_gnn_ub2):
    import jax
    import jax.numpy as jnp

    def _L0_gnn_ref(x, edge_index, W1, b1, W2, b2, gamma, beta):
        import jax, jax.numpy as jnp
        import numpy as np
        N_NODES = 50000
        N_EDGES = 18750
        DIM = 128
        N_LAYERS = 3
        BN_EPS = 1e-05
        n = x.shape[0]
        row, col = (edge_index[0], edge_index[1])
        for i in range(N_LAYERS):
            agg = jax.ops.segment_sum(x[col], row, num_segments=n)
            h = x + agg
            h = jnp.maximum(h @ W1[i] + b1[i], 0.0)
            h = h @ W2[i] + b2[i]
            mean = jnp.mean(h, axis=0)
            var = jnp.var(h, axis=0)
            x = gamma[i] * (h - mean) * jax.lax.rsqrt(var + BN_EPS) + beta[i]
        return x

    def _L1_gnn_ref(x, edge_index, W_in, b_in, Wl0, bl0, Wr0, br0, att0, bo0, g0, be0, Wl1, bl1, Wr1, br1, att1, bo1, g1, be1, Wl2, bl2, Wr2, br2, att2, bo2, g2, be2, W_out, b_out):
        import jax, jax.numpy as jnp
        import numpy as np
        N = 50000
        E = 25000
        IN = 128
        HID = 32
        HEADS = 4
        EMB = 128
        LAYERS = 3
        NEG_SLOPE = 0.2

        def _layer_norm(x, g, b):
            mu = jnp.mean(x, axis=-1, keepdims=True)
            var = jnp.var(x, axis=-1, keepdims=True)
            return g * (x - mu) / jnp.sqrt(var + 1e-05) + b

        def _gatv2(h, src, dst, n, Wl, bl, Wr, br, att, bias):
            H, C = att.shape
            xl = (h @ Wl + bl).reshape(n, H, C)
            xr = (h @ Wr + br).reshape(n, H, C)
            x_i = xl[dst]
            x_j = xr[src]
            e = jax.nn.leaky_relu(x_i + x_j, NEG_SLOPE)
            logit = jnp.einsum('ehc,hc->eh', e, att)
            m = jax.ops.segment_max(logit, dst, num_segments=n)
            ex = jnp.exp(logit - m[dst])
            den = jax.ops.segment_sum(ex, dst, num_segments=n)
            alpha = ex / (den[dst] + 1e-16)
            out = jax.ops.segment_sum(alpha[..., None] * x_j, dst, num_segments=n)
            return out.reshape(n, H * C) + bias
        n = x.shape[0]
        loops = jnp.arange(n, dtype=edge_index.dtype)
        src = jnp.concatenate([edge_index[0], loops])
        dst = jnp.concatenate([edge_index[1], loops])
        h = jax.nn.gelu(x @ W_in + b_in, approximate=False)
        layers = [(Wl0, bl0, Wr0, br0, att0, bo0, g0, be0), (Wl1, bl1, Wr1, br1, att1, bo1, g1, be1), (Wl2, bl2, Wr2, br2, att2, bo2, g2, be2)]
        for Wl, bl, Wr, br, att, bo, g, be in layers:
            h_new = jax.nn.gelu(_layer_norm(_gatv2(h, src, dst, n, Wl, bl, Wr, br, att, bo), g, be), approximate=False)
            h = h + h_new if h.shape == h_new.shape else h_new
        out = h @ W_out + b_out
        norm = jnp.maximum(jnp.linalg.norm(out, axis=-1, keepdims=True), 1e-12)
        return out / norm

    def _L2_gnn_ref(x, hyperedge_index, hyperedge_weight, W, b):
        import jax, jax.numpy as jnp
        import numpy as np
        from jax.ops import segment_sum
        N = 3125
        M = 625
        E = 50000
        D_IN = 128
        D_OUT = 128
        node_idx = hyperedge_index[0]
        he_idx = hyperedge_index[1]
        num_nodes = x.shape[0]
        num_he = hyperedge_weight.shape[0]
        d_e = segment_sum(jnp.ones_like(he_idx, dtype=x.dtype), he_idx, num_segments=num_he)
        d_e = jnp.clip(d_e, 1.0, None)
        d_v = segment_sum(hyperedge_weight[he_idx], node_idx, num_segments=num_nodes)
        d_v = jnp.clip(d_v, 1.0, None)
        d_v_inv_sqrt = d_v ** (-0.5)
        x_prime = x * d_v_inv_sqrt[:, None]
        he_feat = segment_sum(x_prime[node_idx], he_idx, num_segments=num_he)
        he_feat = he_feat * (hyperedge_weight / d_e)[:, None]
        out = segment_sum(he_feat[he_idx], node_idx, num_segments=num_nodes)
        out = out * d_v_inv_sqrt[:, None]
        return out @ W.T + b

    def _L3_gnn_ref(x, edge_index, edge_weight, mW1, mb1, mW2, mb2, uW1, ub1, ln_g, ln_b, uW2, ub2):
        import jax, jax.numpy as jnp
        import numpy as np
        HIDDEN = 128
        N_NODES = 10000
        N_EDGES = 20000

        def _layer_norm(h, g, b, eps=1e-05):
            mu = jnp.mean(h, axis=-1, keepdims=True)
            var = jnp.var(h, axis=-1, keepdims=True)
            return (h - mu) * jax.lax.rsqrt(var + eps) * g + b
        num_nodes = x.shape[0]
        src_idx, dst_idx = (edge_index[0], edge_index[1])
        src_f = x[src_idx]
        dst_f = x[dst_idx]
        ew = edge_weight[:, None]
        msg_in = jnp.concatenate([src_f, dst_f, ew], axis=-1)
        h = jax.nn.silu(msg_in @ mW1 + mb1)
        messages = (h @ mW2 + mb2) * ew
        aggregated = jax.ops.segment_sum(messages, dst_idx, num_segments=num_nodes)
        upd_in = jnp.concatenate([x, aggregated], axis=-1)
        u = jax.nn.silu(_layer_norm(upd_in @ uW1 + ub1, ln_g, ln_b))
        x_new = u @ uW2 + ub2
        return x + x_new
    edge_index = jnp.stack([src, dst])
    x = _layernorm(x + _L0_gnn_ref(x, edge_index, L0_gnn_W1, L0_gnn_b1, L0_gnn_W2, L0_gnn_b2, L0_gnn_gamma, L0_gnn_beta), axis=-1)
    x = _layernorm(x + _L1_gnn_ref(x, edge_index, L1_gnn_W_in, L1_gnn_b_in, L1_gnn_Wl0, L1_gnn_bl0, L1_gnn_Wr0, L1_gnn_br0, L1_gnn_att0, L1_gnn_bo0, L1_gnn_g0, L1_gnn_be0, L1_gnn_Wl1, L1_gnn_bl1, L1_gnn_Wr1, L1_gnn_br1, L1_gnn_att1, L1_gnn_bo1, L1_gnn_g1, L1_gnn_be1, L1_gnn_Wl2, L1_gnn_bl2, L1_gnn_Wr2, L1_gnn_br2, L1_gnn_att2, L1_gnn_bo2, L1_gnn_g2, L1_gnn_be2, L1_gnn_W_out, L1_gnn_b_out), axis=-1)
    x = _layernorm(x + _L2_gnn_ref(x, edge_index, L2_gnn_hyperedge_weight, L2_gnn_W, L2_gnn_b), axis=-1)
    x = _layernorm(x + _L3_gnn_ref(x, edge_index, edge_weight, L3_gnn_mW1, L3_gnn_mb1, L3_gnn_mW2, L3_gnn_mb2, L3_gnn_uW1, L3_gnn_ub1, L3_gnn_ln_g, L3_gnn_ln_b, L3_gnn_uW2, L3_gnn_ub2), axis=-1)
    return x

_drawn_inputs = setup_inputs


def setup_inputs(seed=0):
    import zlib

    import numpy as np

    out = dict(_drawn_inputs(seed))
    spreads = {'L0_gnn_gamma': (1.0, 0.2),
     'L0_gnn_beta': (0.0, 0.1),
     'L1_gnn_b_in': (0.0, 0.516),
     'L1_gnn_bl0': (0.0, 0.8),
     'L1_gnn_br0': (0.0, 0.268),
     'L1_gnn_bo0': (0.0, 0.279),
     'L1_gnn_g0': (1.0, 0.6),
     'L1_gnn_be0': (0.0, 0.8),
     'L1_gnn_bl1': (0.0, 0.8),
     'L1_gnn_br1': (0.0, 0.8),
     'L1_gnn_bo1': (0.0, 0.708),
     'L1_gnn_g1': (1.0, 0.6),
     'L1_gnn_be1': (0.0, 0.8),
     'L1_gnn_bl2': (0.0, 0.8),
     'L1_gnn_br2': (0.0, 0.8),
     'L1_gnn_bo2': (0.0, 0.8),
     'L1_gnn_g2': (1.0, 0.6),
     'L1_gnn_be2': (0.0, 0.8),
     'L1_gnn_b_out': (0.0, 0.8),
     'L3_gnn_mb1': (0.0, 0.326),
     'L3_gnn_mb2': (0.0, 0.1),
     'L3_gnn_ub1': (0.0, 0.8),
     'L3_gnn_ln_g': (1.0, 0.2),
     'L3_gnn_ln_b': (0.0, 0.461),
     'L3_gnn_ub2': (0.0, 0.1)}
    factors = {'edge_weight': 3.677,
     'L0_gnn_b1': 3.524,
     'L0_gnn_b2': 8.0,
     'L1_gnn_Wl0': 8.0,
     'L1_gnn_Wl1': 8.0,
     'L1_gnn_att1': 8.0,
     'L1_gnn_Wl2': 8.0,
     'L1_gnn_att2': 8.0,
     'L2_gnn_b': 4.819}
    for name, (base, spread) in spreads.items():
        noise = np.random.default_rng([zlib.crc32(name.encode()), seed]).standard_normal(out[name].shape)
        drawn = base * np.exp(spread * noise) if base else spread * noise
        out[name] = jnp.asarray(drawn.astype(out[name].dtype))
    for name, factor in factors.items():
        out[name] = (out[name] * factor).astype(out[name].dtype)
    return out
```

```python
from contextlib import ExitStack
from itertools import count

import concourse.bass as bass
from concourse import mybir

F32 = mybir.dt.float32
BF16 = mybir.dt.bfloat16
F16 = mybir.dt.float16
I32 = mybir.dt.int32
ALU = mybir.AluOpType
ACT = mybir.ActivationFunctionType
AX_X = mybir.AxisListType.X

N = 3125
E = 100000
D = 128
HYPER = 625
HEADS, HID = 4, 32
P = 125
WIN = N // P
TILES = E // P
RROWS = 100
TPR = TILES // RROWS
STEPS = TILES + WIN - 1
HALF = 4
PAIR = 2 * HALF
LOOPS = STEPS // PAIR
PAD = STEPS + PAIR
ACCW = D + 2 * HEADS + 1
BIG = 1.0e30
ROUND = 12582912.0
EPS = 1e-5
GROUPS = (WIN + 3) // 4
assert STEPS % PAIR == 0 and WIN * P == N and TILES * P == E


class Link:

    def __init__(self, eng, sem):
        self.eng, self.sem, self.n = eng, sem, 0

    def __call__(self, ins):
        ins.then_inc(self.sem, 1)
        self.n += 1
        self.eng.wait_ge(self.sem, self.n)


def each(ap, n):
    return ap.unsqueeze(2).broadcast_to([ap.shape[0], ap.shape[1], n])


def rows_of(ap, n):
    return ap.unsqueeze(1).broadcast_to([ap.shape[0], n, ap.shape[1]])


def windows(g):
    return range(4 * g, min(4 * g + 4, WIN))


def span(g):
    return len(windows(g)) * P


class Scope:

    stages = count()

    def __init__(self, nc):
        self.nc, self.ctx, self.stage, self.used = nc, ExitStack(), next(Scope.stages), []

    def __enter__(self):
        self.ctx.__enter__()
        return self

    def __exit__(self, *a):
        self.ctx.close()
        if self.used:
            rest = list(self.nc.free_semaphores)
            self.nc.clear_and_free_semaphores(self.used)
            freed = [n for n in self.nc.free_semaphores if n not in rest]
            self.nc.reset_free_semaphores(rest + freed)

    def sb(self, name, shape, dt=F32):
        return self.ctx.enter_context(self.nc.sbuf_tensor(f"{name}_{self.stage}", shape, dt))

    def ps(self, name, shape, dt=F32):
        return self.ctx.enter_context(self.nc.psum_tensor(f"{name}_{self.stage}", shape, dt))

    def sem(self, name):
        self.used.append(self.nc.alloc_semaphore(f"{name}_{self.stage}"))
        return self.used[-1]

    def sems(self, name):
        return [self.sem(f"{name}{p}") for p in range(2)]

    def block(self):
        return self.ctx.enter_context(self.nc.Block())



def load(nc, pairs):
    with Scope(nc) as sc:
        loaded = sc.sem("loaded")
        block = sc.block()

        @block.sync
        def _(sp):
            for dst, src in pairs:
                sp.dma_start(dst, src, allow_slow_non_contiguous=dst.shape[0] * dst.shape[-1] < 1000).then_inc(loaded, 16)
            sp.wait_ge(loaded, 16 * len(pairs))


def to_features(nc, ident, src, width, dst):
    with Scope(nc) as sc:
        bank = sc.ps("bank", [128, GROUPS, 512])
        turned = sc.sem("turned")
        block = sc.block()

        @block.tensor
        def _(pe):
            for g in range(GROUPS):
                for w in windows(g):
                    ins = pe.transpose(bank[0:width, g, (w % 4) * P:(w % 4 + 1) * P], src[:, w, 0:width], ident[0:P, 0:P])
                ins.then_inc(turned, 1)

        @block.scalar
        def _(act):
            for g in range(GROUPS):
                act.wait_ge(turned, g + 1)
                act.copy(dst[0:width, 4 * g * P:4 * g * P + span(g)], bank[0:width, g, 0:span(g)])


def to_nodes(nc, ident, src, dst):
    with Scope(nc) as sc:
        bank = sc.ps("bank", [128, GROUPS, 512])
        turned = sc.sem("turned")
        block = sc.block()

        @block.tensor
        def _(pe):
            for g in range(GROUPS):
                for w in windows(g):
                    ins = pe.transpose(bank[0:P, g, (w % 4) * D:(w % 4 + 1) * D], src[:, w * P:(w + 1) * P], ident[:, :])
                ins.then_inc(turned, 1)

        @block.scalar
        def _(act):
            for g in range(GROUPS):
                n = len(windows(g))
                act.wait_ge(turned, g + 1)
                act.copy(dst[:, 4 * g:4 * g + n, 0:D], bank[0:P, g, 0:n * D].rearrange("p (w f) -> p w f", f=D))


def linear_nodes(nc, terms, bias, dst):
    with Scope(nc) as sc:
        bank = sc.ps("bank", [128, GROUPS, 512])
        summed = sc.sem("summed")
        block = sc.block()

        @block.tensor
        def _(pe):
            for g in range(GROUPS):
                for w in windows(g):
                    for n, (x, m) in enumerate(terms):
                        ins = pe.matmul(bank[0:P, g, (w % 4) * D:(w % 4 + 1) * D], x[:, w * P:(w + 1) * P], m,
                                        start=n == 0, stop=n == len(terms) - 1)
                ins.then_inc(summed, 1)

        @block.vector
        def _(dve):
            for g in range(GROUPS):
                n = len(windows(g))
                dve.wait_ge(summed, g + 1)
                got = bank[0:P, g, 0:n * D].rearrange("p (w f) -> p w f", f=D)
                if bias is None:
                    dve.tensor_copy(dst[:, 4 * g:4 * g + n, 0:D], got)
                else:
                    dve.tensor_tensor(dst[:, 4 * g:4 * g + n, 0:D], got, rows_of(bias, n), ALU.add)


def linear_features(nc, x, w, func, bias, dst):
    m = w.shape[1]
    with Scope(nc) as sc:
        bank = sc.ps("bank", [128, GROUPS, 512])
        summed = sc.sem("summed")
        block = sc.block()

        @block.tensor
        def _(pe):
            for g in range(GROUPS):
                pe.matmul(bank[0:m, g, 0:span(g)], w, x[:, 4 * g * P:4 * g * P + span(g)],
                          start=True, stop=True).then_inc(summed, 1)

        @block.scalar
        def _(act):
            for g in range(GROUPS):
                act.wait_ge(summed, g + 1)
                act.activation(dst[0:m, 4 * g * P:4 * g * P + span(g)], bank[0:m, g, 0:span(g)], func, bias=bias)


def normalize(nc, y, eps, before=None, gain=None, shift=None, func=None, after=None):
    with Scope(nc) as sc:
        sq = sc.sb("sq", [P, WIN, D])
        mean = sc.sb("mean", [P, WIN])
        var = sc.sb("var", [P, WIN])
        std = sc.sb("std", [P, WIN])
        rstd = sc.sb("rstd", [P, WIN])
        step = sc.sem("step")
        var_ready, std_ready, scaled, activated = (sc.sem(x) for x in ("var_ready", "std_ready", "scaled", "activated"))
        block = sc.block()

        @block.vector
        def _(dve):
            link = Link(dve, step)
            if before:
                before(dve, link)
            link(dve.tensor_reduce(mean[:, :], y, AX_X, ALU.add))
            link(dve.tensor_scalar(mean[:, :], mean[:, :], 1.0 / D, None, ALU.mult))
            link(dve.tensor_tensor(y, y, each(mean[:, :], D), ALU.subtract))
            link(dve.tensor_tensor(sq[:, :, :], y, y, ALU.mult))
            dve.tensor_reduce(var[:, :], sq[:, :, :], AX_X, ALU.add).then_inc(var_ready, 1)
            dve.wait_ge(std_ready, 1)
            link(dve.reciprocal(rstd[:, :], std[:, :]))
            if gain is None:
                dve.tensor_tensor(y, y, each(rstd[:, :], D), ALU.mult).then_inc(scaled, 1)
            else:
                link(dve.tensor_tensor(y, y, each(rstd[:, :], D), ALU.mult))
                link(dve.tensor_tensor(y, y, rows_of(gain, WIN), ALU.mult))
                dve.tensor_tensor(y, y, rows_of(shift, WIN), ALU.add).then_inc(scaled, 1)
            dve.wait_ge(scaled, 1)
            if func is not None:
                dve.wait_ge(activated, 1)
            if after:
                after(dve, link)

        @block.scalar
        def _(act):
            act.wait_ge(var_ready, 1)
            act.activation(std[:, :], var[:, :], ACT.Sqrt, bias=eps[0:P, :], scale=1.0 / D).then_inc(std_ready, 1)
            if func is not None:
                act.wait_ge(scaled, 1)
                act.activation(y, y, func).then_inc(activated, 1)


def vector_steps(nc, steps):
    with Scope(nc) as sc:
        step = sc.sem("step")
        block = sc.block()

        @block.vector
        def _(dve):
            steps(dve, Link(dve, step))




def prime(eng, *pairs):
    for pair in pairs:
        for sem in pair:
            eng.sem_inc(sem, 1)


def before(i, unit=1):
    return unit * i + 1


def done(i, unit=1):
    return unit * (i + 1) + 1


def landed(i, dmas=1):
    return 16 * dmas * (i + 1)


def hold(eng, sem, value, held_up):
    eng.wait_ge(sem, value)
    eng.sem_inc(held_up, 1)


def gather_rows(pool, i, p, table, rows, now, idx, held_up, freed, staged, rows_in):
    for sem in freed:
        hold(pool, sem[p], before(i), held_up)
    pool.tensor_copy(now[:, p, :], idx[:, bass.ds(PAIR * i + HALF * p, HALF)]).then_inc(staged[p], 1)
    hold(pool, staged[p], done(i), held_up)
    for j in range(HALF):
        pool.indirect_dma_start(rows[:, p, j, 0:D], None, table,
                                bass.IndirectOffsetOnAxis(ap=now[:, p, j:j + 1], axis=0)).then_inc(rows_in[p], 16)


def window_of(eng, g, i, p, j):
    return eng.value_load(g.win_i[0:1, bass.ds(PAIR * i + HALF * p + j, 1)], min_val=0, max_val=WIN - 1)


def one_hot(eng, g, out, i, p):
    return eng.tensor_tensor(out, rows_of(g.iota[0:P, 0:P], HALF),
                             each(g.slot[:, bass.ds(PAIR * i + HALF * p, HALF)], P), ALU.is_equal)


def add_sums(dve, g, i, p, sums, width, summed, added):
    dve.wait_ge(summed[p], done(i))
    for j in range(HALF):
        w = window_of(dve, g, i, p, j)
        if j == 0:
            dve.wait_ge(added[1 - p], before(i + p, HALF))
        dve.wait_ge(added[p], before(i, HALF) + j)
        row = g.acc[:, bass.ds(w, 1), 0:width]
        dve.tensor_tensor(row, row, sums[:, p, j:j + 1, 0:width], ALU.add).then_inc(added[p], 1)


def sum_steps(pe, i, p, onehot, values, sums, width, made, values_ready, summed, added):
    pe.wait_ge(made[p], done(i))
    for sem, count in values_ready:
        pe.wait_ge(sem[p], count)
    pe.wait_ge(added[p], before(i, HALF))
    for j in range(HALF):
        ins = pe.matmul(sums[:, p, j, 0:width], onehot[:, p, j, :], values[:, p, j, 0:width], start=True, stop=True)
    ins.then_inc(summed[p], 1)


def neighbour_sums(nc, g, table):
    width = D + 1
    with Scope(nc) as sc:
        rows = sc.sb("rows", [P, 2, HALF, width])
        now = sc.sb("now", [P, 2, HALF], I32)
        held_up = sc.sem("held_up")
        onehot = sc.sb("onehot", [P, 2, HALF, P])
        sums = sc.ps("sums", [P, 2, HALF, 256])
        ones_set, acc_clear = sc.sem("ones_set"), sc.sem("acc_clear")
        staged, rows_in, made, summed, added = (sc.sems(x) for x in ("staged", "rows_in", "made", "summed", "added"))
        block = sc.block()

        @block.gpsimd
        def _(pool):
            prime(pool, staged)
            with pool.Fori(0, LOOPS) as i:
                for p in range(2):
                    gather_rows(pool, i, p, table, rows, now, g.idx, held_up, [summed], staged, rows_in)

        @block.vector
        def _(dve):
            prime(dve, made, added)
            dve.memset(rows[:, :, :, D:width], 1.0).then_inc(ones_set, 1)
            dve.memset(g.acc[:, :, :], 0.0).then_inc(acc_clear, 1)
            dve.wait_ge(acc_clear, 1)
            for p in range(2):
                one_hot(dve, g, onehot[:, p, :, :], 0, p).then_inc(made[p], 1)
            with dve.Fori(0, LOOPS) as i:
                for p in range(2):
                    add_sums(dve, g, i, p, sums, width, summed, added)
                    one_hot(dve, g, onehot[:, p, :, :], i + 1, p).then_inc(made[p], 1)

        @block.tensor
        def _(pe):
            prime(pe, summed)
            pe.wait_ge(ones_set, 1)
            with pe.Fori(0, LOOPS) as i:
                for p in range(2):
                    sum_steps(pe, i, p, onehot, rows, sums, width, made, [(rows_in, landed(i, HALF))], summed, added)


def turn_one_hot(pe, i, p, ident, onehot, turn, made, turned, copied):
    pe.wait_ge(made[p], done(i))
    pe.wait_ge(copied[p], before(i))
    for j in range(HALF):
        ins = pe.transpose(turn[:, p, j * P:(j + 1) * P], onehot[:, p, j, :], ident[0:P, 0:P])
    ins.then_inc(turned[p], 1)


def copy_turned(act, i, p, turn, onehot_t, turned, spread, copied):
    act.wait_ge(turned[p], done(i))
    act.wait_ge(spread[p], before(i))
    act.copy(onehot_t[:, p, :], turn[:, p, 0:HALF * P]).then_inc(copied[p], 1)


def attention_logits(nc, g, table, xl, att, spill, logit, capped, weight):
    extra = HEADS + (weight is not None)
    with Scope(nc) as sc:
        rows = sc.sb("rows", [P, 2, HALF, D])
        now = sc.sb("now", [P, 2, HALF], I32)
        held_up = sc.sem("held_up")
        onehot = sc.sb("onehot", [P, 2, HALF, P])
        onehot_t = sc.sb("onehot_t", [P, 2, HALF * P])
        z = sc.sb("z", [P, 2, HALF, D])
        turn = sc.ps("turn", [P, 2, 512])
        zp = sc.ps("zp", [P, 2, HALF, D])
        ep = sc.ps("ep", [P, 2, 512])
        names = ("staged", "rows_in", "made", "turned", "copied", "spread", "added", "leaky", "scaled", "summed", "taken", "spilled", "kept")
        staged, rows_in, made, turned, copied, spread, added, leaky, scaled, summed, taken, spilled, kept = (sc.sems(x) for x in names)
        block = sc.block()

        @block.gpsimd
        def _(pool):
            prime(pool, staged)
            with pool.Fori(0, LOOPS) as i:
                for p in range(2):
                    gather_rows(pool, i, p, table, rows, now, g.idx, held_up, [added, kept], staged, rows_in)

        @block.sync
        def _(sp):
            prime(sp, kept)
            with sp.Fori(0, LOOPS) as i:
                for p in range(2):
                    sp.wait_ge(rows_in[p], landed(i, HALF))
                    sp.dma_start(spill[bass.ds(2 * i + p, 1), :, :].rearrange("a p f -> (a p) f"),
                                 rows[:, p, :, :].rearrange("p j f -> p (j f)")).then_inc(spilled[p], 16)
                    sp.wait_ge(spilled[p], landed(i))
                    sp.sem_inc(kept[p], 1)

        @block.scalar
        def _(act):
            prime(act, copied)
            with act.Fori(0, LOOPS) as i:
                for p in range(2):
                    copy_turned(act, i, p, turn, onehot_t, turned, spread, copied)

        @block.tensor
        def _(pe):
            prime(pe, turned, spread)
            with pe.Fori(0, LOOPS) as i:
                for p in range(2):
                    turn_one_hot(pe, i, p, g.ident, onehot, turn, made, turned, copied)
                    pe.wait_ge(copied[p], done(i))
                    pe.wait_ge(added[p], before(i))
                    pe.wait_ge(taken[p], before(i))
                    for j in range(HALF):
                        w = window_of(pe, g, i, p, j)
                        hot = onehot_t[:, p, j * P:(j + 1) * P]
                        pe.matmul(zp[:, p, j, :], hot, xl[:, bass.ds(w, 1), 0:D].rearrange("p w f -> p (w f)"), start=True, stop=True)
                        ins = pe.matmul(ep[:, p, 8 * j:8 * j + extra], hot,
                                        xl[:, bass.ds(w, 1), D:D + extra].rearrange("p w f -> p (w f)"), start=True, stop=True)
                    ins.then_inc(spread[p], 1)

        @block.vector
        def _(dve):
            prime(dve, made, added, leaky, scaled, summed, taken)
            for p in range(2):
                one_hot(dve, g, onehot[:, p, :, :], 0, p).then_inc(made[p], 1)
            with dve.Fori(0, LOOPS) as i:
                for p in range(2):
                    s = bass.ds(PAIR * i + HALF * p, HALF)
                    zz = z[:, p, :, :]
                    dve.wait_ge(rows_in[p], landed(i, HALF))
                    dve.wait_ge(spread[p], done(i))
                    dve.wait_ge(summed[p], before(i))
                    dve.tensor_tensor(zz, zp[:, p, :, :], rows[:, p, :, :], ALU.add).then_inc(added[p], 1)
                    dve.wait_ge(turned[p], done(i))
                    one_hot(dve, g, onehot[:, p, :, :], i + 1, p).then_inc(made[p], 1)
                    dve.wait_ge(added[p], done(i))
                    dve.scalar_tensor_tensor(out=zz, in0=zz, scalar=0.2, in1=zz, op0=ALU.mult, op1=ALU.max).then_inc(leaky[p], 1)
                    dve.wait_ge(leaky[p], done(i))
                    dve.tensor_tensor(zz, zz, rows_of(att, HALF), ALU.mult).then_inc(scaled[p], 1)
                    dve.wait_ge(scaled[p], done(i))
                    dve.tensor_reduce(logit[:, s, :], zz.rearrange("p j (h c) -> p j h c", h=HEADS), AX_X, ALU.add).then_inc(summed[p], 1)
                    dve.wait_ge(summed[p], done(i))
                    own = ep[:, p, 0:8 * HALF].rearrange("p (j e) -> p j e", e=8)
                    if weight is not None:
                        dve.tensor_copy(weight[:, s].unsqueeze(2), own[:, :, HEADS:HEADS + 1])
                    dve.tensor_tensor(capped[:, s, :], logit[:, s, :], own[:, :, 0:HEADS], ALU.max).then_inc(taken[p], 1)


def softmax_weights(nc, g, logit, capped, first_max):
    lanes = PAIR * P
    with Scope(nc) as sc:
        lrow = sc.sb("lrow", [LOOPS, HEADS, lanes])
        crow = sc.sb("crow", [LOOPS, HEADS, lanes])
        fwd = sc.sb("fwd", [LOOPS, lanes])
        mx = sc.sb("mx", [LOOPS, HEADS, lanes])
        ends = sc.sb("ends", [LOOPS, 2, HEADS])
        ends_t = sc.sb("ends_t", [HEADS, 2, LOOPS])
        run = sc.sb("run", [HEADS, 2, LOOPS])
        carry_t = sc.sb("carry_t", [HEADS, 2, LOOPS])
        carry = sc.sb("carry", [LOOPS, 2, HEADS])
        bank = sc.ps("bank", [128, 8, 512])

        with Scope(nc) as s1:
            turned, copied = s1.sem("turned"), s1.sem("copied")
            block = s1.block()
            jobs = [(a, b, h, q) for a, b in ((logit, lrow), (capped, crow)) for h in range(HEADS) for q in range(2)]

            @block.tensor
            def _(pe):
                for n, (a, b, h, q) in enumerate(jobs):
                    if n >= 8:
                        pe.wait_ge(copied, n - 7)
                    av = a[:, :, h].rearrange("p (c b) -> p c b", b=PAIR)
                    for k in range(4):
                        ins = pe.transpose(bank[0:LOOPS, n % 8, k * P:(k + 1) * P], av[:, :, 4 * q + k], g.ident[0:P, 0:P])
                    ins.then_inc(turned, 1)

            @block.scalar
            def _(act):
                for n, (a, b, h, q) in enumerate(jobs):
                    act.wait_ge(turned, n + 1)
                    act.copy(b[:, h, 4 * q * P:(4 * q + 4) * P], bank[0:LOOPS, n % 8, 0:4 * P]).then_inc(copied, 1)

        with Scope(nc) as s2:
            step, ends_ready, ends_turned, carry_ready, carry_turned = (s2.sem(x) for x in (
                "step", "ends_ready", "ends_turned", "carry_ready", "carry_turned"))
            block = s2.block()

            @block.vector
            def _(dve):
                link = Link(dve, step)
                for h in range(HEADS):
                    link(dve.tensor_tensor_scan(fwd[:, :], g.brk[:, 0:lanes], crow[:, h, :], -BIG, ALU.add, ALU.max))
                    link(dve.tensor_tensor_scan(mx[:, h, ::-1], g.brk[:, 1:lanes + 1][:, ::-1], crow[:, h, ::-1], -BIG, ALU.add, ALU.max))
                    link(dve.tensor_copy(ends[:, 0, h:h + 1], fwd[:, lanes - 1:lanes]))
                    link(dve.tensor_copy(ends[:, 1, h:h + 1], mx[:, h, 0:1]))
                    link(dve.tensor_tensor(mx[:, h, :], mx[:, h, :], fwd[:, :], ALU.max))
                dve.sem_inc(ends_ready, 1)
                dve.wait_ge(ends_turned, 1)
                for k in range(2):
                    link(dve.tensor_copy(ends_t[:, k, :], bank[0:HEADS, k, 0:LOOPS]))
                link(dve.tensor_tensor_scan(run[:, 0, :], g.whole_up[:, :], ends_t[:, 0, :], -BIG, ALU.add, ALU.max))
                link(dve.tensor_tensor_scan(run[:, 1, ::-1], g.whole_down[:, ::-1], ends_t[:, 1, ::-1], -BIG, ALU.add, ALU.max))
                link(dve.memset(carry_t[:, :, :], -BIG))
                link(dve.tensor_tensor(carry_t[:, 0, 1:LOOPS], run[:, 0, 0:LOOPS - 1], g.joint[:, 1:LOOPS], ALU.add))
                link(dve.tensor_tensor(carry_t[:, 1, 0:LOOPS - 1], run[:, 1, 1:LOOPS], g.joint[:, 1:LOOPS], ALU.add))
                dve.sem_inc(carry_ready, 1)
                dve.wait_ge(carry_turned, 1)
                for k in range(2):
                    link(dve.tensor_copy(carry[:, k, :], bank[0:LOOPS, 2 + k, 0:HEADS]))
                for h in range(HEADS):
                    link(dve.scalar_tensor_tensor(out=mx[:, h, :], in0=g.head_run[:, :], scalar=carry[:, 0, h:h + 1], in1=mx[:, h, :], op0=ALU.add, op1=ALU.max))
                    link(dve.scalar_tensor_tensor(out=mx[:, h, :], in0=g.tail_run[:, :], scalar=carry[:, 1, h:h + 1], in1=mx[:, h, :], op0=ALU.add, op1=ALU.max))
                    link(dve.tensor_tensor(lrow[:, h, :], lrow[:, h, :], mx[:, h, :], ALU.subtract))

            @block.tensor
            def _(pe):
                pe.wait_ge(ends_ready, 1)
                for k in range(2):
                    ins = pe.transpose(bank[0:HEADS, k, 0:LOOPS], ends[:, k, :], g.ident[0:LOOPS, 0:LOOPS])
                ins.then_inc(ends_turned, 1)
                pe.wait_ge(carry_ready, 1)
                for k in range(2):
                    ins = pe.transpose(bank[0:LOOPS, 2 + k, 0:HEADS], carry_t[:, k, :], g.ident[0:HEADS, 0:HEADS])
                ins.then_inc(carry_turned, 1)

        with Scope(nc) as s3:
            exped, turned, copied = s3.sem("exped"), s3.sem("turned"), s3.sem("copied")
            block = s3.block()
            jobs = [(a, b, h, q) for h in range(HEADS) for a, b in ((lrow, logit), (mx, first_max)) for q in range(2)]

            @block.scalar
            def _(act):
                for h in range(HEADS):
                    act.activation(lrow[:, h, :], lrow[:, h, :], ACT.Exp).then_inc(exped, 1)

            @block.tensor
            def _(pe):
                for n, (a, b, h, q) in enumerate(jobs):
                    pe.wait_ge(exped, h + 1)
                    if n >= 8:
                        pe.wait_ge(copied, n - 7)
                    for k in range(4):
                        ins = pe.transpose(bank[0:P, n % 8, k * LOOPS:(k + 1) * LOOPS], a[:, h, (4 * q + k) * P:(4 * q + k + 1) * P],
                                           g.ident[0:LOOPS, 0:LOOPS])
                    ins.then_inc(turned, 1)

            @block.vector
            def _(dve):
                for n, (a, b, h, q) in enumerate(jobs):
                    dve.wait_ge(turned, n + 1)
                    out = b[:, :, h].rearrange("p (c b) -> p b c", b=PAIR)[:, 4 * q:4 * q + 4, :]
                    got = bank[0:P, n % 8, 0:4 * LOOPS].rearrange("p (k c) -> p k c", k=4)
                    if b is first_max:
                        flag = g.first[:, 0:STEPS].rearrange("p (c b) -> p b c", b=PAIR)[:, 4 * q:4 * q + 4, :]
                        dve.tensor_tensor(out, got, flag, ALU.mult).then_inc(copied, 1)
                    else:
                        dve.tensor_copy(out, got).then_inc(copied, 1)


def attention_sums(nc, g, spill, weight, first_max):
    width = ACCW
    with Scope(nc) as sc:
        rows = sc.sb("rows", [P, 2, HALF, D])
        values = sc.sb("values", [P, 2, HALF, width])
        held_up = sc.sem("held_up")
        onehot = sc.sb("onehot", [P, 2, HALF, P])
        sums = sc.ps("sums", [P, 2, HALF, 256])
        acc_clear = sc.sem("acc_clear")
        names = ("rows_in", "made", "weighted", "tailed", "maxed", "marked", "summed", "added")
        rows_in, made, weighted, tailed, maxed, marked, summed, added = (sc.sems(x) for x in names)
        block = sc.block()

        @block.sync
        def _(sp):
            with sp.Fori(0, LOOPS) as i:
                for p in range(2):
                    sp.wait_ge(weighted[p], before(i))
                    sp.dma_start(rows[:, p, :, :].rearrange("p j f -> p (j f)"),
                                 spill[bass.ds(2 * i + p, 1), :, :].rearrange("a p f -> (a p) f")).then_inc(rows_in[p], 16)

        @block.scalar
        def _(act):
            prime(act, tailed, maxed, marked)
            with act.Fori(0, LOOPS) as i:
                for p in range(2):
                    s = bass.ds(PAIR * i + HALF * p, HALF)
                    act.wait_ge(summed[p], before(i))
                    act.copy(values[:, p, :, D:D + HEADS], weight[:, s, :]).then_inc(tailed[p], 1)
                    act.copy(values[:, p, :, D + HEADS:width - 1], first_max[:, s, :]).then_inc(maxed[p], 1)
                    act.copy(values[:, p, :, width - 1:width], g.first[:, s].unsqueeze(2)).then_inc(marked[p], 1)

        @block.gpsimd
        def _(pool):
            prime(pool, weighted)
            with pool.Fori(0, LOOPS) as i:
                for p in range(2):
                    s = bass.ds(PAIR * i + HALF * p, HALF)
                    pool.wait_ge(rows_in[p], landed(i))
                    hold(pool, summed[p], before(i), held_up)
                    pool.tensor_tensor(values[:, p, :, 0:D].rearrange("p j (h c) -> p j h c", h=HEADS),
                                       rows[:, p, :, :].rearrange("p j (h c) -> p j h c", h=HEADS),
                                       weight[:, s, :].unsqueeze(3).broadcast_to([P, HALF, HEADS, HID]), ALU.mult).then_inc(weighted[p], 1)

        @block.vector
        def _(dve):
            prime(dve, made, added)
            dve.memset(g.acc[:, :, :], 0.0).then_inc(acc_clear, 1)
            dve.wait_ge(acc_clear, 1)
            for p in range(2):
                one_hot(dve, g, onehot[:, p, :, :], 0, p).then_inc(made[p], 1)
            with dve.Fori(0, LOOPS) as i:
                for p in range(2):
                    add_sums(dve, g, i, p, sums, width, summed, added)
                    one_hot(dve, g, onehot[:, p, :, :], i + 1, p).then_inc(made[p], 1)

        @block.tensor
        def _(pe):
            prime(pe, summed)
            with pe.Fori(0, LOOPS) as i:
                for p in range(2):
                    sum_steps(pe, i, p, onehot, values, sums, width, made,
                              [(weighted, done(i)), (tailed, done(i)), (maxed, done(i)), (marked, done(i))], summed, added)


def message_sums(nc, g, table, own, w_edge):
    width = D + 1
    with Scope(nc) as sc:
        rows = sc.sb("rows", [P, 2, HALF, D])
        now = sc.sb("now", [P, 2, HALF], I32)
        held_up = sc.sem("held_up")
        onehot = sc.sb("onehot", [P, 2, HALF, P])
        onehot_t = sc.sb("onehot_t", [P, 2, HALF * P])
        z = sc.sb("z", [P, 2, HALF, D])
        edge = sc.sb("edge", [P, 2, HALF, D])
        hidden = sc.sb("hidden", [P, 2, HALF, D])
        values = sc.sb("values", [P, 2, HALF, width])
        turn = sc.ps("turn", [P, 2, 512])
        zp = sc.ps("zp", [P, 2, HALF, D])
        sums = sc.ps("sums", [P, 2, HALF, 256])
        acc_clear = sc.sem("acc_clear")
        names = ("staged", "rows_in", "made", "turned", "copied", "spread", "edged", "added", "whole", "active", "weighted", "tailed", "summed", "accd")
        staged, rows_in, made, turned, copied, spread, edged, added, whole, active, weighted, tailed, summed, accd = (sc.sems(x) for x in names)
        block = sc.block()

        @block.gpsimd
        def _(pool):
            prime(pool, staged)
            with pool.Fori(0, LOOPS) as i:
                for p in range(2):
                    gather_rows(pool, i, p, table, rows, now, g.idx, held_up, [added], staged, rows_in)

        @block.scalar
        def _(act):
            prime(act, copied, active)
            with act.Fori(0, LOOPS) as i:
                for p in range(2):
                    copy_turned(act, i, p, turn, onehot_t, turned, spread, copied)
                    act.wait_ge(whole[p], done(i))
                    act.wait_ge(weighted[p], before(i))
                    act.activation(hidden[:, p, :, :], z[:, p, :, :], ACT.Silu).then_inc(active[p], 1)

        @block.tensor
        def _(pe):
            prime(pe, turned, spread, summed)
            with pe.Fori(0, LOOPS) as i:
                for p in range(2):
                    turn_one_hot(pe, i, p, g.ident, onehot, turn, made, turned, copied)
                    pe.wait_ge(copied[p], done(i))
                    pe.wait_ge(added[p], before(i))
                    for j in range(HALF):
                        w = window_of(pe, g, i, p, j)
                        ins = pe.matmul(zp[:, p, j, :], onehot_t[:, p, j * P:(j + 1) * P],
                                        own[:, bass.ds(w, 1), :].rearrange("p w f -> p (w f)"), start=True, stop=True)
                    ins.then_inc(spread[p], 1)
                for p in range(2):
                    sum_steps(pe, i, p, onehot, values, sums, width, made, [(weighted, done(i)), (tailed, done(i))], summed, accd)

        @block.vector
        def _(dve):
            prime(dve, made, edged, added, whole, weighted, tailed, accd)
            dve.memset(g.acc[:, :, :], 0.0).then_inc(acc_clear, 1)
            dve.wait_ge(acc_clear, 1)
            for p in range(2):
                one_hot(dve, g, onehot[:, p, :, :], 0, p).then_inc(made[p], 1)
            with dve.Fori(0, LOOPS) as i:
                for p in range(2):
                    s = bass.ds(PAIR * i + HALF * p, HALF)
                    zz = z[:, p, :, :]
                    dve.wait_ge(added[p], before(i))
                    dve.tensor_tensor(edge[:, p, :, :], rows_of(w_edge, HALF), each(g.ew[:, s], D), ALU.mult).then_inc(edged[p], 1)
                    dve.wait_ge(edged[p], done(i))
                    dve.wait_ge(rows_in[p], landed(i, HALF))
                    dve.tensor_tensor(edge[:, p, :, :], edge[:, p, :, :], rows[:, p, :, :], ALU.add).then_inc(added[p], 1)
                    dve.wait_ge(added[p], done(i))
                    dve.wait_ge(spread[p], done(i))
                    dve.wait_ge(active[p], before(i))
                    dve.tensor_tensor(zz, zp[:, p, :, :], edge[:, p, :, :], ALU.add).then_inc(whole[p], 1)
                    dve.wait_ge(whole[p], done(i))
                for p in range(2):
                    s = bass.ds(PAIR * i + HALF * p, HALF)
                    dve.wait_ge(active[p], done(i))
                    dve.wait_ge(summed[p], before(i))
                    dve.tensor_tensor(values[:, p, :, 0:D], hidden[:, p, :, :], each(g.ew[:, s], D), ALU.mult).then_inc(weighted[p], 1)
                    dve.tensor_copy(values[:, p, :, D:width], g.ew[:, s].unsqueeze(2)).then_inc(tailed[p], 1)
                for p in range(2):
                    add_sums(dve, g, i, p, sums, width, summed, accd)
                    one_hot(dve, g, onehot[:, p, :, :], i + 1, p).then_inc(made[p], 1)


def source_weights(nc, g, weight, out):
    with Scope(nc) as sc:
        tile = sc.sb("tile", [P, PAD])
        lane = sc.sb("lane", [P, PAD])
        hot_tile = sc.sb("hot_tile", [P, 2, HALF, WIN])
        hot_lane = sc.sb("hot_lane", [P, 2, HALF, P])
        scaled = sc.sb("scaled", [P, 2, HALF, P])
        table = sc.sb("table", [WIN, P])
        hist = sc.ps("hist", [WIN, 512])
        turn = sc.ps("turn", [P, 512])
        zero = sc.sb("zero", [P, P])
        step, cleared, finished, copied, turned = (sc.sem(x) for x in ("step", "cleared", "finished", "copied", "turned"))
        tiled, laned, ready, used = (sc.sems(x) for x in ("tiled", "laned", "ready", "used"))
        block = sc.block()

        @block.vector
        def _(dve):
            prime(dve, tiled, laned, ready)
            link = Link(dve, step)
            link(dve.tensor_scalar(tile[:, :], g.src[:, :], -float(P // 2), 1.0 / P, ALU.add, ALU.mult))
            link(dve.tensor_scalar(tile[:, :], tile[:, :], ROUND, None, ALU.add))
            link(dve.tensor_scalar(tile[:, :], tile[:, :], -ROUND, None, ALU.add))
            link(dve.scalar_tensor_tensor(out=lane[:, :], in0=tile[:, :], scalar=-float(P), in1=g.src[:, :], op0=ALU.mult, op1=ALU.add))
            dve.memset(zero[:, :], 0.0).then_inc(cleared, 1)
            with dve.Fori(0, LOOPS) as i:
                for p in range(2):
                    s = bass.ds(PAIR * i + HALF * p, HALF)
                    dve.wait_ge(used[p], before(i))
                    dve.tensor_tensor(hot_tile[:, p, :, :], rows_of(g.iota[0:P, 0:WIN], HALF), each(tile[:, s], WIN), ALU.is_equal).then_inc(tiled[p], 1)
                    dve.tensor_tensor(hot_lane[:, p, :, :], rows_of(g.iota[0:P, 0:P], HALF), each(lane[:, s], P), ALU.is_equal).then_inc(laned[p], 1)
                    dve.wait_ge(laned[p], done(i))
                    dve.tensor_tensor(scaled[:, p, :, :], hot_lane[:, p, :, :], each(weight[:, s], P), ALU.mult).then_inc(ready[p], 1)
                    dve.wait_ge(ready[p], done(i))
            dve.wait_ge(finished, 1)
            dve.tensor_copy(table[:, :], hist[:, 0:P]).then_inc(copied, 1)
            dve.wait_ge(turned, 1)
            dve.tensor_copy(out, turn[:, 0:WIN])

        @block.tensor
        def _(pe):
            prime(pe, used)
            pe.wait_ge(cleared, 1)
            pe.matmul(hist[:, 0:P], zero[:, 0:WIN], zero[:, :], start=True, stop=False, skip_group_check=True)
            with pe.Fori(0, LOOPS) as i:
                for p in range(2):
                    pe.wait_ge(tiled[p], done(i))
                    pe.wait_ge(ready[p], done(i))
                    for j in range(HALF):
                        ins = pe.matmul(hist[:, 0:P], hot_tile[:, p, j, :], scaled[:, p, j, :], start=False, stop=False, skip_group_check=True)
                    ins.then_inc(used[p], 1)
            pe.matmul(hist[:, 0:P], zero[:, 0:WIN], zero[:, :], start=False, stop=True, skip_group_check=True).then_inc(finished, 1)
            pe.wait_ge(copied, 1)
            pe.transpose(turn[:, 0:WIN], table[:, :], g.ident[0:WIN, 0:WIN]).then_inc(turned, 1)


def scatter_to_sources(nc, g, table, idx, out):
    wide = N + 1
    chunks = [(k, min(512, N - 512 * k)) for k in range((N + 511) // 512)]
    with Scope(nc) as sc:
        rows = sc.sb("rows", [P, 2, HALF, D])
        now = sc.sb("now", [P, 2, HALF], I32)
        held_up = sc.sem("held_up")
        parts = [sc.sb(f"part{k}", [P, 2, HALF, D], BF16) for k in range(3)]
        nodes = sc.sb("nodes", [P, wide], F16)
        hot = sc.sb("hot", [P, 2, wide], BF16)
        zero = sc.sb("zero", [P, 512], BF16)
        bank = sc.ps("bank", [128, len(chunks), 512])
        cleared, finished, noded = sc.sem("cleared"), sc.sem("finished"), sc.sem("noded")
        staged, rows_in, hot_made, hot_used = (sc.sems(x) for x in ("staged", "rows_in", "hot_made", "hot_used"))
        cut = [sc.sems(f"cut{k}") for k in range(3)]
        left = [sc.sems(f"left{k}") for k in range(2)]
        block = sc.block()

        @block.gpsimd
        def _(pool):
            prime(pool, staged)
            pool.iota(nodes[:, :], pattern=[[1, wide]], base=-(N // 2), channel_multiplier=0,
                      allow_small_or_imprecise_dtypes=True).then_inc(noded, 1)
            with pool.Fori(0, LOOPS) as i:
                for p in range(2):
                    gather_rows(pool, i, p, table, rows, now, idx, held_up, [cut[2]], staged, rows_in)

        @block.vector
        def _(dve):
            prime(dve, hot_made, *cut, *left)
            dve.memset(zero[:, :], 0.0).then_inc(cleared, 1)
            dve.wait_ge(noded, 1)
            with dve.Fori(0, LOOPS) as i:
                for p in range(2):
                    row = rows[:, p, :, :]
                    dve.wait_ge(rows_in[p], landed(i, HALF))
                    for b in range(2):
                        dve.wait_ge(hot_used[b], HALF * i + 2 * p + 1)
                    for k in range(3):
                        dve.tensor_copy(parts[k][:, p, :, :], row).then_inc(cut[k][p], 1)
                        if k < 2:
                            dve.wait_ge(cut[k][p], done(i))
                            dve.tensor_tensor(row, row, parts[k][:, p, :, :], ALU.subtract).then_inc(left[k][p], 1)
                            dve.wait_ge(left[k][p], done(i))
                    for j in range(HALF):
                        b, use = j % 2, HALF * i + 2 * p + j // 2
                        dve.wait_ge(hot_used[b], use + 3)
                        dve.tensor_scalar(hot[:, b, :], nodes[:, :], g.src_key[:, bass.ds(PAIR * i + HALF * p + j, 1)], None,
                                          ALU.is_equal).then_inc(hot_made[b], 1)

        @block.tensor
        def _(pe):
            for sem in hot_used:
                pe.sem_inc(sem, 3)
            pe.wait_ge(cleared, 1)
            for k, n in chunks:
                pe.matmul(bank[:, k, 0:n], zero[:, 0:D], zero[:, 0:n], start=True, stop=False, skip_group_check=True)
            with pe.Fori(0, LOOPS) as i:
                for p in range(2):
                    pe.wait_ge(cut[2][p], done(i))
                    for j in range(HALF):
                        b, use = j % 2, HALF * i + 2 * p + j // 2
                        pe.wait_ge(hot_made[b], use + 2)
                        for part in parts:
                            for k, n in chunks:
                                ins = pe.matmul(bank[:, k, 0:n], part[:, p, j, :], hot[:, b, 512 * k:512 * k + n],
                                                start=False, stop=False, skip_group_check=True)
                        ins.then_inc(hot_used[b], 1)
            for k, n in chunks:
                ins = pe.matmul(bank[:, k, 0:n], zero[:, 0:D], zero[:, 0:n], start=False, stop=True, skip_group_check=True)
            ins.then_inc(finished, 1)

        @block.scalar
        def _(act):
            act.wait_ge(finished, 1)
            for k, n in chunks:
                act.copy(out[:, 512 * k:512 * k + n], bank[:, k, 0:n])



class Graph:
    pass


def prepare(nc, g, sc, src, dst, edge_weight):
    lanes = PAIR * P
    g.ident = sc.sb("ident", [128, 128])
    g.iota = sc.sb("iota", [128, P])
    g.eps = sc.sb("eps", [128, 1])
    g.idx = sc.sb("idx", [P, PAD], I32)
    g.src = sc.sb("src", [P, PAD])
    g.slot = sc.sb("slot", [P, PAD])
    g.first = sc.sb("first", [P, PAD])
    g.ew = sc.sb("ew", [P, PAD])
    g.key = sc.sb("key", [P, PAD])
    g.src_key = sc.sb("src_key", [P, PAD])
    g.near = sc.sb("near", [P, PAD], I32)
    g.win_i = sc.sb("win_i", [1, PAD], I32)
    g.brk = sc.sb("brk", [LOOPS, lanes + 1])
    g.head_run = sc.sb("head_run", [LOOPS, lanes])
    g.tail_run = sc.sb("tail_run", [LOOPS, lanes])
    g.whole_up = sc.sb("whole_up", [HEADS, LOOPS])
    g.whole_down = sc.sb("whole_down", [HEADS, LOOPS])
    g.joint = sc.sb("joint", [HEADS, LOOPS])
    g.acc = sc.sb("acc", [P, WIN, ACCW])

    with Scope(nc) as s1:
        rlen = E // RROWS
        src_i = s1.sb("src_i", [RROWS, rlen], I32)
        dst_i = s1.sb("dst_i", [RROWS, rlen], I32)
        pre_i = s1.sb("pre_i", [RROWS, rlen], I32)
        row = [s1.sb(f"row{k}", [RROWS, rlen]) for k in range(4)]
        pre = s1.sb("pre", [RROWS, rlen])
        ones = s1.sb("ones", [RROWS, rlen])
        junk = s1.sb("junk", [RROWS, rlen])
        below = s1.sb("below", [RROWS, WIN - 1])
        turn_at = s1.sb("turn_at", [P, WIN - 1])
        steps = s1.sb("steps", [P, STEPS])
        order = s1.sb("order", [P, WIN - 1])
        eight = s1.sb("eight", [P, 1])
        win = s1.sb("win", [P, STEPS])
        win2 = s1.sb("win2", [P, STEPS])
        tile = s1.sb("tile", [P, STEPS])
        pick = s1.sb("pick", [RROWS, TPR, STEPS])
        got = s1.sb("got", [P, STEPS])
        valid = s1.sb("valid", [P, STEPS])
        half = STEPS // 2

        with Scope(nc) as s2:
            loaded, pre_set, zeroed, drawn = (s2.sem(x) for x in ("loaded", "pre_set", "zeroed", "drawn"))
            step, counted, totals = s2.sem("step"), s2.sem("counted"), s2.sem("totals")
            total = s2.ps("total", [P, 512])
            block = s2.block()

            @block.sync
            def _(sp):
                sp.dma_start(src_i[:, :], src.rearrange("(r l) -> r l", l=rlen)).then_inc(loaded, 16)
                sp.dma_start(dst_i[:, :], dst.rearrange("(r l) -> r l", l=rlen)).then_inc(loaded, 16)
                sp.dma_start(row[2][:, :], edge_weight.rearrange("(r l) -> r l", l=rlen)).then_inc(loaded, 16)
                sp.dma_start(pre_i[1:RROWS, :], dst[rlen - 1:E - 1].rearrange("(r l) -> r l", l=rlen)).then_inc(loaded, 16)
                sp.dma_start(pre_i[0:1, 1:rlen], dst[0:rlen - 1].rearrange("(r l) -> r l", r=1)).then_inc(loaded, 16)

            @block.gpsimd
            def _(pool):
                pool.memset(pre_i[0:1, 0:1], -1).then_inc(pre_set, 1)
                pool.memset(g.ident[:, :], 0.0).then_inc(zeroed, 1)
                pool.wait_ge(zeroed, 1)
                pool.affine_select(out=g.ident[:, :], in_=g.ident[:, :], compare_op=ALU.not_equal, fill=1.0, base=0,
                                   pattern=[[-1, 128]], channel_multiplier=1).then_inc(drawn, 1)
                for out, pattern, base, by in ((g.iota, [[1, P]], 0, 0), (steps, [[1, STEPS]], 0, 0),
                                               (order, [[1, WIN - 1]], 1, 0), (eight, [[0, 1]], 0, TPR)):
                    pool.iota(out[:, :], pattern=pattern, base=base, channel_multiplier=by,
                              allow_small_or_imprecise_dtypes=True).then_inc(drawn, 1)

            @block.vector
            def _(dve):
                link = Link(dve, step)
                link(dve.memset(g.eps[:, :], EPS))
                link(dve.memset(ones[:, :], 1.0))
                for t, v in ((g.idx, 0), (g.src, 0.0), (g.slot, -1.0), (g.first, 0.0), (g.ew, 0.0), (g.key, -1.0), (g.src_key, -2000.0), (g.near, 0), (g.win_i, 0)):
                    link(dve.memset(t[:, STEPS:PAD], v))
                dve.wait_ge(loaded, 16 * 5)
                dve.wait_ge(pre_set, 1)
                link(dve.tensor_copy(row[0][:, :], src_i[:, :]))
                link(dve.tensor_copy(row[1][:, :], dst_i[:, :]))
                link(dve.tensor_copy(pre[:, :], pre_i[:, :]))
                link(dve.tensor_tensor(row[3][:, :], row[1][:, :], pre[:, :], ALU.not_equal))
                for w in range(1, WIN):
                    link(dve.scalar_tensor_tensor(out=junk[:, :], in0=row[1][:, :], scalar=float(P * w), in1=ones[:, :],
                                                  op0=ALU.is_lt, op1=ALU.mult, accum_out=below[:, w - 1:w]))
                dve.sem_inc(counted, 1)
                dve.wait_ge(totals, 1)
                link(dve.tensor_scalar(turn_at[:, :], total[:, 0:WIN - 1], -float(P // 2), 1.0 / P, ALU.add, ALU.mult))
                link(dve.tensor_scalar(turn_at[:, :], turn_at[:, :], ROUND, None, ALU.add))
                link(dve.tensor_scalar(turn_at[:, :], turn_at[:, :], -ROUND, float(TILES - 1), ALU.add, ALU.min))
                dve.wait_ge(drawn, 5)
                link(dve.tensor_tensor(turn_at[:, :], turn_at[:, :], order[:, :], ALU.add))
                link(dve.memset(win[:, :], 0.0))
                a, b = win, win2
                for w in range(WIN - 1):
                    link(dve.scalar_tensor_tensor(out=b[:, :], in0=steps[:, :], scalar=turn_at[:, w:w + 1], in1=a[:, :],
                                                  op0=ALU.is_ge, op1=ALU.add))
                    a, b = b, a
                link(dve.tensor_copy(g.win_i[:, 0:STEPS], a[0:1, :]))
                link(dve.tensor_tensor(tile[:, :], steps[:, :], a[:, :], ALU.subtract))
                link(dve.tensor_scalar(tile[:, :], tile[:, :], eight[:, :], None, ALU.subtract))
                for b8 in range(TPR):
                    link(dve.tensor_scalar(pick[:, b8, :], tile[0:RROWS, :], float(b8), None, ALU.is_equal))

            @block.tensor
            def _(pe):
                pe.wait_ge(counted, 1)
                pe.matmul(total[:, 0:WIN - 1], ones[:, 0:P], below[:, :], start=True, stop=True).then_inc(totals, 1)
        assert (WIN - 1) % 2 == 0

        with Scope(nc) as s2:
            bank = s2.ps("bank", [P, 8, 512])
            step, picked = s2.sem("step"), s2.sem("picked")
            block = s2.block()

            @block.tensor
            def _(pe):
                for k in range(4):
                    for h in range(2):
                        for b8 in range(TPR):
                            ins = pe.matmul(bank[:, 2 * k + h, 0:half], row[k][:, b8 * P:(b8 + 1) * P],
                                            pick[:, b8, h * half:(h + 1) * half], start=b8 == 0, stop=b8 == TPR - 1)
                    ins.then_inc(picked, 1)

            @block.vector
            def _(dve):
                link = Link(dve, step)

                def two(t):
                    return t.rearrange("p (h s) -> p h s", h=2)

                dve.wait_ge(picked, 4)
                link(dve.tensor_copy(two(g.src[:, 0:STEPS]), bank[:, 0:2, 0:half]))
                link(dve.tensor_copy(g.idx[:, 0:STEPS], g.src[:, 0:STEPS]))
                link(dve.tensor_copy(two(got[:, :]), bank[:, 2:4, 0:half]))
                link(dve.tensor_copy(two(g.ew[:, 0:STEPS]), bank[:, 4:6, 0:half]))
                link(dve.tensor_copy(two(g.first[:, 0:STEPS]), bank[:, 6:8, 0:half]))
                link(dve.scalar_tensor_tensor(out=g.slot[:, 0:STEPS], in0=win[:, :], scalar=-float(P), in1=got[:, :], op0=ALU.mult, op1=ALU.add))
                link(dve.tensor_scalar(valid[:, :], g.slot[:, 0:STEPS], 0.0, None, ALU.is_ge))
                link(dve.scalar_tensor_tensor(out=valid[:, :], in0=g.slot[:, 0:STEPS], scalar=float(P), in1=valid[:, :], op0=ALU.is_lt, op1=ALU.mult))
                link(dve.scalar_tensor_tensor(out=g.key[:, 0:STEPS], in0=got[:, :], scalar=1.0, in1=valid[:, :], op0=ALU.add, op1=ALU.mult))
                link(dve.tensor_scalar(g.key[:, 0:STEPS], g.key[:, 0:STEPS], -1.0, None, ALU.add))
                link(dve.tensor_copy(g.near[:, 0:STEPS], got[:, :]))
                link(dve.scalar_tensor_tensor(out=g.src_key[:, 0:STEPS], in0=g.src[:, 0:STEPS], scalar=2000.0 - N // 2, in1=valid[:, :], op0=ALU.add, op1=ALU.mult))
                link(dve.tensor_scalar(g.src_key[:, 0:STEPS], g.src_key[:, 0:STEPS], -2000.0, None, ALU.add))

    with Scope(nc) as s1:
        krow = s1.sb("krow", [LOOPS, lanes])
        cols = s1.sb("cols", [LOOPS, 3, HEADS])
        edge = s1.sb("edge", [HEADS, 3, LOOPS])
        bank = s1.ps("bank", [128, 8, 512])
        step, turned, cols_ready, cols_turned = (s1.sem(x) for x in ("step", "turned", "cols_ready", "cols_turned"))
        block = s1.block()

        @block.tensor
        def _(pe):
            kv = g.key[:, 0:STEPS].rearrange("p (c b) -> p c b", b=PAIR)
            for b in range(PAIR):
                ins = pe.transpose(bank[0:LOOPS, b // 4, (b % 4) * P:(b % 4 + 1) * P], kv[:, :, b], g.ident[0:P, 0:P])
            ins.then_inc(turned, 1)
            pe.wait_ge(cols_ready, 1)
            for k in range(3):
                ins = pe.transpose(bank[0:HEADS, 2 + k, 0:LOOPS], cols[:, k, :], g.ident[0:LOOPS, 0:LOOPS])
            ins.then_inc(cols_turned, 1)

        @block.vector
        def _(dve):
            link = Link(dve, step)
            dve.wait_ge(turned, 1)
            link(dve.tensor_copy(krow[:, :].rearrange("p (a l) -> p a l", a=2), bank[0:LOOPS, 0:2, 0:4 * P]))
            link(dve.memset(g.brk[:, :], 0.0))
            link(dve.tensor_tensor(g.brk[:, 1:lanes], krow[:, 1:lanes], krow[:, 0:lanes - 1], ALU.not_equal))
            link(dve.tensor_scalar(g.brk[:, 1:lanes], g.brk[:, 1:lanes], -BIG, None, ALU.mult))
            link(dve.tensor_tensor_scan(g.head_run[:, :], g.brk[:, 0:lanes], g.brk[:, 0:lanes], 0.0, ALU.min, ALU.min))
            back = g.brk[:, 1:lanes + 1][:, ::-1]
            link(dve.tensor_tensor_scan(g.tail_run[:, ::-1], back, back, 0.0, ALU.min, ALU.min))
            for k, c in enumerate((krow[:, 0:1], krow[:, lanes - 1:lanes], g.head_run[:, lanes - 1:lanes])):
                link(dve.tensor_copy(cols[:, k, :], c.to_broadcast([LOOPS, HEADS])))
            dve.sem_inc(cols_ready, 1)
            dve.wait_ge(cols_turned, 1)
            link(dve.tensor_copy(edge[:, :, :], bank[0:HEADS, 2:5, 0:LOOPS]))
            link(dve.memset(g.joint[:, :], -BIG))
            link(dve.tensor_tensor(g.joint[:, 1:LOOPS], edge[:, 0, 1:LOOPS], edge[:, 1, 0:LOOPS - 1], ALU.not_equal))
            link(dve.tensor_scalar(g.joint[:, 1:LOOPS], g.joint[:, 1:LOOPS], -BIG, None, ALU.mult))
            link(dve.tensor_tensor(g.whole_up[:, :], g.joint[:, :], edge[:, 2, :], ALU.add))
            link(dve.memset(g.whole_down[:, :], -BIG))
            link(dve.tensor_tensor(g.whole_down[:, 0:LOOPS - 1], g.joint[:, 1:LOOPS], edge[:, 2, 0:LOOPS - 1], ALU.add))



def by_window(table):
    return table.rearrange("(w p) f -> p w f", p=P)


def column(v):
    return v.rearrange("(f a) -> f a", a=1)


def layer0(nc, g, a, x, table):
    with Scope(nc) as sc:
        cur = sc.sb("cur", [P, WIN, D])
        ft = sc.sb("ft", [128, N])
        ht = sc.sb("ht", [128, N])
        w1 = sc.sb("w1", [128, 3, D])
        w2 = sc.sb("w2", [128, 3, D])
        cols = sc.sb("cols", [128, 3, 4])
        pairs = [(w1[:, :, :], a["L0_gnn_W1"].rearrange("l i o -> i l o")), (w2[:, :, :], a["L0_gnn_W2"].rearrange("l i o -> i l o"))]
        for i in range(3):
            for k, n in enumerate(("b1", "b2", "gamma", "beta")):
                pairs.append((cols[:, i, k:k + 1], column(a[f"L0_gnn_{n}"][i, :])))
        load(nc, pairs)
        to_features(nc, g.ident, x, D, ht)
        for i in range(3):
            scatter_to_sources(nc, g, a["x"] if i == 0 else table, g.near, ft)
            vector_steps(nc, lambda dve, link: link(dve.tensor_tensor(ft[:, :], ft[:, :], ht[:, :], ALU.add)))
            linear_features(nc, ft[:, :], w1[:, i, :], ACT.Relu, cols[:, i, 0:1], ht)
            linear_features(nc, ht[:, :], w2[:, i, :], ACT.Identity, cols[:, i, 1:2], ft)
            with Scope(nc) as s1:
                mean, var, std, gain = (s1.sb(k, [128, 1]) for k in ("mean", "var", "std", "gain"))
                step, var_ready, std_ready = s1.sem("step"), s1.sem("var_ready"), s1.sem("std_ready")
                block = s1.block()

                @block.vector
                def _(dve):
                    link = Link(dve, step)
                    link(dve.tensor_reduce(mean[:, :], ft[:, :], AX_X, ALU.add))
                    link(dve.tensor_scalar(mean[:, :], mean[:, :], 1.0 / N, None, ALU.mult))
                    link(dve.tensor_scalar(ft[:, :], ft[:, :], mean[:, :], None, ALU.subtract))
                    link(dve.tensor_tensor(ht[:, :], ft[:, :], ft[:, :], ALU.mult))
                    dve.tensor_reduce(var[:, :], ht[:, :], AX_X, ALU.add).then_inc(var_ready, 1)
                    dve.wait_ge(std_ready, 1)
                    link(dve.reciprocal(gain[:, :], std[:, :]))
                    link(dve.tensor_tensor(gain[:, :], gain[:, :], cols[:, i, 2:3], ALU.mult))
                    link(dve.tensor_scalar(ft[:, :], ft[:, :], gain[:, :], cols[:, i, 3:4], ALU.mult, ALU.add))

                @block.scalar
                def _(act):
                    act.wait_ge(var_ready, 1)
                    act.activation(std[:, :], var[:, :], ACT.Sqrt, bias=g.eps[:, :], scale=1.0 / N).then_inc(std_ready, 1)
            to_nodes(nc, g.ident, ft, cur)
            vector_steps(nc, lambda dve, link: link(dve.tensor_copy(ht[:, :], ft[:, :])))
            if i < 2:
                load(nc, [(by_window(table), cur[:, :, :])])
        normalize(nc, x[:, :, :], g.eps, before=lambda dve, link: link(dve.tensor_tensor(x[:, :, :], x[:, :, :], cur[:, :, :], ALU.add)))


def layer1(nc, g, a, x, table, spill):
    with Scope(nc) as sc:
        h = sc.sb("h", [P, WIN, D])
        ft = sc.sb("ft", [128, N])
        xr = sc.sb("xr", [P, WIN, D])
        xl = sc.sb("xl", [P, WIN, D + HEADS + 1])
        win = sc.sb("win", [128, HID])
        wout = sc.sb("wout", [128, D])
        low = HYPER // P
        hw = sc.sb("hw", [P, low + 1])
        bin_ = sc.sb("bin", [HID, 1])
        bout = sc.sb("bout", [P, D])
        load(nc, [(win[:, :], a["L1_gnn_W_in"]), (wout[:, :], a["L1_gnn_W_out"]), (bin_[:, :], column(a["L1_gnn_b_in"])),
                  (bout[:, :], a["L1_gnn_b_out"].partition_broadcast(P)),
                  (hw[:, 0:low], a["L2_gnn_hyperedge_weight"].rearrange("(w p) -> p w", p=P)),
                  (hw[:, low:low + 1], a["L2_gnn_hyperedge_weight"][HYPER - 1:HYPER].partition_broadcast(P))])

        def look_up(dve, link):
            link(dve.tensor_copy(xl[:, 0:low, D + HEADS:], hw[:, 0:low].unsqueeze(2)))
            link(dve.tensor_copy(xl[:, low:WIN, D + HEADS:], rows_of(hw[:, low:low + 1], WIN - low)))

        vector_steps(nc, look_up)
        to_features(nc, g.ident, x, D, ft)
        with Scope(nc) as s1:
            f0 = s1.sb("f0", [HID, N])
            linear_features(nc, ft[:, :], win[:, :], ACT.Gelu, bin_[:, :], f0)
            vector_steps(nc, lambda dve, link: link(dve.tensor_copy(ft[0:HID, :], f0[:, :])))
        for i in range(3):
            k = HID if i == 0 else D
            with Scope(nc) as s1:
                wl = s1.sb("wl", [k, D])
                wr = s1.sb("wr", [k, D])
                row = s1.sb("row", [P, 6, D])
                logit = s1.sb("logit", [P, STEPS, HEADS])
                capped = s1.sb("capped", [P, STEPS, HEADS])
                ls = s1.sb("ls", [P, WIN, HEADS])
                names = [a[f"L1_gnn_{n}{i}"] for n in ("bl", "br", "att", "bo", "g", "be")]
                names[2] = names[2].rearrange("h c -> (h c)")
                load(nc, [(wl[:, :], a[f"L1_gnn_Wl{i}"]), (wr[:, :], a[f"L1_gnn_Wr{i}"])]
                     + [(row[:, n, :], v.partition_broadcast(P)) for n, v in enumerate(names)])
                bl, br, att, bo, gain, shift = (row[:, n, :] for n in range(6))
                linear_nodes(nc, [(ft[0:k, :], wl[:, :])], bl, xl)
                linear_nodes(nc, [(ft[0:k, :], wr[:, :])], br, xr)
                load(nc, [(by_window(table), xr[:, :, :])])
                with Scope(nc) as s2:
                    z = s2.sb("z", [P, WIN, D])

                    def self_logits(dve, link):
                        link(dve.tensor_tensor(z[:, :, :], xl[:, :, 0:D], xr[:, :, :], ALU.add))
                        link(dve.scalar_tensor_tensor(out=z[:, :, :], in0=z[:, :, :], scalar=0.2, in1=z[:, :, :], op0=ALU.mult, op1=ALU.max))
                        link(dve.tensor_tensor(z[:, :, :], z[:, :, :], rows_of(att, WIN), ALU.mult))
                        link(dve.tensor_reduce(ls[:, :, :], z[:, :, :].rearrange("p w (h c) -> p w h c", h=HEADS), AX_X, ALU.add))
                        link(dve.tensor_copy(xl[:, :, D:D + HEADS], ls[:, :, :]))

                    vector_steps(nc, self_logits)
                attention_logits(nc, g, table, xl, att, spill, logit, capped, g.hyper if i == 0 else None)
                softmax_weights(nc, g, logit, capped, capped)
                attention_sums(nc, g, spill, logit, capped)
                with Scope(nc) as s2:
                    m = s2.sb("m", [P, WIN, HEADS])
                    some = s2.sb("some", [P, WIN])
                    es = s2.sb("es", [P, WIN, HEADS])
                    step, shifted, exped = s2.sem("step"), s2.sem("shifted"), s2.sem("exped")
                    block = s2.block()
                    heads = lambda t: t.rearrange("p w (h c) -> p w h c", h=HEADS)
                    over = lambda t: t.unsqueeze(3).broadcast_to([P, WIN, HEADS, HID])

                    @block.vector
                    def _(dve):
                        link = Link(dve, step)
                        link(dve.tensor_scalar(some[:, :].unsqueeze(2), g.acc[:, :, ACCW - 1:ACCW], 0.0, -BIG, ALU.is_equal, ALU.mult))
                        link(dve.tensor_tensor(m[:, :, :], g.acc[:, :, D + HEADS:ACCW - 1], each(some[:, :], HEADS), ALU.add))
                        link(dve.tensor_tensor(m[:, :, :], m[:, :, :], ls[:, :, :], ALU.max))
                        dve.tensor_tensor(m[:, :, :], ls[:, :, :], m[:, :, :], ALU.subtract).then_inc(shifted, 1)
                        dve.wait_ge(exped, 1)
                        link(dve.tensor_tensor(heads(xr[:, :, :]), heads(xr[:, :, :]), over(es[:, :, :]), ALU.mult))
                        link(dve.tensor_tensor(xr[:, :, :], xr[:, :, :], g.acc[:, :, 0:D], ALU.add))
                        link(dve.tensor_tensor(m[:, :, :], es[:, :, :], g.acc[:, :, D:D + HEADS], ALU.add))
                        link(dve.tensor_scalar(m[:, :, :], m[:, :, :], 1e-16, None, ALU.add))
                        link(dve.reciprocal(m[:, :, :], m[:, :, :]))
                        link(dve.tensor_tensor(heads(xr[:, :, :]), heads(xr[:, :, :]), over(m[:, :, :]), ALU.mult))
                        link(dve.tensor_tensor(xr[:, :, :], xr[:, :, :], rows_of(bo, WIN), ALU.add))

                    @block.scalar
                    def _(act):
                        act.wait_ge(shifted, 1)
                        act.activation(es[:, :, :], m[:, :, :], ACT.Exp).then_inc(exped, 1)
                def keep(dve, link):
                    if i == 0:
                        link(dve.tensor_copy(h[:, :, :], xr[:, :, :]))
                    else:
                        link(dve.tensor_tensor(h[:, :, :], h[:, :, :], xr[:, :, :], ALU.add))

                normalize(nc, xr[:, :, :], g.eps, gain=gain, shift=shift, func=ACT.Gelu, after=keep)
                to_features(nc, g.ident, h, D, ft)
        linear_nodes(nc, [(ft[:, :], wout[:, :])], bout[:, :], h)
        with Scope(nc) as s1:
            sq = s1.sb("sq", [P, WIN, D])
            length = s1.sb("length", [P, WIN])
            root = s1.sb("root", [P, WIN])
            step, summed, rooted = s1.sem("step"), s1.sem("summed"), s1.sem("rooted")
            block = s1.block()

            @block.vector
            def _(dve):
                link = Link(dve, step)
                link(dve.tensor_tensor(sq[:, :, :], h[:, :, :], h[:, :, :], ALU.mult))
                dve.tensor_reduce(length[:, :], sq[:, :, :], AX_X, ALU.add).then_inc(summed, 1)
                dve.wait_ge(rooted, 1)
                link(dve.tensor_scalar(root[:, :], root[:, :], 1e-12, None, ALU.max))
                link(dve.reciprocal(root[:, :], root[:, :]))
                link(dve.tensor_tensor(h[:, :, :], h[:, :, :], each(root[:, :], D), ALU.mult))

            @block.scalar
            def _(act):
                act.wait_ge(summed, 1)
                act.activation(root[:, :], length[:, :], ACT.Sqrt).then_inc(rooted, 1)
        normalize(nc, x[:, :, :], g.eps, before=lambda dve, link: link(dve.tensor_tensor(x[:, :, :], x[:, :, :], h[:, :, :], ALU.add)))


def layer2(nc, g, a, x, table):
    low = HYPER // P
    with Scope(nc) as sc:
        dv = sc.sb("dv", [P, WIN])
        y = sc.sb("y", [P, WIN, D])
        he = sc.sb("he", [P, low, D])
        hw = sc.sb("hw", [P, low])
        de = sc.sb("de", [P, low])
        idx = sc.sb("idx", [P, PAD], I32)
        key = sc.sb("key", [P, PAD])
        ft = sc.sb("ft", [128, N])
        w = sc.sb("w", [128, D])
        wt = sc.sb("wt", [128, D])
        bias = sc.sb("bias", [P, D])
        load(nc, [(hw[:, :], a["L2_gnn_hyperedge_weight"].rearrange("(w p) -> p w", p=P)), (w[:, :], a["L2_gnn_W"]),
                  (bias[:, :], a["L2_gnn_b"].partition_broadcast(P))])
        source_weights(nc, g, g.hyper, dv[:, :])
        with Scope(nc) as s1:
            root = s1.sb("root", [P, WIN])
            turn = s1.ps("turn", [128, 512])
            step, clipped, rooted, turned = s1.sem("step"), s1.sem("clipped"), s1.sem("rooted"), s1.sem("turned")
            block = s1.block()

            @block.tensor
            def _(pe):
                pe.transpose(turn[:, 0:D], w[:, :], g.ident[:, :]).then_inc(turned, 1)

            @block.vector
            def _(dve):
                link = Link(dve, step)
                dve.tensor_scalar(dv[:, :], dv[:, :], 1.0, None, ALU.max).then_inc(clipped, 1)
                dve.wait_ge(rooted, 1)
                link(dve.reciprocal(dv[:, :], root[:, :]))
                link(dve.tensor_tensor(y[:, :, :], x[:, :, :], each(dv[:, :], D), ALU.mult))
                link(dve.tensor_scalar(key[:, :], g.key[:, :], float(HYPER - 1), 0.0, ALU.min, ALU.max))
                link(dve.tensor_copy(idx[:, :], key[:, :]))
                dve.wait_ge(turned, 1)
                link(dve.tensor_copy(wt[:, :], turn[:, 0:D]))

            @block.scalar
            def _(act):
                act.wait_ge(clipped, 1)
                act.activation(root[:, :], dv[:, :], ACT.Sqrt).then_inc(rooted, 1)
        load(nc, [(by_window(table), y[:, :, :])])
        neighbour_sums(nc, g, table)

        def hyperedges(dve, link):
            link(dve.tensor_scalar(de[:, :].unsqueeze(2), g.acc[:, 0:low, D:D + 1], 1.0, None, ALU.max))
            link(dve.reciprocal(de[:, :], de[:, :]))
            link(dve.tensor_tensor(de[:, :], de[:, :], hw[:, :], ALU.mult))
            link(dve.tensor_tensor(he[:, :, :], g.acc[:, 0:low, 0:D], each(de[:, :], D), ALU.mult))

        vector_steps(nc, hyperedges)
        load(nc, [(by_window(table[0:HYPER, :]), he[:, :, :])])
        scatter_to_sources(nc, g, table, idx, ft)
        linear_nodes(nc, [(ft[:, :], wt[:, :])], None, y)

        def scale(dve, link):
            link(dve.tensor_tensor(y[:, :, :], y[:, :, :], each(dv[:, :], D), ALU.mult))
            link(dve.tensor_tensor(y[:, :, :], y[:, :, :], rows_of(bias[:, :], WIN), ALU.add))
            link(dve.tensor_tensor(x[:, :, :], x[:, :, :], y[:, :, :], ALU.add))

        normalize(nc, x[:, :, :], g.eps, before=scale)


def layer3(nc, g, a, x, table):
    with Scope(nc) as sc:
        ft = sc.sb("ft", [128, N])
        at = sc.sb("at", [128, N])
        pa = sc.sb("pa", [P, WIN, D])
        pb = sc.sb("pb", [P, WIN, D])
        m1 = sc.sb("m1", [128, 2, D])
        u1 = sc.sb("u1", [128, 2, D])
        m2 = sc.sb("m2", [128, D])
        u2 = sc.sb("u2", [128, D])
        row = sc.sb("row", [P, 7, D])
        n3 = lambda n: a[f"L3_gnn_{n}"]
        rows = [n3("mW1")[2 * D, :], n3("mb1"), n3("mb2"), n3("ub1"), n3("ln_g"), n3("ln_b"), n3("ub2")]
        load(nc, [(m1[:, :, :], n3("mW1")[0:2 * D, :].rearrange("(b i) o -> i b o", b=2)),
                  (u1[:, :, :], n3("uW1").rearrange("(b i) o -> i b o", b=2)), (m2[:, :], n3("mW2")), (u2[:, :], n3("uW2"))]
             + [(row[:, n, :], v.partition_broadcast(P)) for n, v in enumerate(rows)])
        w_edge, mb1, mb2, ub1, ln_g, ln_b, ub2 = (row[:, n, :] for n in range(7))
        to_features(nc, g.ident, x, D, ft)
        linear_nodes(nc, [(ft[:, :], m1[:, 0, :])], None, pa)
        linear_nodes(nc, [(ft[:, :], m1[:, 1, :])], mb1, pb)
        load(nc, [(by_window(table), pa[:, :, :])])
        message_sums(nc, g, table, pb, w_edge)
        to_features(nc, g.ident, g.acc, D, at)
        linear_nodes(nc, [(at[:, :], m2[:, :])], None, pa)

        def bias(dve, link):
            link(dve.tensor_tensor(pb[:, :, :], rows_of(mb2, WIN), g.acc[:, :, D:D + 1].broadcast_to([P, WIN, D]), ALU.mult))
            link(dve.tensor_tensor(pa[:, :, :], pa[:, :, :], pb[:, :, :], ALU.add))

        vector_steps(nc, bias)
        to_features(nc, g.ident, pa, D, at)
        linear_nodes(nc, [(ft[:, :], u1[:, 0, :]), (at[:, :], u1[:, 1, :])], ub1, pa)
        normalize(nc, pa[:, :, :], g.eps, gain=ln_g, shift=ln_b, func=ACT.Silu)
        to_features(nc, g.ident, pa, D, at)
        linear_nodes(nc, [(at[:, :], u2[:, :])], ub2, pa)

        def residual(dve, link):
            link(dve.scalar_tensor_tensor(out=x[:, :, :], in0=x[:, :, :], scalar=2.0, in1=pa[:, :, :], op0=ALU.mult, op1=ALU.add))

        normalize(nc, x[:, :, :], g.eps, before=residual)


def program(nc, a, out, upto=4):
    table = nc.dram_tensor("node_table", (N, D), F32, kind="Internal").ap()
    spill = nc.dram_tensor("gathered", (2 * LOOPS, P, HALF * D), F32, kind="Internal").ap()
    g = Graph()
    with Scope(nc) as sc:
        prepare(nc, g, sc, a["src"], a["dst"], a["edge_weight"])
        x = sc.sb("x", [P, WIN, D])
        load(nc, [(x[:, :, :], by_window(a["x"]))])
        with Scope(nc) as s1:
            layer0(nc, g, a, x, table)
        g.hyper = sc.sb("hyper", [P, PAD])
        if upto >= 2:
            layer1(nc, g, a, x, table, spill)
        if upto >= 3:
            layer2(nc, g, a, x, table)
        if upto >= 4:
            layer3(nc, g, a, x, table)
        load(nc, [(by_window(out), x[:, :, :])])


_INS = ['x', 'src', 'dst', 'edge_weight'] + [f'L0_gnn_{n}' for n in ('W1', 'b1', 'W2', 'b2', 'gamma', 'beta')] + [
    'L1_gnn_W_in', 'L1_gnn_b_in'] + [f'L1_gnn_{n}{i}' for i in range(3) for n in ('Wl', 'bl', 'Wr', 'br', 'att', 'bo', 'g', 'be')] + [
    'L1_gnn_W_out', 'L1_gnn_b_out', 'L2_gnn_hyperedge_weight', 'L2_gnn_W', 'L2_gnn_b'] + [
    f'L3_gnn_{n}' for n in ('mW1', 'mb1', 'mW2', 'mb2', 'uW1', 'ub1', 'ln_g', 'ln_b', 'uW2', 'ub2')]


def kernel(**inputs):
    import numpy as _np
    import concourse.bacc as _bacc
    from concourse.bass_utils import run_bass_kernel_spmd as _run

    nc = _bacc.Bacc("TRN2", target_bir_lowering=False, num_devices=1)
    arrays, args = {}, {}
    for name in _INS:
        v = _np.ascontiguousarray(inputs[name])
        arrays[f"in_{name}"] = v
        args[name] = nc.dram_tensor(f"in_{name}", v.shape, mybir.dt.from_np(v.dtype), kind="ExternalInput").ap()
    out = nc.dram_tensor("out", (N, D), F32, kind="ExternalOutput").ap()
    program(nc, args, out)
    r = _run(nc, [arrays], core_ids=[0])
    return r.results[0]["out"]
```

```python
from contextlib import ExitStack
from itertools import count

import concourse.bass as bass
from concourse import mybir

F32 = mybir.dt.float32
BF16 = mybir.dt.bfloat16
F16 = mybir.dt.float16
I32 = mybir.dt.int32
ALU = mybir.AluOpType
ACT = mybir.ActivationFunctionType
AX_X = mybir.AxisListType.X

N = 3125
E = 100000
D = 128
HYPER = 625
HEADS, HID = 4, 32
P = 125
WIN = N // P
TILES = E // P
RROWS = 100
TPR = TILES // RROWS
STEPS = TILES + WIN - 1
HALF = 4
PAIR = 2 * HALF
LOOPS = STEPS // PAIR
PAD = STEPS + PAIR
ACCW = D + 2 * HEADS + 1
BIG = 1.0e30
ROUND = 12582912.0
EPS = 1e-5
GROUPS = (WIN + 3) // 4
TEAM = 4
TEAMS = (STEPS + (TEAM - 1) * WIN) // TEAM // 2 * 2
CHUNK = 391
SIDE = 4 * CHUNK
FEW = 256
FIVE = 5
assert (STEPS + (TEAM - 1) * WIN) // TEAM % 2 == 0 and 2 * SIDE >= N and WIN % FIVE == 0
assert STEPS % PAIR == 0 and WIN * P == N and TILES * P == E


class Link:

    def __init__(self, eng, sem):
        self.eng, self.sem, self.n = eng, sem, 0

    def __call__(self, ins):
        ins.then_inc(self.sem, 1)
        self.n += 1
        self.eng.wait_ge(self.sem, self.n)


def each(ap, n):
    return ap.unsqueeze(2).broadcast_to([ap.shape[0], ap.shape[1], n])


def rows_of(ap, n):
    return ap.unsqueeze(1).broadcast_to([ap.shape[0], n, ap.shape[1]])


def windows(g):
    return range(4 * g, min(4 * g + 4, WIN))


def span(g):
    return len(windows(g)) * P


class Scope:

    stages = count()

    def __init__(self, nc):
        self.nc, self.ctx, self.stage, self.used = nc, ExitStack(), next(Scope.stages), []

    def __enter__(self):
        self.ctx.__enter__()
        return self

    def __exit__(self, *a):
        self.ctx.close()
        if self.used:
            rest = list(self.nc.free_semaphores)
            self.nc.clear_and_free_semaphores(self.used)
            freed = [n for n in self.nc.free_semaphores if n not in rest]
            self.nc.reset_free_semaphores(rest + freed)

    def sb(self, name, shape, dt=F32):
        return self.ctx.enter_context(self.nc.sbuf_tensor(f"{name}_{self.stage}", shape, dt))

    def ps(self, name, shape, dt=F32):
        return self.ctx.enter_context(self.nc.psum_tensor(f"{name}_{self.stage}", shape, dt))

    def sem(self, name):
        self.used.append(self.nc.alloc_semaphore(f"{name}_{self.stage}"))
        return self.used[-1]

    def sems(self, name):
        return [self.sem(f"{name}{p}") for p in range(2)]

    def block(self):
        return self.ctx.enter_context(self.nc.Block())



def load(nc, pairs):
    with Scope(nc) as sc:
        loaded = sc.sem("loaded")
        block = sc.block()

        @block.sync
        def _(sp):
            for dst, src in pairs:
                sp.dma_start(dst, src, allow_slow_non_contiguous=dst.shape[0] * dst.shape[-1] < 1000).then_inc(loaded, 16)
            sp.wait_ge(loaded, 16 * len(pairs))


def to_features(nc, ident, src, width, dst):
    with Scope(nc) as sc:
        bank = sc.ps("bank", [128, GROUPS, 512])
        turned = sc.sem("turned")
        block = sc.block()

        @block.tensor
        def _(pe):
            for g in range(GROUPS):
                for w in windows(g):
                    ins = pe.transpose(bank[0:width, g, (w % 4) * P:(w % 4 + 1) * P], src[:, w, 0:width], ident[0:P, 0:P])
                ins.then_inc(turned, 1)

        @block.scalar
        def _(act):
            for g in range(GROUPS):
                act.wait_ge(turned, g + 1)
                act.copy(dst[0:width, 4 * g * P:4 * g * P + span(g)], bank[0:width, g, 0:span(g)])


def to_nodes(nc, ident, src, dst):
    with Scope(nc) as sc:
        bank = sc.ps("bank", [128, GROUPS, 512])
        turned = sc.sem("turned")
        block = sc.block()

        @block.tensor
        def _(pe):
            for g in range(GROUPS):
                for w in windows(g):
                    ins = pe.transpose(bank[0:P, g, (w % 4) * D:(w % 4 + 1) * D], src[:, w * P:(w + 1) * P], ident[:, :])
                ins.then_inc(turned, 1)

        @block.scalar
        def _(act):
            for g in range(GROUPS):
                n = len(windows(g))
                act.wait_ge(turned, g + 1)
                act.copy(dst[:, 4 * g:4 * g + n, 0:D], bank[0:P, g, 0:n * D].rearrange("p (w f) -> p w f", f=D))


def linear_nodes(nc, terms, bias, dst):
    with Scope(nc) as sc:
        bank = sc.ps("bank", [128, GROUPS, 512])
        summed = sc.sem("summed")
        block = sc.block()

        @block.tensor
        def _(pe):
            for g in range(GROUPS):
                for w in windows(g):
                    for n, (x, m) in enumerate(terms):
                        ins = pe.matmul(bank[0:P, g, (w % 4) * D:(w % 4 + 1) * D], x[:, w * P:(w + 1) * P], m,
                                        start=n == 0, stop=n == len(terms) - 1)
                ins.then_inc(summed, 1)

        @block.vector
        def _(dve):
            for g in range(GROUPS):
                n = len(windows(g))
                dve.wait_ge(summed, g + 1)
                got = bank[0:P, g, 0:n * D].rearrange("p (w f) -> p w f", f=D)
                if bias is None:
                    dve.tensor_copy(dst[:, 4 * g:4 * g + n, 0:D], got)
                else:
                    dve.tensor_tensor(dst[:, 4 * g:4 * g + n, 0:D], got, rows_of(bias, n), ALU.add)


def linear_features(nc, x, w, func, bias, dst):
    m = w.shape[1]
    with Scope(nc) as sc:
        bank = sc.ps("bank", [128, GROUPS, 512])
        summed = sc.sem("summed")
        block = sc.block()

        @block.tensor
        def _(pe):
            for g in range(GROUPS):
                pe.matmul(bank[0:m, g, 0:span(g)], w, x[:, 4 * g * P:4 * g * P + span(g)],
                          start=True, stop=True).then_inc(summed, 1)

        @block.scalar
        def _(act):
            for g in range(GROUPS):
                act.wait_ge(summed, g + 1)
                act.activation(dst[0:m, 4 * g * P:4 * g * P + span(g)], bank[0:m, g, 0:span(g)], func, bias=bias)


def normalize(nc, y, eps, before=None, gain=None, shift=None, func=None, after=None):
    with Scope(nc) as sc:
        sq = sc.sb("sq", [P, WIN, D])
        mean = sc.sb("mean", [P, WIN])
        var = sc.sb("var", [P, WIN])
        std = sc.sb("std", [P, WIN])
        rstd = sc.sb("rstd", [P, WIN])
        step = sc.sem("step")
        var_ready, std_ready, scaled, activated = (sc.sem(x) for x in ("var_ready", "std_ready", "scaled", "activated"))
        block = sc.block()

        @block.vector
        def _(dve):
            link = Link(dve, step)
            if before:
                before(dve, link)
            link(dve.tensor_reduce(mean[:, :], y, AX_X, ALU.add))
            link(dve.tensor_scalar(mean[:, :], mean[:, :], 1.0 / D, None, ALU.mult))
            link(dve.tensor_tensor(y, y, each(mean[:, :], D), ALU.subtract))
            link(dve.tensor_tensor(sq[:, :, :], y, y, ALU.mult))
            dve.tensor_reduce(var[:, :], sq[:, :, :], AX_X, ALU.add).then_inc(var_ready, 1)
            dve.wait_ge(std_ready, 1)
            link(dve.reciprocal(rstd[:, :], std[:, :]))
            if gain is None:
                dve.tensor_tensor(y, y, each(rstd[:, :], D), ALU.mult).then_inc(scaled, 1)
            else:
                link(dve.tensor_tensor(y, y, each(rstd[:, :], D), ALU.mult))
                link(dve.tensor_tensor(y, y, rows_of(gain, WIN), ALU.mult))
                dve.tensor_tensor(y, y, rows_of(shift, WIN), ALU.add).then_inc(scaled, 1)
            dve.wait_ge(scaled, 1)
            if func is not None:
                dve.wait_ge(activated, 1)
            if after:
                after(dve, link)

        @block.scalar
        def _(act):
            act.wait_ge(var_ready, 1)
            act.activation(std[:, :], var[:, :], ACT.Sqrt, bias=eps[0:P, :], scale=1.0 / D).then_inc(std_ready, 1)
            if func is not None:
                act.wait_ge(scaled, 1)
                act.activation(y, y, func).then_inc(activated, 1)


def vector_steps(nc, steps):
    with Scope(nc) as sc:
        step = sc.sem("step")
        block = sc.block()

        @block.vector
        def _(dve):
            steps(dve, Link(dve, step))




def prime(eng, *pairs):
    for pair in pairs:
        for sem in pair:
            eng.sem_inc(sem, 1)


def before(i, unit=1):
    return unit * i + 1


def done(i, unit=1):
    return unit * (i + 1) + 1


def landed(i, dmas=1):
    return 16 * dmas * (i + 1)


def hold(eng, sem, value, held_up):
    eng.wait_ge(sem, value)
    eng.sem_inc(held_up, 1)


def gather_rows(pool, i, p, table, rows, now, idx, held_up, freed, staged, rows_in):
    for sem in freed:
        hold(pool, sem[p], before(i), held_up)
    pool.tensor_copy(now[:, p, :], idx[:, bass.ds(PAIR * i + HALF * p, HALF)]).then_inc(staged[p], 1)
    hold(pool, staged[p], done(i), held_up)
    for j in range(HALF):
        pool.indirect_dma_start(rows[:, p, j, 0:D], None, table,
                                bass.IndirectOffsetOnAxis(ap=now[:, p, j:j + 1], axis=0)).then_inc(rows_in[p], 16)


def window_of(eng, g, i, p, j):
    return eng.value_load(g.win_i[0:1, bass.ds(PAIR * i + HALF * p + j, 1)], min_val=0, max_val=WIN - 1)


def one_hot(eng, g, out, i, p):
    return eng.tensor_tensor(out, rows_of(g.iota[0:P, 0:P], HALF),
                             each(g.slot[:, bass.ds(PAIR * i + HALF * p, HALF)], P), ALU.is_equal)


def add_sums(dve, g, i, p, sums, width, summed, added):
    dve.wait_ge(summed[p], done(i))
    for j in range(HALF):
        w = window_of(dve, g, i, p, j)
        if j == 0:
            dve.wait_ge(added[1 - p], before(i + p, HALF))
        dve.wait_ge(added[p], before(i, HALF) + j)
        row = g.acc[:, bass.ds(w, 1), 0:width]
        dve.tensor_tensor(row, row, sums[:, p, j:j + 1, 0:width], ALU.add).then_inc(added[p], 1)


def sum_steps(pe, i, p, onehot, values, sums, width, made, values_ready, summed, added):
    pe.wait_ge(made[p], done(i))
    for sem, count in values_ready:
        pe.wait_ge(sem[p], count)
    pe.wait_ge(added[p], before(i, HALF))
    for j in range(HALF):
        ins = pe.matmul(sums[:, p, j, 0:width], onehot[:, p, j, :], values[:, p, j, 0:width], start=True, stop=True)
    ins.then_inc(summed[p], 1)


def many_pairs(eng, g):
    return eng.value_load(g.many[0:1, 0:1], min_val=0, max_val=1) > 0


def neighbour_sums(nc, g, table, y):
    width = D + 1
    with Scope(nc) as sc:
        rows = sc.sb("rows", [P, 2, HALF, width])
        now = sc.sb("now", [P, 2, HALF], I32)
        held_up = sc.sem("held_up")
        onehot = sc.sb("onehot", [P, 2, HALF, P])
        sums = sc.ps("sums", [P, 2, HALF, 256])
        ones_set, acc_clear, tabled = sc.sem("ones_set"), sc.sem("acc_clear"), sc.sem("tabled")
        staged, rows_in, made, summed, added = (sc.sems(x) for x in ("staged", "rows_in", "made", "summed", "added"))
        block = sc.block()

        @block.sync
        def _(sp):
            with sp.If(many_pairs(sp, g)):
                sp.dma_start(by_window(table), y[:, :, :]).then_inc(tabled, 16)
                sp.wait_ge(tabled, 16)

        @block.gpsimd
        def _(pool):
            with pool.If(many_pairs(pool, g)):
                prime(pool, staged)
                pool.wait_ge(tabled, 16)
                with pool.Fori(0, LOOPS) as i:
                    for p in range(2):
                        gather_rows(pool, i, p, table, rows, now, g.idx, held_up, [summed], staged, rows_in)

        @block.vector
        def _(dve):
            with dve.If(many_pairs(dve, g)):
                prime(dve, made, added)
                dve.memset(rows[:, :, :, D:width], 1.0).then_inc(ones_set, 1)
                dve.memset(g.acc[:, :, :], 0.0).then_inc(acc_clear, 1)
                dve.wait_ge(acc_clear, 1)
                for p in range(2):
                    one_hot(dve, g, onehot[:, p, :, :], 0, p).then_inc(made[p], 1)
                with dve.Fori(0, LOOPS) as i:
                    for p in range(2):
                        add_sums(dve, g, i, p, sums, width, summed, added)
                        one_hot(dve, g, onehot[:, p, :, :], i + 1, p).then_inc(made[p], 1)

        @block.tensor
        def _(pe):
            with pe.If(many_pairs(pe, g)):
                prime(pe, summed)
                pe.wait_ge(ones_set, 1)
                with pe.Fori(0, LOOPS) as i:
                    for p in range(2):
                        sum_steps(pe, i, p, onehot, rows, sums, width, made, [(rows_in, landed(i, HALF))], summed, added)


def turn_one_hot(pe, i, p, ident, onehot, turn, made, turned, copied):
    pe.wait_ge(made[p], done(i))
    pe.wait_ge(copied[p], before(i))
    for j in range(HALF):
        ins = pe.transpose(turn[:, p, j * P:(j + 1) * P], onehot[:, p, j, :], ident[0:P, 0:P])
    ins.then_inc(turned[p], 1)


def copy_turned(act, i, p, turn, onehot_t, turned, spread, copied):
    act.wait_ge(turned[p], done(i))
    act.wait_ge(spread[p], before(i))
    act.copy(onehot_t[:, p, :], turn[:, p, 0:HALF * P]).then_inc(copied[p], 1)


def attention_logits(nc, g, table, xl, att, spill, logit, capped):
    with Scope(nc) as sc:
        rows = sc.sb("rows", [P, 2, HALF, D])
        now = sc.sb("now", [P, 2, HALF], I32)
        held_up = sc.sem("held_up")
        onehot = sc.sb("onehot", [P, 2, HALF, P])
        onehot_t = sc.sb("onehot_t", [P, 2, HALF * P])
        z = sc.sb("z", [P, 2, HALF, D])
        turn = sc.ps("turn", [P, 2, 512])
        zp = sc.ps("zp", [P, 2, HALF, D])
        ep = sc.ps("ep", [P, 2, 512])
        names = ("staged", "rows_in", "made", "turned", "copied", "spread", "added", "leaky", "scaled", "summed", "taken", "spilled", "kept")
        staged, rows_in, made, turned, copied, spread, added, leaky, scaled, summed, taken, spilled, kept = (sc.sems(x) for x in names)
        block = sc.block()

        @block.gpsimd
        def _(pool):
            prime(pool, staged)
            with pool.Fori(0, LOOPS) as i:
                for p in range(2):
                    gather_rows(pool, i, p, table, rows, now, g.idx, held_up, [added, kept], staged, rows_in)

        @block.sync
        def _(sp):
            prime(sp, kept)
            with sp.Fori(0, LOOPS) as i:
                for p in range(2):
                    sp.wait_ge(rows_in[p], landed(i, HALF))
                    sp.dma_start(spill[bass.ds(2 * i + p, 1), :, :].rearrange("a p f -> (a p) f"),
                                 rows[:, p, :, :].rearrange("p j f -> p (j f)")).then_inc(spilled[p], 16)
                    sp.wait_ge(spilled[p], landed(i))
                    sp.sem_inc(kept[p], 1)

        @block.scalar
        def _(act):
            prime(act, copied)
            with act.Fori(0, LOOPS) as i:
                for p in range(2):
                    copy_turned(act, i, p, turn, onehot_t, turned, spread, copied)

        @block.tensor
        def _(pe):
            prime(pe, turned, spread)
            with pe.Fori(0, LOOPS) as i:
                for p in range(2):
                    turn_one_hot(pe, i, p, g.ident, onehot, turn, made, turned, copied)
                    pe.wait_ge(copied[p], done(i))
                    pe.wait_ge(added[p], before(i))
                    pe.wait_ge(taken[p], before(i))
                    for j in range(HALF):
                        w = window_of(pe, g, i, p, j)
                        hot = onehot_t[:, p, j * P:(j + 1) * P]
                        pe.matmul(zp[:, p, j, :], hot, xl[:, bass.ds(w, 1), 0:D].rearrange("p w f -> p (w f)"), start=True, stop=True)
                        ins = pe.matmul(ep[:, p, 8 * j:8 * j + HEADS], hot,
                                        xl[:, bass.ds(w, 1), D:D + HEADS].rearrange("p w f -> p (w f)"), start=True, stop=True)
                    ins.then_inc(spread[p], 1)

        @block.vector
        def _(dve):
            prime(dve, made, added, leaky, scaled, summed, taken)
            for p in range(2):
                one_hot(dve, g, onehot[:, p, :, :], 0, p).then_inc(made[p], 1)
            with dve.Fori(0, LOOPS) as i:
                for p in range(2):
                    s = bass.ds(PAIR * i + HALF * p, HALF)
                    zz = z[:, p, :, :]
                    dve.wait_ge(rows_in[p], landed(i, HALF))
                    dve.wait_ge(spread[p], done(i))
                    dve.wait_ge(summed[p], before(i))
                    dve.tensor_tensor(zz, zp[:, p, :, :], rows[:, p, :, :], ALU.add).then_inc(added[p], 1)
                    dve.wait_ge(turned[p], done(i))
                    one_hot(dve, g, onehot[:, p, :, :], i + 1, p).then_inc(made[p], 1)
                    dve.wait_ge(added[p], done(i))
                    dve.scalar_tensor_tensor(out=zz, in0=zz, scalar=0.2, in1=zz, op0=ALU.mult, op1=ALU.max).then_inc(leaky[p], 1)
                    dve.wait_ge(leaky[p], done(i))
                    dve.tensor_tensor(zz, zz, rows_of(att, HALF), ALU.mult).then_inc(scaled[p], 1)
                    dve.wait_ge(scaled[p], done(i))
                    dve.tensor_reduce(logit[:, s, :], zz.rearrange("p j (h c) -> p j h c", h=HEADS), AX_X, ALU.add).then_inc(summed[p], 1)
                    dve.wait_ge(summed[p], done(i))
                    own = ep[:, p, 0:8 * HALF].rearrange("p (j e) -> p j e", e=8)
                    dve.tensor_tensor(capped[:, s, :], logit[:, s, :], own[:, :, 0:HEADS], ALU.max).then_inc(taken[p], 1)


def softmax_weights(nc, g, logit, capped, first_max):
    lanes = PAIR * P
    with Scope(nc) as sc:
        lrow = sc.sb("lrow", [LOOPS, HEADS, lanes])
        crow = sc.sb("crow", [LOOPS, HEADS, lanes])
        fwd = sc.sb("fwd", [LOOPS, lanes])
        mx = sc.sb("mx", [LOOPS, HEADS, lanes])
        ends = sc.sb("ends", [LOOPS, 2, HEADS])
        ends_t = sc.sb("ends_t", [HEADS, 2, LOOPS])
        run = sc.sb("run", [HEADS, 2, LOOPS])
        carry_t = sc.sb("carry_t", [HEADS, 2, LOOPS])
        carry = sc.sb("carry", [LOOPS, 2, HEADS])
        bank = sc.ps("bank", [128, 8, 512])

        with Scope(nc) as s1:
            turned, copied = s1.sem("turned"), s1.sem("copied")
            block = s1.block()
            jobs = [(a, b, h, q) for a, b in ((logit, lrow), (capped, crow)) for h in range(HEADS) for q in range(2)]

            @block.tensor
            def _(pe):
                for n, (a, b, h, q) in enumerate(jobs):
                    if n >= 8:
                        pe.wait_ge(copied, n - 7)
                    av = a[:, :, h].rearrange("p (c b) -> p c b", b=PAIR)
                    for k in range(4):
                        ins = pe.transpose(bank[0:LOOPS, n % 8, k * P:(k + 1) * P], av[:, :, 4 * q + k], g.ident[0:P, 0:P])
                    ins.then_inc(turned, 1)

            @block.scalar
            def _(act):
                for n, (a, b, h, q) in enumerate(jobs):
                    act.wait_ge(turned, n + 1)
                    act.copy(b[:, h, 4 * q * P:(4 * q + 4) * P], bank[0:LOOPS, n % 8, 0:4 * P]).then_inc(copied, 1)

        with Scope(nc) as s2:
            step, ends_ready, ends_turned, carry_ready, carry_turned = (s2.sem(x) for x in (
                "step", "ends_ready", "ends_turned", "carry_ready", "carry_turned"))
            block = s2.block()

            @block.vector
            def _(dve):
                link = Link(dve, step)
                for h in range(HEADS):
                    link(dve.tensor_tensor_scan(fwd[:, :], g.brk[:, 0:lanes], crow[:, h, :], -BIG, ALU.add, ALU.max))
                    link(dve.tensor_tensor_scan(mx[:, h, ::-1], g.brk[:, 1:lanes + 1][:, ::-1], crow[:, h, ::-1], -BIG, ALU.add, ALU.max))
                    link(dve.tensor_copy(ends[:, 0, h:h + 1], fwd[:, lanes - 1:lanes]))
                    link(dve.tensor_copy(ends[:, 1, h:h + 1], mx[:, h, 0:1]))
                    link(dve.tensor_tensor(mx[:, h, :], mx[:, h, :], fwd[:, :], ALU.max))
                dve.sem_inc(ends_ready, 1)
                dve.wait_ge(ends_turned, 1)
                for k in range(2):
                    link(dve.tensor_copy(ends_t[:, k, :], bank[0:HEADS, k, 0:LOOPS]))
                link(dve.tensor_tensor_scan(run[:, 0, :], g.whole_up[:, :], ends_t[:, 0, :], -BIG, ALU.add, ALU.max))
                link(dve.tensor_tensor_scan(run[:, 1, ::-1], g.whole_down[:, ::-1], ends_t[:, 1, ::-1], -BIG, ALU.add, ALU.max))
                link(dve.memset(carry_t[:, :, :], -BIG))
                link(dve.tensor_tensor(carry_t[:, 0, 1:LOOPS], run[:, 0, 0:LOOPS - 1], g.joint[:, 1:LOOPS], ALU.add))
                link(dve.tensor_tensor(carry_t[:, 1, 0:LOOPS - 1], run[:, 1, 1:LOOPS], g.joint[:, 1:LOOPS], ALU.add))
                dve.sem_inc(carry_ready, 1)
                dve.wait_ge(carry_turned, 1)
                for k in range(2):
                    link(dve.tensor_copy(carry[:, k, :], bank[0:LOOPS, 2 + k, 0:HEADS]))
                for h in range(HEADS):
                    link(dve.scalar_tensor_tensor(out=mx[:, h, :], in0=g.head_run[:, :], scalar=carry[:, 0, h:h + 1], in1=mx[:, h, :], op0=ALU.add, op1=ALU.max))
                    link(dve.scalar_tensor_tensor(out=mx[:, h, :], in0=g.tail_run[:, :], scalar=carry[:, 1, h:h + 1], in1=mx[:, h, :], op0=ALU.add, op1=ALU.max))
                    link(dve.tensor_tensor(lrow[:, h, :], lrow[:, h, :], mx[:, h, :], ALU.subtract))

            @block.tensor
            def _(pe):
                pe.wait_ge(ends_ready, 1)
                for k in range(2):
                    ins = pe.transpose(bank[0:HEADS, k, 0:LOOPS], ends[:, k, :], g.ident[0:LOOPS, 0:LOOPS])
                ins.then_inc(ends_turned, 1)
                pe.wait_ge(carry_ready, 1)
                for k in range(2):
                    ins = pe.transpose(bank[0:LOOPS, 2 + k, 0:HEADS], carry_t[:, k, :], g.ident[0:HEADS, 0:HEADS])
                ins.then_inc(carry_turned, 1)

        with Scope(nc) as s3:
            exped, turned, copied = s3.sem("exped"), s3.sem("turned"), s3.sem("copied")
            block = s3.block()
            jobs = [(a, b, h, q) for h in range(HEADS) for a, b in ((lrow, logit), (mx, first_max)) for q in range(2)]

            @block.scalar
            def _(act):
                for h in range(HEADS):
                    act.activation(lrow[:, h, :], lrow[:, h, :], ACT.Exp).then_inc(exped, 1)

            @block.tensor
            def _(pe):
                for n, (a, b, h, q) in enumerate(jobs):
                    pe.wait_ge(exped, h + 1)
                    if n >= 8:
                        pe.wait_ge(copied, n - 7)
                    for k in range(4):
                        ins = pe.transpose(bank[0:P, n % 8, k * LOOPS:(k + 1) * LOOPS], a[:, h, (4 * q + k) * P:(4 * q + k + 1) * P],
                                           g.ident[0:LOOPS, 0:LOOPS])
                    ins.then_inc(turned, 1)

            @block.vector
            def _(dve):
                for n, (a, b, h, q) in enumerate(jobs):
                    dve.wait_ge(turned, n + 1)
                    out = b[:, :, h].rearrange("p (c b) -> p b c", b=PAIR)[:, 4 * q:4 * q + 4, :]
                    got = bank[0:P, n % 8, 0:4 * LOOPS].rearrange("p (k c) -> p k c", k=4)
                    if b is first_max:
                        flag = g.first[:, 0:STEPS].rearrange("p (c b) -> p b c", b=PAIR)[:, 4 * q:4 * q + 4, :]
                        dve.tensor_tensor(out, got, flag, ALU.mult).then_inc(copied, 1)
                    else:
                        dve.tensor_copy(out, got).then_inc(copied, 1)


def attention_sums(nc, g, spill, weight, first_max):
    width = ACCW
    with Scope(nc) as sc:
        rows = sc.sb("rows", [P, 2, HALF, D])
        values = sc.sb("values", [P, 2, HALF, width])
        held_up = sc.sem("held_up")
        onehot = sc.sb("onehot", [P, 2, HALF, P])
        sums = sc.ps("sums", [P, 2, HALF, 256])
        acc_clear = sc.sem("acc_clear")
        names = ("rows_in", "made", "weighted", "tailed", "maxed", "marked", "summed", "added")
        rows_in, made, weighted, tailed, maxed, marked, summed, added = (sc.sems(x) for x in names)
        block = sc.block()

        @block.sync
        def _(sp):
            with sp.Fori(0, LOOPS) as i:
                for p in range(2):
                    sp.wait_ge(weighted[p], before(i))
                    sp.dma_start(rows[:, p, :, :].rearrange("p j f -> p (j f)"),
                                 spill[bass.ds(2 * i + p, 1), :, :].rearrange("a p f -> (a p) f")).then_inc(rows_in[p], 16)

        @block.scalar
        def _(act):
            prime(act, tailed, maxed, marked)
            with act.Fori(0, LOOPS) as i:
                for p in range(2):
                    s = bass.ds(PAIR * i + HALF * p, HALF)
                    act.wait_ge(summed[p], before(i))
                    act.copy(values[:, p, :, D:D + HEADS], weight[:, s, :]).then_inc(tailed[p], 1)
                    act.copy(values[:, p, :, D + HEADS:width - 1], first_max[:, s, :]).then_inc(maxed[p], 1)
                    act.copy(values[:, p, :, width - 1:width], g.first[:, s].unsqueeze(2)).then_inc(marked[p], 1)

        @block.gpsimd
        def _(pool):
            prime(pool, weighted)
            with pool.Fori(0, LOOPS) as i:
                for p in range(2):
                    s = bass.ds(PAIR * i + HALF * p, HALF)
                    pool.wait_ge(rows_in[p], landed(i))
                    hold(pool, summed[p], before(i), held_up)
                    pool.tensor_tensor(values[:, p, :, 0:D].rearrange("p j (h c) -> p j h c", h=HEADS),
                                       rows[:, p, :, :].rearrange("p j (h c) -> p j h c", h=HEADS),
                                       weight[:, s, :].unsqueeze(3).broadcast_to([P, HALF, HEADS, HID]), ALU.mult).then_inc(weighted[p], 1)

        @block.vector
        def _(dve):
            prime(dve, made, added)
            dve.memset(g.acc[:, :, :], 0.0).then_inc(acc_clear, 1)
            dve.wait_ge(acc_clear, 1)
            for p in range(2):
                one_hot(dve, g, onehot[:, p, :, :], 0, p).then_inc(made[p], 1)
            with dve.Fori(0, LOOPS) as i:
                for p in range(2):
                    add_sums(dve, g, i, p, sums, width, summed, added)
                    one_hot(dve, g, onehot[:, p, :, :], i + 1, p).then_inc(made[p], 1)

        @block.tensor
        def _(pe):
            prime(pe, summed)
            with pe.Fori(0, LOOPS) as i:
                for p in range(2):
                    sum_steps(pe, i, p, onehot, values, sums, width, made,
                              [(weighted, done(i)), (tailed, done(i)), (maxed, done(i)), (marked, done(i))], summed, added)


def message_sums(nc, g, table, own, w_edge):
    width = D + 1
    with Scope(nc) as sc:
        rows = sc.sb("rows", [P, 2, HALF, D])
        now = sc.sb("now", [P, 2, HALF], I32)
        held_up = sc.sem("held_up")
        onehot = sc.sb("onehot", [P, 2, HALF, P])
        onehot_t = sc.sb("onehot_t", [P, 2, HALF * P])
        z = sc.sb("z", [P, 2, HALF, D])
        edge = sc.sb("edge", [P, 2, HALF, D])
        hidden = sc.sb("hidden", [P, 2, HALF, D])
        values = sc.sb("values", [P, 2, HALF, width])
        turn = sc.ps("turn", [P, 2, 512])
        zp = sc.ps("zp", [P, 2, HALF, D])
        sums = sc.ps("sums", [P, 2, HALF, 256])
        acc_clear = sc.sem("acc_clear")
        names = ("staged", "rows_in", "made", "turned", "copied", "spread", "edged", "added", "whole", "active", "weighted", "tailed", "summed", "accd")
        staged, rows_in, made, turned, copied, spread, edged, added, whole, active, weighted, tailed, summed, accd = (sc.sems(x) for x in names)
        block = sc.block()

        @block.gpsimd
        def _(pool):
            prime(pool, staged)
            with pool.Fori(0, LOOPS) as i:
                for p in range(2):
                    gather_rows(pool, i, p, table, rows, now, g.idx, held_up, [added], staged, rows_in)

        @block.scalar
        def _(act):
            prime(act, copied, active)
            with act.Fori(0, LOOPS) as i:
                for p in range(2):
                    copy_turned(act, i, p, turn, onehot_t, turned, spread, copied)
                    act.wait_ge(whole[p], done(i))
                    act.wait_ge(weighted[p], before(i))
                    act.activation(hidden[:, p, :, :], z[:, p, :, :], ACT.Silu).then_inc(active[p], 1)

        @block.tensor
        def _(pe):
            prime(pe, turned, spread, summed)
            with pe.Fori(0, LOOPS) as i:
                for p in range(2):
                    turn_one_hot(pe, i, p, g.ident, onehot, turn, made, turned, copied)
                    pe.wait_ge(copied[p], done(i))
                    pe.wait_ge(added[p], before(i))
                    for j in range(HALF):
                        w = window_of(pe, g, i, p, j)
                        ins = pe.matmul(zp[:, p, j, :], onehot_t[:, p, j * P:(j + 1) * P],
                                        own[:, bass.ds(w, 1), :].rearrange("p w f -> p (w f)"), start=True, stop=True)
                    ins.then_inc(spread[p], 1)
                for p in range(2):
                    sum_steps(pe, i, p, onehot, values, sums, width, made, [(weighted, done(i)), (tailed, done(i))], summed, accd)

        @block.vector
        def _(dve):
            prime(dve, made, edged, added, whole, weighted, tailed, accd)
            dve.memset(g.acc[:, :, :], 0.0).then_inc(acc_clear, 1)
            dve.wait_ge(acc_clear, 1)
            for p in range(2):
                one_hot(dve, g, onehot[:, p, :, :], 0, p).then_inc(made[p], 1)
            with dve.Fori(0, LOOPS) as i:
                for p in range(2):
                    s = bass.ds(PAIR * i + HALF * p, HALF)
                    zz = z[:, p, :, :]
                    dve.wait_ge(added[p], before(i))
                    dve.tensor_tensor(edge[:, p, :, :], rows_of(w_edge, HALF), each(g.ew[:, s], D), ALU.mult).then_inc(edged[p], 1)
                    dve.wait_ge(edged[p], done(i))
                    dve.wait_ge(rows_in[p], landed(i, HALF))
                    dve.tensor_tensor(edge[:, p, :, :], edge[:, p, :, :], rows[:, p, :, :], ALU.add).then_inc(added[p], 1)
                    dve.wait_ge(added[p], done(i))
                    dve.wait_ge(spread[p], done(i))
                    dve.wait_ge(active[p], before(i))
                    dve.tensor_tensor(zz, zp[:, p, :, :], edge[:, p, :, :], ALU.add).then_inc(whole[p], 1)
                    dve.wait_ge(whole[p], done(i))
                for p in range(2):
                    s = bass.ds(PAIR * i + HALF * p, HALF)
                    dve.wait_ge(active[p], done(i))
                    dve.wait_ge(summed[p], before(i))
                    dve.tensor_tensor(values[:, p, :, 0:D], hidden[:, p, :, :], each(g.ew[:, s], D), ALU.mult).then_inc(weighted[p], 1)
                    dve.tensor_copy(values[:, p, :, D:width], g.ew[:, s].unsqueeze(2)).then_inc(tailed[p], 1)
                for p in range(2):
                    add_sums(dve, g, i, p, sums, width, summed, accd)
                    one_hot(dve, g, onehot[:, p, :, :], i + 1, p).then_inc(made[p], 1)


def scatter_to_sources(nc, g, table, y, out):
    wide = N + 1
    chunks = [(k, min(512, N - 512 * k)) for k in range((N + 511) // 512)]
    with Scope(nc) as sc:
        rows = sc.sb("rows", [P, 2, HALF, D])
        now = sc.sb("now", [P, 2, HALF], I32)
        held_up = sc.sem("held_up")
        parts = [sc.sb(f"part{k}", [P, 2, HALF, D], BF16) for k in range(3)]
        nodes = sc.sb("nodes", [P, wide], F16)
        hot = sc.sb("hot", [P, 2, wide], BF16)
        zero = sc.sb("zero", [P, 512], BF16)
        bank = sc.ps("bank", [128, len(chunks), 512])
        cleared, finished, noded = sc.sem("cleared"), sc.sem("finished"), sc.sem("noded")
        tabled = sc.sem("tabled")
        staged, rows_in, hot_made, hot_used = (sc.sems(x) for x in ("staged", "rows_in", "hot_made", "hot_used"))
        cut = [sc.sems(f"cut{k}") for k in range(3)]
        left = [sc.sems(f"left{k}") for k in range(2)]
        block = sc.block()

        @block.sync
        def _(sp):
            with sp.If(many_pairs(sp, g)):
                sp.dma_start(by_window(table), y[:, :, :]).then_inc(tabled, 16)
                sp.wait_ge(tabled, 16)

        @block.gpsimd
        def _(pool):
            with pool.If(many_pairs(pool, g)):
                prime(pool, staged)
                pool.iota(nodes[:, :], pattern=[[1, wide]], base=-(N // 2), channel_multiplier=0,
                          allow_small_or_imprecise_dtypes=True).then_inc(noded, 1)
                pool.wait_ge(tabled, 16)
                with pool.Fori(0, LOOPS) as i:
                    for p in range(2):
                        gather_rows(pool, i, p, table, rows, now, g.near, held_up, [cut[2]], staged, rows_in)

        @block.vector
        def _(dve):
            with dve.If(many_pairs(dve, g)):
                prime(dve, hot_made, *cut, *left)
                dve.memset(zero[:, :], 0.0).then_inc(cleared, 1)
                dve.wait_ge(noded, 1)
                with dve.Fori(0, LOOPS) as i:
                    for p in range(2):
                        row = rows[:, p, :, :]
                        dve.wait_ge(rows_in[p], landed(i, HALF))
                        for b in range(2):
                            dve.wait_ge(hot_used[b], HALF * i + 2 * p + 1)
                        for k in range(3):
                            dve.tensor_copy(parts[k][:, p, :, :], row).then_inc(cut[k][p], 1)
                            if k < 2:
                                dve.wait_ge(cut[k][p], done(i))
                                dve.tensor_tensor(row, row, parts[k][:, p, :, :], ALU.subtract).then_inc(left[k][p], 1)
                                dve.wait_ge(left[k][p], done(i))
                        for j in range(HALF):
                            b, use = j % 2, HALF * i + 2 * p + j // 2
                            dve.wait_ge(hot_used[b], use + 3)
                            dve.tensor_scalar(hot[:, b, :], nodes[:, :], g.src_key[:, bass.ds(PAIR * i + HALF * p + j, 1)], None,
                                              ALU.is_equal).then_inc(hot_made[b], 1)

        @block.tensor
        def _(pe):
            with pe.If(many_pairs(pe, g)):
                for sem in hot_used:
                    pe.sem_inc(sem, 3)
                pe.wait_ge(cleared, 1)
                for k, n in chunks:
                    pe.matmul(bank[:, k, 0:n], zero[:, 0:D], zero[:, 0:n], start=True, stop=False, skip_group_check=True)
                with pe.Fori(0, LOOPS) as i:
                    for p in range(2):
                        pe.wait_ge(cut[2][p], done(i))
                        for j in range(HALF):
                            b, use = j % 2, HALF * i + 2 * p + j // 2
                            pe.wait_ge(hot_made[b], use + 2)
                            for part in parts:
                                for k, n in chunks:
                                    ins = pe.matmul(bank[:, k, 0:n], part[:, p, j, :], hot[:, b, 512 * k:512 * k + n],
                                                    start=False, stop=False, skip_group_check=True)
                            ins.then_inc(hot_used[b], 1)
                for k, n in chunks:
                    ins = pe.matmul(bank[:, k, 0:n], zero[:, 0:D], zero[:, 0:n], start=False, stop=True, skip_group_check=True)
                ins.then_inc(finished, 1)

        @block.scalar
        def _(act):
            with act.If(many_pairs(act, g)):
                act.wait_ge(finished, 1)
                for k, n in chunks:
                    act.copy(out[:, 512 * k:512 * k + n], bank[:, k, 0:n])



def count_pairs(nc, g, pairs):
    for half in range(2):
        with Scope(nc) as sc:
            nodes = sc.sb("nodes", [P, SIDE], F16)
            lanes = sc.sb("lanes", [P, P], BF16)
            hot = sc.sb("hot", [P, 2, SIDE], BF16)
            hot_dst = sc.sb("hot_dst", [P, 2, TEAM, P], BF16)
            part = sc.sb("part", [P, 2, 4, CHUNK], BF16)
            counts = sc.sb("counts", [P, WIN, SIDE], BF16)
            bank = sc.ps("bank", [128, 8, 512])
            noded, cleared, laned, added, stored = (sc.sem(x) for x in ("noded", "cleared", "laned", "added", "stored"))
            made, hot_made, hot_used, copied = (sc.sems(x) for x in ("made", "hot_made", "hot_used", "copied"))
            block = sc.block()

            @block.gpsimd
            def _(pool):
                pool.iota(nodes[:, :], pattern=[[1, SIDE]], base=half * SIDE - N // 2, channel_multiplier=0,
                          allow_small_or_imprecise_dtypes=True).then_inc(noded, 1)
                pool.memset(counts[:, 0:WIN // 2, :], 0.0).then_inc(cleared, 1)
                pool.memset(part[:, 1, :, :], 0.0).then_inc(cleared, 1)

            @block.vector
            def _(dve):
                prime(dve, made, hot_made)
                dve.sem_inc(added, 1)
                dve.tensor_copy(lanes[:, :], g.iota[0:P, :]).then_inc(laned, 1)
                dve.memset(counts[:, WIN // 2:WIN, :], 0.0).then_inc(cleared, 1)
                dve.wait_ge(laned, 1)
                dve.wait_ge(noded, 1)
                dve.wait_ge(cleared, 3)

                def add(k, p):
                    w = dve.value_load(g.pair_win[0:1, bass.ds(k, 1)], min_val=0, max_val=WIN - 1)
                    dve.wait_ge(added, k + 1)
                    row = counts[:, bass.ds(w, 1), :].rearrange("p w (c n) -> p (w c) n", n=CHUNK)
                    dve.tensor_tensor(row, row, part[:, p, :, :], ALU.add).then_inc(added, 1)

                with dve.Fori(0, TEAMS // 2) as i:
                    for p in range(2):
                        k = 2 * i + p
                        dve.wait_ge(hot_used[1], 2 * k + 1)
                        dve.tensor_tensor(hot_dst[:, p, :, :], rows_of(lanes[:, :], TEAM),
                                          each(g.pair_slot[:, bass.ds(TEAM * k, TEAM)], P), ALU.is_equal).then_inc(made[p], 1)
                        for j in range(TEAM):
                            b = j % 2
                            dve.wait_ge(hot_used[b], 2 * k + j // 2 + 3)
                            dve.tensor_scalar(hot[:, b, :], nodes[:, :], g.pair_src[:, bass.ds(TEAM * k + j, 1)], None,
                                              ALU.is_equal).then_inc(hot_made[b], 1)
                        dve.wait_ge(copied[1 - p], before(i + p))
                        add(k, 1 - p)
                dve.wait_ge(copied[1], before(TEAMS // 2))
                add(TEAMS, 1)

            @block.tensor
            def _(pe):
                for sem in hot_used:
                    pe.sem_inc(sem, 3)
                with pe.Fori(0, TEAMS // 2) as i:
                    for p in range(2):
                        k = 2 * i + p
                        pe.wait_ge(made[p], done(i))
                        pe.wait_ge(copied[p], before(i))
                        for j in range(TEAM):
                            b = j % 2
                            pe.wait_ge(hot_made[b], 2 * k + j // 2 + 2)
                            for c in range(4):
                                ins = pe.matmul(bank[0:P, 4 * p + c, 0:CHUNK], hot_dst[:, p, j, :], hot[:, b, c * CHUNK:(c + 1) * CHUNK],
                                                start=j == 0, stop=j == TEAM - 1)
                            ins.then_inc(hot_used[b], 1)

            @block.scalar
            def _(act):
                prime(act, copied)
                with act.Fori(0, TEAMS // 2) as i:
                    for p in range(2):
                        k = 2 * i + p
                        act.wait_ge(hot_used[1], 2 * k + 5)
                        act.wait_ge(added, k + 1)
                        act.copy(part[:, p, :, :], bank[0:P, 4 * p:4 * p + 4, 0:CHUNK]).then_inc(copied[p], 1)

            @block.sync
            def _(sp):
                sp.wait_ge(added, TEAMS + 2)
                sp.dma_start(pairs[:, :, half * SIDE:(half + 1) * SIDE].rearrange("w p n -> p w n"), counts[:, :, :]).then_inc(stored, 16)
                sp.wait_ge(stored, 16)


def cut_rows(dve, link, rest, parts):
    for k in range(3):
        link(dve.tensor_copy(parts[:, k, :, :], rest))
        if k < 2:
            link(dve.tensor_tensor(rest, rest, parts[:, k, :, :], ALU.subtract))


def sums_to_sources(nc, g, table, pairs, y, out):
    chunks = [(k, min(512, N - 512 * k)) for k in range((N + 511) // 512)]
    with Scope(nc) as sc:
        rest = sc.sb("rest", [P, WIN, D])
        parts = sc.sb("parts", [P, 3, WIN, D], BF16)
        counts = sc.sb("counts", [P, FIVE, 2 * SIDE], BF16)
        zero = sc.sb("zero", [P, 512], BF16)
        bank = sc.ps("bank", [128, len(chunks), 512])
        step, cleared, cut, finished = (sc.sem(x) for x in ("step", "cleared", "cut", "finished"))
        counts_in = [sc.sem(f"counts_in{b}") for b in range(FIVE)]
        counts_used = [sc.sem(f"counts_used{b}") for b in range(FIVE)]
        block = sc.block()

        @block.sync
        def _(sp):
            with sp.Fori(0, WIN // FIVE) as i:
                for b in range(FIVE):
                    sp.wait_ge(counts_used[b], before(i))
                    sp.dma_start(counts[:, b, :], pairs[bass.ds(FIVE * i + b, 1), :, :].rearrange("w p n -> (w p) n")).then_inc(counts_in[b], 16)

        @block.vector
        def _(dve):
            link = Link(dve, step)
            dve.memset(zero[:, :], 0.0).then_inc(cleared, 1)
            link(dve.tensor_copy(rest[:, :, :], y[:, :, :]))
            cut_rows(dve, link, rest[:, :, :], parts)
            dve.sem_inc(cut, 1)

        @block.tensor
        def _(pe):
            prime(pe, counts_used)
            pe.wait_ge(cleared, 1)
            for k, n in chunks:
                pe.matmul(bank[:, k, 0:n], zero[:, 0:D], zero[:, 0:n], start=True, stop=False, skip_group_check=True)
            pe.wait_ge(cut, 1)
            with pe.Fori(0, WIN // FIVE) as i:
                for b in range(FIVE):
                    pe.wait_ge(counts_in[b], landed(i))
                    for part in range(3):
                        rows = parts[:, part, bass.ds(FIVE * i + b, 1), :].rearrange("p w f -> p (w f)")
                        for k, n in chunks:
                            ins = pe.matmul(bank[:, k, 0:n], rows, counts[:, b, 512 * k:512 * k + n], start=False, stop=False, skip_group_check=True)
                    ins.then_inc(counts_used[b], 1)
            for k, n in chunks:
                ins = pe.matmul(bank[:, k, 0:n], zero[:, 0:D], zero[:, 0:n], start=False, stop=True, skip_group_check=True)
            ins.then_inc(finished, 1)

        @block.scalar
        def _(act):
            act.wait_ge(finished, 1)
            for k, n in chunks:
                act.copy(out[:, 512 * k:512 * k + n], bank[:, k, 0:n])
    scatter_to_sources(nc, g, table, y, out)


def sums_to_hyperedges(nc, g, table, pairs, y):
    low = HYPER // P
    with Scope(nc) as sc:
        rest = sc.sb("rest", [P, WIN, D])
        parts = sc.sb("parts", [P, 3, WIN, D], BF16)
        counts = sc.sb("counts", [P, low, 2 * SIDE], BF16)
        counts_t = sc.sb("counts_t", [P, FIVE, HYPER], BF16)
        ident = sc.sb("ident", [P, P], BF16)
        zero = sc.sb("zero", [P, 512], BF16)
        turn = sc.ps("turn", [P, FIVE, 8, D], BF16)
        sums = sc.ps("sums", [P, 2, 512])
        step, cleared, cut, finished, counts_in = (sc.sem(x) for x in ("step", "cleared", "cut", "finished", "counts_in"))
        turned, copied, used = ([sc.sem(f"{x}{b}") for b in range(FIVE)] for x in ("turned", "copied", "used"))
        block = sc.block()
        at = lambda w: sums[:, w // 4, (w % 4) * D:(w % 4 + 1) * D]

        @block.sync
        def _(sp):
            sp.dma_start(counts[:, :, :], pairs[0:low, :, :].rearrange("w p n -> p w n")).then_inc(counts_in, 16)

        @block.vector
        def _(dve):
            link = Link(dve, step)
            link(dve.tensor_copy(ident[:, :], g.ident[0:P, 0:P]))
            dve.memset(zero[:, :], 0.0).then_inc(cleared, 1)
            dve.wait_ge(cleared, 1)
            dve.sem_inc(cleared, 1)
            link(dve.tensor_copy(rest[:, :, :], y[:, :, :]))
            cut_rows(dve, link, rest[:, :, :], parts)
            dve.sem_inc(cut, 1)
            dve.wait_ge(counts_in, 16)
            dve.tensor_reduce(g.acc[:, 0:low, D], counts[:, :, :], AX_X, ALU.add)
            dve.wait_ge(finished, 1)
            dve.tensor_copy(g.acc[:, 0:4, 0:D], sums[:, 0, :].rearrange("p (w f) -> p w f", f=D))
            dve.tensor_copy(g.acc[:, 4, 0:D], at(4))

        @block.tensor
        def _(pe):
            prime(pe, used)
            pe.wait_ge(cleared, 2)
            pe.matmul(sums[:, 0, :], zero[:, 0:P], zero[:, :], start=True, stop=False, skip_group_check=True)
            pe.matmul(at(4), zero[:, 0:P], zero[:, 0:D], start=True, stop=False, skip_group_check=True)
            pe.wait_ge(counts_in, 16)
            pe.wait_ge(cut, 1)
            with pe.Fori(0, WIN // FIVE) as i:
                for b in range(FIVE):
                    pe.wait_ge(copied[b], before(i))
                    for w in range(low):
                        ins = pe.transpose(turn[:, b, w, 0:P], counts[:, w, bass.ds(P * (FIVE * i + b), P)], ident[:, :])
                    ins.then_inc(turned[b], 1)
                for b in range(FIVE):
                    pe.wait_ge(copied[b], done(i))
                    for w in range(low):
                        for part in range(3):
                            ins = pe.matmul(at(w), counts_t[:, b, w * P:(w + 1) * P], parts[:, part, bass.ds(FIVE * i + b, 1), :].rearrange("p w f -> p (w f)"),
                                            start=False, stop=False, skip_group_check=True)
                    ins.then_inc(used[b], 1)
            pe.matmul(sums[:, 0, :], zero[:, 0:P], zero[:, :], start=False, stop=True, skip_group_check=True)
            pe.matmul(at(4), zero[:, 0:P], zero[:, 0:D], start=False, stop=True, skip_group_check=True).then_inc(finished, 1)

        @block.scalar
        def _(act):
            prime(act, copied)
            with act.Fori(0, WIN // FIVE) as i:
                for b in range(FIVE):
                    act.wait_ge(turned[b], i + 1)
                    act.wait_ge(used[b], before(i))
                    act.copy(counts_t[:, b, :].rearrange("p (w n) -> p w n", n=P), turn[:, b, 0:low, 0:P]).then_inc(copied[b], 1)
    neighbour_sums(nc, g, table, y)



class Graph:
    pass


def prepare(nc, g, sc, team, src, dst, edge_weight):
    lanes = PAIR * P
    g.ident = sc.sb("ident", [128, 128])
    g.iota = sc.sb("iota", [128, P])
    g.eps = sc.sb("eps", [128, 1])
    g.idx = sc.sb("idx", [P, PAD], I32)
    g.many = sc.sb("many", [1, 1], I32)
    g.slot = sc.sb("slot", [P, PAD])
    g.first = sc.sb("first", [P, PAD])
    g.ew = sc.sb("ew", [P, PAD])
    g.key = sc.sb("key", [P, PAD])
    g.src_key = sc.sb("src_key", [P, PAD])
    g.near = sc.sb("near", [P, PAD], I32)
    g.win_i = sc.sb("win_i", [1, PAD], I32)
    g.brk = sc.sb("brk", [LOOPS, lanes + 1])
    g.head_run = sc.sb("head_run", [LOOPS, lanes])
    g.tail_run = sc.sb("tail_run", [LOOPS, lanes])
    g.whole_up = sc.sb("whole_up", [HEADS, LOOPS])
    g.whole_down = sc.sb("whole_down", [HEADS, LOOPS])
    g.joint = sc.sb("joint", [HEADS, LOOPS])
    g.acc = sc.sb("acc", [P, WIN, ACCW])
    g.pair_slot = team.sb("pair_slot", [P, TEAMS * TEAM])
    g.pair_src = team.sb("pair_src", [P, TEAMS * TEAM])
    g.pair_win = team.sb("pair_win", [1, TEAMS + 1], I32)

    with Scope(nc) as s1:
        rlen = E // RROWS
        src_i = s1.sb("src_i", [RROWS, rlen], I32)
        dst_i = s1.sb("dst_i", [RROWS, rlen], I32)
        pre_i = s1.sb("pre_i", [RROWS, rlen], I32)
        row = [s1.sb(f"row{k}", [RROWS, rlen]) for k in range(4)]
        pre = s1.sb("pre", [RROWS, rlen])
        far_i = s1.sb("far_i", [RROWS, rlen], I32)
        ones = s1.sb("ones", [RROWS, rlen])
        junk = s1.sb("junk", [RROWS, rlen])
        below = s1.sb("below", [RROWS, WIN])
        turn_at = s1.sb("turn_at", [P, WIN - 1])
        steps = s1.sb("steps", [P, STEPS])
        order = s1.sb("order", [P, WIN - 1])
        eight = s1.sb("eight", [P, 1])
        win = s1.sb("win", [P, STEPS])
        win2 = s1.sb("win2", [P, STEPS])
        tile = s1.sb("tile", [P, STEPS])
        pick = s1.sb("pick", [RROWS, TPR, STEPS])
        got = s1.sb("got", [P, STEPS])
        from_ = s1.sb("from", [P, STEPS])
        valid = s1.sb("valid", [P, STEPS])
        half = STEPS // 2
        teams = s1.sb("teams", [P, TEAMS])
        place = s1.sb("place", [P, TEAMS * TEAM])
        team_win = [s1.sb(f"team_win{k}", [P, TEAMS]) for k in range(2)]
        offset = s1.sb("offset", [P, TEAMS])
        move = s1.sb("move", [P, TEAMS])
        low = s1.sb("low", [P, WIN])
        span_ = s1.sb("span", [P, WIN])
        upto = s1.sb("upto", [P, WIN])
        none = s1.sb("none", [P, WIN])
        start = s1.sb("start", [P, WIN])
        pick_team = s1.sb("pick_team", [RROWS, TPR, TEAMS * TEAM])

        with Scope(nc) as s2:
            loaded, pre_set, zeroed, drawn = (s2.sem(x) for x in ("loaded", "pre_set", "zeroed", "drawn"))
            step, counted, totals = s2.sem("step"), s2.sem("counted"), s2.sem("totals")
            total = s2.ps("total", [P, 512])
            block = s2.block()

            @block.sync
            def _(sp):
                sp.dma_start(src_i[:, :], src.rearrange("(r l) -> r l", l=rlen)).then_inc(loaded, 16)
                sp.dma_start(dst_i[:, :], dst.rearrange("(r l) -> r l", l=rlen)).then_inc(loaded, 16)
                sp.dma_start(row[2][:, :], edge_weight.rearrange("(r l) -> r l", l=rlen)).then_inc(loaded, 16)
                sp.dma_start(pre_i[1:RROWS, :], dst[rlen - 1:E - 1].rearrange("(r l) -> r l", l=rlen)).then_inc(loaded, 16)
                sp.dma_start(pre_i[0:1, 1:rlen], dst[0:rlen - 1].rearrange("(r l) -> r l", r=1)).then_inc(loaded, 16)
                sp.dma_start(far_i[1:RROWS, :], dst[rlen - FEW:E - FEW].rearrange("(r l) -> r l", l=rlen)).then_inc(loaded, 16)
                sp.dma_start(far_i[0:1, FEW:rlen], dst[0:rlen - FEW].rearrange("(r l) -> r l", r=1)).then_inc(loaded, 16)

            @block.gpsimd
            def _(pool):
                pool.memset(pre_i[0:1, 0:1], -1).then_inc(pre_set, 1)
                pool.memset(far_i[0:1, 0:FEW], -1).then_inc(pre_set, 1)
                pool.memset(g.ident[:, :], 0.0).then_inc(zeroed, 1)
                pool.wait_ge(zeroed, 1)
                pool.affine_select(out=g.ident[:, :], in_=g.ident[:, :], compare_op=ALU.not_equal, fill=1.0, base=0,
                                   pattern=[[-1, 128]], channel_multiplier=1).then_inc(drawn, 1)
                for out, pattern, base, by in ((g.iota, [[1, P]], 0, 0), (steps, [[1, STEPS]], 0, 0),
                                               (order, [[1, WIN - 1]], 1, 0), (eight, [[0, 1]], 0, TPR),
                                               (teams, [[1, TEAMS]], 0, 0), (place, [[1, TEAMS * TEAM]], 0, 0)):
                    pool.iota(out[:, :], pattern=pattern, base=base, channel_multiplier=by,
                              allow_small_or_imprecise_dtypes=True).then_inc(drawn, 1)

            @block.vector
            def _(dve):
                link = Link(dve, step)
                link(dve.memset(g.eps[:, :], EPS))
                link(dve.memset(ones[:, :], 1.0))
                for t, v in ((g.idx, 0), (g.slot, -1.0), (g.first, 0.0), (g.ew, 0.0), (g.key, -1.0), (g.src_key, -2000.0), (g.near, 0), (g.win_i, 0)):
                    link(dve.memset(t[:, STEPS:PAD], v))
                dve.wait_ge(loaded, 16 * 7)
                dve.wait_ge(pre_set, 2)
                link(dve.tensor_copy(row[0][:, :], src_i[:, :]))
                link(dve.tensor_copy(row[1][:, :], dst_i[:, :]))
                link(dve.tensor_copy(pre[:, :], pre_i[:, :]))
                link(dve.tensor_tensor(row[3][:, :], row[1][:, :], pre[:, :], ALU.not_equal))
                for w in range(1, WIN):
                    link(dve.scalar_tensor_tensor(out=junk[:, :], in0=row[1][:, :], scalar=float(P * w), in1=ones[:, :],
                                                  op0=ALU.is_lt, op1=ALU.mult, accum_out=below[:, w - 1:w]))
                link(dve.tensor_copy(pre[:, :], far_i[:, :]))
                link(dve.tensor_tensor(pre[:, :], pre[:, :], row[1][:, :], ALU.is_equal))
                link(dve.scalar_tensor_tensor(out=junk[:, :], in0=pre[:, :], scalar=0.5, in1=ones[:, :],
                                              op0=ALU.is_ge, op1=ALU.mult, accum_out=below[:, WIN - 1:WIN]))
                dve.sem_inc(counted, 1)
                dve.wait_ge(totals, 1)
                link(dve.tensor_scalar(start[:, 0:1], total[:, WIN - 1:WIN], 1.0, None, ALU.min))
                link(dve.tensor_copy(g.many[:, :], start[0:1, 0:1]))
                link(dve.memset(low[:, :], 0.0))
                link(dve.tensor_scalar(low[:, 1:WIN], total[:, 0:WIN - 1], -float(P // 2), 1.0 / P, ALU.add, ALU.mult))
                link(dve.tensor_scalar(low[:, 1:WIN], low[:, 1:WIN], ROUND, None, ALU.add))
                link(dve.tensor_scalar(low[:, 1:WIN], low[:, 1:WIN], -ROUND, None, ALU.add))
                link(dve.memset(span_[:, :], float(TILES)))
                link(dve.tensor_scalar(span_[:, 0:WIN - 1], total[:, 0:WIN - 1], float(P // 2), 1.0 / P, ALU.add, ALU.mult))
                link(dve.tensor_scalar(span_[:, 0:WIN - 1], span_[:, 0:WIN - 1], ROUND, None, ALU.add))
                link(dve.tensor_scalar(span_[:, 0:WIN - 1], span_[:, 0:WIN - 1], -ROUND, None, ALU.add))
                link(dve.tensor_tensor(span_[:, :], span_[:, :], low[:, :], ALU.subtract))
                link(dve.tensor_scalar(span_[:, :], span_[:, :], (TEAM - 1) / 2, 1.0 / TEAM, ALU.add, ALU.mult))
                link(dve.tensor_scalar(span_[:, :], span_[:, :], ROUND, None, ALU.add))
                link(dve.tensor_scalar(span_[:, :], span_[:, :], -ROUND, None, ALU.add))
                link(dve.memset(none[:, :], 0.0))
                link(dve.tensor_tensor_scan(upto[:, :], none[:, :], span_[:, :], 0.0, ALU.add, ALU.add))
                link(dve.memset(start[:, :], 0.0))
                link(dve.scalar_tensor_tensor(out=start[:, 1:WIN], in0=upto[:, 0:WIN - 1], scalar=-float(TEAM), in1=low[:, 1:WIN], op0=ALU.mult, op1=ALU.add))
                link(dve.tensor_tensor(none[:, 1:WIN], start[:, 1:WIN], start[:, 0:WIN - 1], ALU.subtract))
                link(dve.memset(team_win[0][:, :], 0.0))
                link(dve.memset(offset[:, :], 0.0))
                dve.wait_ge(drawn, 7)
                for w in range(1, WIN):
                    link(dve.scalar_tensor_tensor(out=team_win[w % 2][:, :], in0=teams[:, :], scalar=upto[:, w - 1:w], in1=team_win[1 - w % 2][:, :],
                                                  op0=ALU.is_ge, op1=ALU.add))
                    link(dve.tensor_scalar(move[:, :], teams[:, :], upto[:, w - 1:w], none[:, w:w + 1], ALU.is_ge, ALU.mult))
                    link(dve.tensor_tensor(offset[:, :], offset[:, :], move[:, :], ALU.add))
                link(dve.memset(g.pair_win[:, :], 0))
                link(dve.tensor_copy(g.pair_win[:, 1:TEAMS + 1], team_win[0][0:1, :]))
                link(dve.tensor_tensor(place[:, :].rearrange("p (t j) -> p t j", j=TEAM), place[:, :].rearrange("p (t j) -> p t j", j=TEAM),
                                       each(offset[:, :], TEAM), ALU.add))
                link(dve.tensor_scalar(place[:, :], place[:, :], eight[:, :], None, ALU.subtract))
                for b8 in range(TPR):
                    link(dve.tensor_scalar(pick_team[:, b8, :], place[0:RROWS, :], float(b8), None, ALU.is_equal))
                link(dve.tensor_scalar(turn_at[:, :], total[:, 0:WIN - 1], -float(P // 2), 1.0 / P, ALU.add, ALU.mult))
                link(dve.tensor_scalar(turn_at[:, :], turn_at[:, :], ROUND, None, ALU.add))
                link(dve.tensor_scalar(turn_at[:, :], turn_at[:, :], -ROUND, float(TILES - 1), ALU.add, ALU.min))
                dve.wait_ge(drawn, 7)
                link(dve.tensor_tensor(turn_at[:, :], turn_at[:, :], order[:, :], ALU.add))
                link(dve.memset(win[:, :], 0.0))
                a, b = win, win2
                for w in range(WIN - 1):
                    link(dve.scalar_tensor_tensor(out=b[:, :], in0=steps[:, :], scalar=turn_at[:, w:w + 1], in1=a[:, :],
                                                  op0=ALU.is_ge, op1=ALU.add))
                    a, b = b, a
                link(dve.tensor_copy(g.win_i[:, 0:STEPS], a[0:1, :]))
                link(dve.tensor_tensor(tile[:, :], steps[:, :], a[:, :], ALU.subtract))
                link(dve.tensor_scalar(tile[:, :], tile[:, :], eight[:, :], None, ALU.subtract))
                for b8 in range(TPR):
                    link(dve.tensor_scalar(pick[:, b8, :], tile[0:RROWS, :], float(b8), None, ALU.is_equal))

            @block.tensor
            def _(pe):
                pe.wait_ge(counted, 1)
                pe.matmul(total[:, 0:WIN], ones[:, 0:P], below[:, :], start=True, stop=True).then_inc(totals, 1)
        assert (WIN - 1) % 2 == 0

        with Scope(nc) as s2:
            bank = s2.ps("bank", [P, 8, 512])
            step, picked = s2.sem("step"), s2.sem("picked")
            block = s2.block()

            @block.tensor
            def _(pe):
                for k in range(4):
                    for h in range(2):
                        for b8 in range(TPR):
                            ins = pe.matmul(bank[:, 2 * k + h, 0:half], row[k][:, b8 * P:(b8 + 1) * P],
                                            pick[:, b8, h * half:(h + 1) * half], start=b8 == 0, stop=b8 == TPR - 1)
                    ins.then_inc(picked, 1)

            @block.vector
            def _(dve):
                link = Link(dve, step)

                def two(t):
                    return t.rearrange("p (h s) -> p h s", h=2)

                dve.wait_ge(picked, 4)
                link(dve.tensor_copy(two(from_[:, :]), bank[:, 0:2, 0:half]))
                link(dve.tensor_copy(g.idx[:, 0:STEPS], from_[:, :]))
                link(dve.tensor_copy(two(got[:, :]), bank[:, 2:4, 0:half]))
                link(dve.tensor_copy(two(g.ew[:, 0:STEPS]), bank[:, 4:6, 0:half]))
                link(dve.tensor_copy(two(g.first[:, 0:STEPS]), bank[:, 6:8, 0:half]))
                link(dve.scalar_tensor_tensor(out=g.slot[:, 0:STEPS], in0=win[:, :], scalar=-float(P), in1=got[:, :], op0=ALU.mult, op1=ALU.add))
                link(dve.tensor_scalar(valid[:, :], g.slot[:, 0:STEPS], 0.0, None, ALU.is_ge))
                link(dve.scalar_tensor_tensor(out=valid[:, :], in0=g.slot[:, 0:STEPS], scalar=float(P), in1=valid[:, :], op0=ALU.is_lt, op1=ALU.mult))
                link(dve.scalar_tensor_tensor(out=g.key[:, 0:STEPS], in0=got[:, :], scalar=1.0, in1=valid[:, :], op0=ALU.add, op1=ALU.mult))
                link(dve.tensor_scalar(g.key[:, 0:STEPS], g.key[:, 0:STEPS], -1.0, None, ALU.add))
                link(dve.tensor_copy(g.near[:, 0:STEPS], got[:, :]))
                link(dve.scalar_tensor_tensor(out=g.src_key[:, 0:STEPS], in0=from_[:, :], scalar=2000.0 - N // 2, in1=valid[:, :], op0=ALU.add, op1=ALU.mult))
                link(dve.tensor_scalar(g.src_key[:, 0:STEPS], g.src_key[:, 0:STEPS], -2000.0, None, ALU.add))

        with Scope(nc) as s2:
            side = TEAMS * TEAM // 2
            bank = s2.ps("bank", [P, 4, 512])
            step, picked = s2.sem("step"), s2.sem("picked")
            block = s2.block()

            @block.tensor
            def _(pe):
                for k in range(2):
                    for h in range(2):
                        for b8 in range(TPR):
                            ins = pe.matmul(bank[:, 2 * k + h, 0:side], row[k][:, b8 * P:(b8 + 1) * P],
                                            pick_team[:, b8, h * side:(h + 1) * side], start=b8 == 0, stop=b8 == TPR - 1)
                ins.then_inc(picked, 1)

            @block.vector
            def _(dve):
                link = Link(dve, step)
                dve.wait_ge(picked, 1)
                link(dve.tensor_scalar(g.pair_src[:, :].rearrange("p (h s) -> p h s", h=2), bank[:, 0:2, 0:side], -float(N // 2), None, ALU.add))
                link(dve.tensor_copy(g.pair_slot[:, :].rearrange("p (h s) -> p h s", h=2), bank[:, 2:4, 0:side]))
                four = g.pair_slot[:, :].rearrange("p (t j) -> p t j", j=TEAM)
                link(dve.scalar_tensor_tensor(out=four, in0=each(team_win[0][:, :], TEAM), scalar=-float(P), in1=four, op0=ALU.mult, op1=ALU.add))

    with Scope(nc) as s1:
        krow = s1.sb("krow", [LOOPS, lanes])
        cols = s1.sb("cols", [LOOPS, 3, HEADS])
        edge = s1.sb("edge", [HEADS, 3, LOOPS])
        bank = s1.ps("bank", [128, 8, 512])
        step, turned, cols_ready, cols_turned = (s1.sem(x) for x in ("step", "turned", "cols_ready", "cols_turned"))
        block = s1.block()

        @block.tensor
        def _(pe):
            kv = g.key[:, 0:STEPS].rearrange("p (c b) -> p c b", b=PAIR)
            for b in range(PAIR):
                ins = pe.transpose(bank[0:LOOPS, b // 4, (b % 4) * P:(b % 4 + 1) * P], kv[:, :, b], g.ident[0:P, 0:P])
            ins.then_inc(turned, 1)
            pe.wait_ge(cols_ready, 1)
            for k in range(3):
                ins = pe.transpose(bank[0:HEADS, 2 + k, 0:LOOPS], cols[:, k, :], g.ident[0:LOOPS, 0:LOOPS])
            ins.then_inc(cols_turned, 1)

        @block.vector
        def _(dve):
            link = Link(dve, step)
            dve.wait_ge(turned, 1)
            link(dve.tensor_copy(krow[:, :].rearrange("p (a l) -> p a l", a=2), bank[0:LOOPS, 0:2, 0:4 * P]))
            link(dve.memset(g.brk[:, :], 0.0))
            link(dve.tensor_tensor(g.brk[:, 1:lanes], krow[:, 1:lanes], krow[:, 0:lanes - 1], ALU.not_equal))
            link(dve.tensor_scalar(g.brk[:, 1:lanes], g.brk[:, 1:lanes], -BIG, None, ALU.mult))
            link(dve.tensor_tensor_scan(g.head_run[:, :], g.brk[:, 0:lanes], g.brk[:, 0:lanes], 0.0, ALU.min, ALU.min))
            back = g.brk[:, 1:lanes + 1][:, ::-1]
            link(dve.tensor_tensor_scan(g.tail_run[:, ::-1], back, back, 0.0, ALU.min, ALU.min))
            for k, c in enumerate((krow[:, 0:1], krow[:, lanes - 1:lanes], g.head_run[:, lanes - 1:lanes])):
                link(dve.tensor_copy(cols[:, k, :], c.to_broadcast([LOOPS, HEADS])))
            dve.sem_inc(cols_ready, 1)
            dve.wait_ge(cols_turned, 1)
            link(dve.tensor_copy(edge[:, :, :], bank[0:HEADS, 2:5, 0:LOOPS]))
            link(dve.memset(g.joint[:, :], -BIG))
            link(dve.tensor_tensor(g.joint[:, 1:LOOPS], edge[:, 0, 1:LOOPS], edge[:, 1, 0:LOOPS - 1], ALU.not_equal))
            link(dve.tensor_scalar(g.joint[:, 1:LOOPS], g.joint[:, 1:LOOPS], -BIG, None, ALU.mult))
            link(dve.tensor_tensor(g.whole_up[:, :], g.joint[:, :], edge[:, 2, :], ALU.add))
            link(dve.memset(g.whole_down[:, :], -BIG))
            link(dve.tensor_tensor(g.whole_down[:, 0:LOOPS - 1], g.joint[:, 1:LOOPS], edge[:, 2, 0:LOOPS - 1], ALU.add))



def by_window(table):
    return table.rearrange("(w p) f -> p w f", p=P)


def column(v):
    return v.rearrange("(f a) -> f a", a=1)


def layer0(nc, g, a, x, table, pairs):
    with Scope(nc) as sc:
        cur = sc.sb("cur", [P, WIN, D])
        ft = sc.sb("ft", [128, N])
        ht = sc.sb("ht", [128, N])
        w1 = sc.sb("w1", [128, 3, D])
        w2 = sc.sb("w2", [128, 3, D])
        cols = sc.sb("cols", [128, 3, 4])
        loads = [(w1[:, :, :], a["L0_gnn_W1"].rearrange("l i o -> i l o")), (w2[:, :, :], a["L0_gnn_W2"].rearrange("l i o -> i l o"))]
        for i in range(3):
            for k, n in enumerate(("b1", "b2", "gamma", "beta")):
                loads.append((cols[:, i, k:k + 1], column(a[f"L0_gnn_{n}"][i, :])))
        load(nc, loads)
        to_features(nc, g.ident, x, D, ht)
        for i in range(3):
            sums_to_sources(nc, g, table, pairs, x if i == 0 else cur, ft)
            vector_steps(nc, lambda dve, link: link(dve.tensor_tensor(ft[:, :], ft[:, :], ht[:, :], ALU.add)))
            linear_features(nc, ft[:, :], w1[:, i, :], ACT.Relu, cols[:, i, 0:1], ht)
            linear_features(nc, ht[:, :], w2[:, i, :], ACT.Identity, cols[:, i, 1:2], ft)
            with Scope(nc) as s1:
                mean, var, std, gain = (s1.sb(k, [128, 1]) for k in ("mean", "var", "std", "gain"))
                step, var_ready, std_ready = s1.sem("step"), s1.sem("var_ready"), s1.sem("std_ready")
                block = s1.block()

                @block.vector
                def _(dve):
                    link = Link(dve, step)
                    link(dve.tensor_reduce(mean[:, :], ft[:, :], AX_X, ALU.add))
                    link(dve.tensor_scalar(mean[:, :], mean[:, :], 1.0 / N, None, ALU.mult))
                    link(dve.tensor_scalar(ft[:, :], ft[:, :], mean[:, :], None, ALU.subtract))
                    link(dve.tensor_tensor(ht[:, :], ft[:, :], ft[:, :], ALU.mult))
                    dve.tensor_reduce(var[:, :], ht[:, :], AX_X, ALU.add).then_inc(var_ready, 1)
                    dve.wait_ge(std_ready, 1)
                    link(dve.reciprocal(gain[:, :], std[:, :]))
                    link(dve.tensor_tensor(gain[:, :], gain[:, :], cols[:, i, 2:3], ALU.mult))
                    link(dve.tensor_scalar(ft[:, :], ft[:, :], gain[:, :], cols[:, i, 3:4], ALU.mult, ALU.add))

                @block.scalar
                def _(act):
                    act.wait_ge(var_ready, 1)
                    act.activation(std[:, :], var[:, :], ACT.Sqrt, bias=g.eps[:, :], scale=1.0 / N).then_inc(std_ready, 1)
            to_nodes(nc, g.ident, ft, cur)
            vector_steps(nc, lambda dve, link: link(dve.tensor_copy(ht[:, :], ft[:, :])))
        normalize(nc, x[:, :, :], g.eps, before=lambda dve, link: link(dve.tensor_tensor(x[:, :, :], x[:, :, :], cur[:, :, :], ALU.add)))


def layer1(nc, g, a, x, table, spill):
    with Scope(nc) as sc:
        h = sc.sb("h", [P, WIN, D])
        ft = sc.sb("ft", [128, N])
        xr = sc.sb("xr", [P, WIN, D])
        xl = sc.sb("xl", [P, WIN, D + HEADS])
        win = sc.sb("win", [128, HID])
        wout = sc.sb("wout", [128, D])
        bin_ = sc.sb("bin", [HID, 1])
        bout = sc.sb("bout", [P, D])
        load(nc, [(win[:, :], a["L1_gnn_W_in"]), (wout[:, :], a["L1_gnn_W_out"]), (bin_[:, :], column(a["L1_gnn_b_in"])),
                  (bout[:, :], a["L1_gnn_b_out"].partition_broadcast(P))])
        to_features(nc, g.ident, x, D, ft)
        with Scope(nc) as s1:
            f0 = s1.sb("f0", [HID, N])
            linear_features(nc, ft[:, :], win[:, :], ACT.Gelu, bin_[:, :], f0)
            vector_steps(nc, lambda dve, link: link(dve.tensor_copy(ft[0:HID, :], f0[:, :])))
        for i in range(3):
            k = HID if i == 0 else D
            with Scope(nc) as s1:
                wl = s1.sb("wl", [k, D])
                wr = s1.sb("wr", [k, D])
                row = s1.sb("row", [P, 6, D])
                logit = s1.sb("logit", [P, STEPS, HEADS])
                capped = s1.sb("capped", [P, STEPS, HEADS])
                ls = s1.sb("ls", [P, WIN, HEADS])
                names = [a[f"L1_gnn_{n}{i}"] for n in ("bl", "br", "att", "bo", "g", "be")]
                names[2] = names[2].rearrange("h c -> (h c)")
                load(nc, [(wl[:, :], a[f"L1_gnn_Wl{i}"]), (wr[:, :], a[f"L1_gnn_Wr{i}"])]
                     + [(row[:, n, :], v.partition_broadcast(P)) for n, v in enumerate(names)])
                bl, br, att, bo, gain, shift = (row[:, n, :] for n in range(6))
                linear_nodes(nc, [(ft[0:k, :], wl[:, :])], bl, xl)
                linear_nodes(nc, [(ft[0:k, :], wr[:, :])], br, xr)
                load(nc, [(by_window(table), xr[:, :, :])])
                with Scope(nc) as s2:
                    z = s2.sb("z", [P, WIN, D])

                    def self_logits(dve, link):
                        link(dve.tensor_tensor(z[:, :, :], xl[:, :, 0:D], xr[:, :, :], ALU.add))
                        link(dve.scalar_tensor_tensor(out=z[:, :, :], in0=z[:, :, :], scalar=0.2, in1=z[:, :, :], op0=ALU.mult, op1=ALU.max))
                        link(dve.tensor_tensor(z[:, :, :], z[:, :, :], rows_of(att, WIN), ALU.mult))
                        link(dve.tensor_reduce(ls[:, :, :], z[:, :, :].rearrange("p w (h c) -> p w h c", h=HEADS), AX_X, ALU.add))
                        link(dve.tensor_copy(xl[:, :, D:D + HEADS], ls[:, :, :]))

                    vector_steps(nc, self_logits)
                attention_logits(nc, g, table, xl, att, spill, logit, capped)
                softmax_weights(nc, g, logit, capped, capped)
                attention_sums(nc, g, spill, logit, capped)
                with Scope(nc) as s2:
                    m = s2.sb("m", [P, WIN, HEADS])
                    some = s2.sb("some", [P, WIN])
                    es = s2.sb("es", [P, WIN, HEADS])
                    step, shifted, exped = s2.sem("step"), s2.sem("shifted"), s2.sem("exped")
                    block = s2.block()
                    heads = lambda t: t.rearrange("p w (h c) -> p w h c", h=HEADS)
                    over = lambda t: t.unsqueeze(3).broadcast_to([P, WIN, HEADS, HID])

                    @block.vector
                    def _(dve):
                        link = Link(dve, step)
                        link(dve.tensor_scalar(some[:, :].unsqueeze(2), g.acc[:, :, ACCW - 1:ACCW], 0.0, -BIG, ALU.is_equal, ALU.mult))
                        link(dve.tensor_tensor(m[:, :, :], g.acc[:, :, D + HEADS:ACCW - 1], each(some[:, :], HEADS), ALU.add))
                        link(dve.tensor_tensor(m[:, :, :], m[:, :, :], ls[:, :, :], ALU.max))
                        dve.tensor_tensor(m[:, :, :], ls[:, :, :], m[:, :, :], ALU.subtract).then_inc(shifted, 1)
                        dve.wait_ge(exped, 1)
                        link(dve.tensor_tensor(heads(xr[:, :, :]), heads(xr[:, :, :]), over(es[:, :, :]), ALU.mult))
                        link(dve.tensor_tensor(xr[:, :, :], xr[:, :, :], g.acc[:, :, 0:D], ALU.add))
                        link(dve.tensor_tensor(m[:, :, :], es[:, :, :], g.acc[:, :, D:D + HEADS], ALU.add))
                        link(dve.tensor_scalar(m[:, :, :], m[:, :, :], 1e-16, None, ALU.add))
                        link(dve.reciprocal(m[:, :, :], m[:, :, :]))
                        link(dve.tensor_tensor(heads(xr[:, :, :]), heads(xr[:, :, :]), over(m[:, :, :]), ALU.mult))
                        link(dve.tensor_tensor(xr[:, :, :], xr[:, :, :], rows_of(bo, WIN), ALU.add))

                    @block.scalar
                    def _(act):
                        act.wait_ge(shifted, 1)
                        act.activation(es[:, :, :], m[:, :, :], ACT.Exp).then_inc(exped, 1)
                def keep(dve, link):
                    if i == 0:
                        link(dve.tensor_copy(h[:, :, :], xr[:, :, :]))
                    else:
                        link(dve.tensor_tensor(h[:, :, :], h[:, :, :], xr[:, :, :], ALU.add))

                normalize(nc, xr[:, :, :], g.eps, gain=gain, shift=shift, func=ACT.Gelu, after=keep)
                to_features(nc, g.ident, h, D, ft)
        linear_nodes(nc, [(ft[:, :], wout[:, :])], bout[:, :], h)
        with Scope(nc) as s1:
            sq = s1.sb("sq", [P, WIN, D])
            length = s1.sb("length", [P, WIN])
            root = s1.sb("root", [P, WIN])
            step, summed, rooted = s1.sem("step"), s1.sem("summed"), s1.sem("rooted")
            block = s1.block()

            @block.vector
            def _(dve):
                link = Link(dve, step)
                link(dve.tensor_tensor(sq[:, :, :], h[:, :, :], h[:, :, :], ALU.mult))
                dve.tensor_reduce(length[:, :], sq[:, :, :], AX_X, ALU.add).then_inc(summed, 1)
                dve.wait_ge(rooted, 1)
                link(dve.tensor_scalar(root[:, :], root[:, :], 1e-12, None, ALU.max))
                link(dve.reciprocal(root[:, :], root[:, :]))
                link(dve.tensor_tensor(h[:, :, :], h[:, :, :], each(root[:, :], D), ALU.mult))

            @block.scalar
            def _(act):
                act.wait_ge(summed, 1)
                act.activation(root[:, :], length[:, :], ACT.Sqrt).then_inc(rooted, 1)
        normalize(nc, x[:, :, :], g.eps, before=lambda dve, link: link(dve.tensor_tensor(x[:, :, :], x[:, :, :], h[:, :, :], ALU.add)))


def layer2(nc, g, a, x, table, pairs):
    low = HYPER // P
    with Scope(nc) as sc:
        dv = sc.sb("dv", [P, WIN])
        y = sc.sb("y", [P, WIN, D])
        he = sc.sb("he", [P, WIN, D])
        hw = sc.sb("hw", [P, low + 1])
        de = sc.sb("de", [P, low])
        ft = sc.sb("ft", [128, N])
        w = sc.sb("w", [128, D])
        wt = sc.sb("wt", [128, D])
        last = sc.sb("last", [P, P])
        bias = sc.sb("bias", [P, D])
        load(nc, [(hw[:, 0:low], a["L2_gnn_hyperedge_weight"].rearrange("(w p) -> p w", p=P)), (w[:, :], a["L2_gnn_W"]),
                  (hw[:, low:low + 1], a["L2_gnn_hyperedge_weight"][HYPER - 1:HYPER].partition_broadcast(P)),
                  (bias[:, :], a["L2_gnn_b"].partition_broadcast(P))])

        def look_up(dve, link):
            link(dve.tensor_copy(he[:, 0:low, :], each(hw[:, 0:low], D)))
            link(dve.tensor_copy(he[:, low:WIN, :], hw[:, low:low + 1].unsqueeze(2).broadcast_to([P, WIN - low, D])))

        vector_steps(nc, look_up)
        sums_to_sources(nc, g, table, pairs, he, ft)
        to_nodes(nc, g.ident, ft, y)
        with Scope(nc) as s1:
            root = s1.sb("root", [P, WIN])
            turn = s1.ps("turn", [128, 512])
            step, clipped, rooted, turned = s1.sem("step"), s1.sem("clipped"), s1.sem("rooted"), s1.sem("turned")
            block = s1.block()

            @block.tensor
            def _(pe):
                pe.transpose(turn[:, 0:D], w[:, :], g.ident[:, :]).then_inc(turned, 1)

            @block.vector
            def _(dve):
                link = Link(dve, step)
                dve.tensor_scalar(dv[:, :].unsqueeze(2), y[:, :, 0:1], 1.0, None, ALU.max).then_inc(clipped, 1)
                dve.wait_ge(rooted, 1)
                link(dve.reciprocal(dv[:, :], root[:, :]))
                link(dve.tensor_tensor(y[:, :, :], x[:, :, :], each(dv[:, :], D), ALU.mult))
                link(dve.tensor_copy(last[:, :], g.ident[0:P, P - 1:P].to_broadcast([P, P])))
                dve.wait_ge(turned, 1)
                link(dve.tensor_copy(wt[:, :], turn[:, 0:D]))

            @block.scalar
            def _(act):
                act.wait_ge(clipped, 1)
                act.activation(root[:, :], dv[:, :], ACT.Sqrt).then_inc(rooted, 1)
        sums_to_hyperedges(nc, g, table, pairs, y)

        def hyperedges(dve, link):
            link(dve.tensor_scalar(de[:, :].unsqueeze(2), g.acc[:, 0:low, D:D + 1], 1.0, None, ALU.max))
            link(dve.reciprocal(de[:, :], de[:, :]))
            link(dve.tensor_tensor(de[:, :], de[:, :], hw[:, 0:low], ALU.mult))
            link(dve.tensor_tensor(he[:, 0:low, :], g.acc[:, 0:low, 0:D], each(de[:, :], D), ALU.mult))

        vector_steps(nc, hyperedges)
        with Scope(nc) as s1:
            row = s1.ps("row", [P, 512])
            taken = s1.sem("taken")
            block = s1.block()

            @block.tensor
            def _(pe):
                pe.matmul(row[:, 0:D], last[:, :], he[:, low - 1, :], start=True, stop=True).then_inc(taken, 1)

            @block.vector
            def _(dve):
                dve.wait_ge(taken, 1)
                dve.tensor_copy(he[:, low:WIN, :], rows_of(row[:, 0:D], WIN - low))

        sums_to_sources(nc, g, table, pairs, he, ft)
        linear_nodes(nc, [(ft[:, :], wt[:, :])], None, y)

        def scale(dve, link):
            link(dve.tensor_tensor(y[:, :, :], y[:, :, :], each(dv[:, :], D), ALU.mult))
            link(dve.tensor_tensor(y[:, :, :], y[:, :, :], rows_of(bias[:, :], WIN), ALU.add))
            link(dve.tensor_tensor(x[:, :, :], x[:, :, :], y[:, :, :], ALU.add))

        normalize(nc, x[:, :, :], g.eps, before=scale)


def layer3(nc, g, a, x, table):
    with Scope(nc) as sc:
        ft = sc.sb("ft", [128, N])
        at = sc.sb("at", [128, N])
        pa = sc.sb("pa", [P, WIN, D])
        pb = sc.sb("pb", [P, WIN, D])
        m1 = sc.sb("m1", [128, 2, D])
        u1 = sc.sb("u1", [128, 2, D])
        m2 = sc.sb("m2", [128, D])
        u2 = sc.sb("u2", [128, D])
        row = sc.sb("row", [P, 7, D])
        n3 = lambda n: a[f"L3_gnn_{n}"]
        rows = [n3("mW1")[2 * D, :], n3("mb1"), n3("mb2"), n3("ub1"), n3("ln_g"), n3("ln_b"), n3("ub2")]
        load(nc, [(m1[:, :, :], n3("mW1")[0:2 * D, :].rearrange("(b i) o -> i b o", b=2)),
                  (u1[:, :, :], n3("uW1").rearrange("(b i) o -> i b o", b=2)), (m2[:, :], n3("mW2")), (u2[:, :], n3("uW2"))]
             + [(row[:, n, :], v.partition_broadcast(P)) for n, v in enumerate(rows)])
        w_edge, mb1, mb2, ub1, ln_g, ln_b, ub2 = (row[:, n, :] for n in range(7))
        to_features(nc, g.ident, x, D, ft)
        linear_nodes(nc, [(ft[:, :], m1[:, 0, :])], None, pa)
        linear_nodes(nc, [(ft[:, :], m1[:, 1, :])], mb1, pb)
        load(nc, [(by_window(table), pa[:, :, :])])
        message_sums(nc, g, table, pb, w_edge)
        to_features(nc, g.ident, g.acc, D, at)
        linear_nodes(nc, [(at[:, :], m2[:, :])], None, pa)

        def bias(dve, link):
            link(dve.tensor_tensor(pb[:, :, :], rows_of(mb2, WIN), g.acc[:, :, D:D + 1].broadcast_to([P, WIN, D]), ALU.mult))
            link(dve.tensor_tensor(pa[:, :, :], pa[:, :, :], pb[:, :, :], ALU.add))

        vector_steps(nc, bias)
        to_features(nc, g.ident, pa, D, at)
        linear_nodes(nc, [(ft[:, :], u1[:, 0, :]), (at[:, :], u1[:, 1, :])], ub1, pa)
        normalize(nc, pa[:, :, :], g.eps, gain=ln_g, shift=ln_b, func=ACT.Silu)
        to_features(nc, g.ident, pa, D, at)
        linear_nodes(nc, [(at[:, :], u2[:, :])], ub2, pa)

        def residual(dve, link):
            link(dve.scalar_tensor_tensor(out=x[:, :, :], in0=x[:, :, :], scalar=2.0, in1=pa[:, :, :], op0=ALU.mult, op1=ALU.add))

        normalize(nc, x[:, :, :], g.eps, before=residual)


def program(nc, a, out, upto=4):
    table = nc.dram_tensor("node_table", (N, D), F32, kind="Internal").ap()
    spill = nc.dram_tensor("gathered", (2 * LOOPS, P, HALF * D), F32, kind="Internal").ap()
    pairs = nc.dram_tensor("pairs", (WIN, P, 2 * SIDE), BF16, kind="Internal").ap()
    g = Graph()
    with Scope(nc) as sc:
        with Scope(nc) as team:
            prepare(nc, g, sc, team, a["src"], a["dst"], a["edge_weight"])
            count_pairs(nc, g, pairs)
        x = sc.sb("x", [P, WIN, D])
        load(nc, [(x[:, :, :], by_window(a["x"]))])
        with Scope(nc) as s1:
            layer0(nc, g, a, x, table, pairs)
        if upto >= 2:
            layer1(nc, g, a, x, table, spill)
        if upto >= 3:
            layer2(nc, g, a, x, table, pairs)
        if upto >= 4:
            layer3(nc, g, a, x, table)
        load(nc, [(by_window(out), x[:, :, :])])


_INS = ['x', 'src', 'dst', 'edge_weight'] + [f'L0_gnn_{n}' for n in ('W1', 'b1', 'W2', 'b2', 'gamma', 'beta')] + [
    'L1_gnn_W_in', 'L1_gnn_b_in'] + [f'L1_gnn_{n}{i}' for i in range(3) for n in ('Wl', 'bl', 'Wr', 'br', 'att', 'bo', 'g', 'be')] + [
    'L1_gnn_W_out', 'L1_gnn_b_out', 'L2_gnn_hyperedge_weight', 'L2_gnn_W', 'L2_gnn_b'] + [
    f'L3_gnn_{n}' for n in ('mW1', 'mb1', 'mW2', 'mb2', 'uW1', 'ub1', 'ln_g', 'ln_b', 'uW2', 'ub2')]


def kernel(**inputs):
    import numpy as _np
    import concourse.bacc as _bacc
    from concourse.bass_utils import run_bass_kernel_spmd as _run

    nc = _bacc.Bacc("TRN2", target_bir_lowering=False, num_devices=1)
    arrays, args = {}, {}
    for name in _INS:
        v = _np.ascontiguousarray(inputs[name])
        arrays[f"in_{name}"] = v
        args[name] = nc.dram_tensor(f"in_{name}", v.shape, mybir.dt.from_np(v.dtype), kind="ExternalInput").ap()
    out = nc.dram_tensor("out", (N, D), F32, kind="ExternalOutput").ap()
    program(nc, args, out)
    r = _run(nc, [arrays], core_ids=[0])
    return r.results[0]["out"]
```

```python
from contextlib import ExitStack
from itertools import count

import concourse.bass as bass
from concourse import mybir

F32 = mybir.dt.float32
BF16 = mybir.dt.bfloat16
F16 = mybir.dt.float16
I32 = mybir.dt.int32
ALU = mybir.AluOpType
ACT = mybir.ActivationFunctionType
AX_X = mybir.AxisListType.X

N = 3125
E = 100000
D = 128
HYPER = 625
HEADS, HID = 4, 32
P = 125
WIN = N // P
TILES = E // P
RROWS = 100
TPR = TILES // RROWS
HALF = 4
TEAMS = (TILES + WIN - 1 + (HALF - 1) * WIN) // HALF
STEPS = TEAMS * HALF
PAIR = 2 * HALF
LOOPS = TEAMS // 2
AHEAD = 4
PAD = STEPS + AHEAD * HALF
ACCW = D + 2 * HEADS + 1
BIG = 1.0e30
ROUND = 12582912.0
EPS = 1e-5
GROUPS = (WIN + 3) // 4
CHUNK = 391
SIDE = 4 * CHUNK
UNIT = 4096
FEW = 256
FIVE = 5
assert TEAMS % AHEAD == 0 and 2 * SIDE >= N and WIN % FIVE == 0
assert STEPS % PAIR == 0 and WIN * P == N and TILES * P == E


class Link:

    def __init__(self, eng, sem):
        self.eng, self.sem, self.n = eng, sem, 0

    def __call__(self, ins):
        ins.then_inc(self.sem, 1)
        self.n += 1
        self.eng.wait_ge(self.sem, self.n)


def each(ap, n):
    return ap.unsqueeze(2).broadcast_to([ap.shape[0], ap.shape[1], n])


def rows_of(ap, n):
    return ap.unsqueeze(1).broadcast_to([ap.shape[0], n, ap.shape[1]])


def windows(g):
    return range(4 * g, min(4 * g + 4, WIN))


def span(g):
    return len(windows(g)) * P


class Scope:

    stages = count()

    def __init__(self, nc):
        self.nc, self.ctx, self.stage, self.used = nc, ExitStack(), next(Scope.stages), []

    def __enter__(self):
        self.ctx.__enter__()
        return self

    def __exit__(self, *a):
        self.ctx.close()
        if self.used:
            rest = list(self.nc.free_semaphores)
            self.nc.clear_and_free_semaphores(self.used)
            freed = [n for n in self.nc.free_semaphores if n not in rest]
            self.nc.reset_free_semaphores(rest + freed)

    def sb(self, name, shape, dt=F32):
        return self.ctx.enter_context(self.nc.sbuf_tensor(f"{name}_{self.stage}", shape, dt))

    def ps(self, name, shape, dt=F32):
        return self.ctx.enter_context(self.nc.psum_tensor(f"{name}_{self.stage}", shape, dt))

    def sem(self, name):
        self.used.append(self.nc.alloc_semaphore(f"{name}_{self.stage}"))
        return self.used[-1]

    def sems(self, name):
        return [self.sem(f"{name}{p}") for p in range(2)]

    def block(self):
        return self.ctx.enter_context(self.nc.Block())



def load(nc, pairs):
    with Scope(nc) as sc:
        loaded = sc.sem("loaded")
        block = sc.block()

        @block.sync
        def _(sp):
            for dst, src in pairs:
                sp.dma_start(dst, src, allow_slow_non_contiguous=dst.shape[0] * dst.shape[-1] < 1000).then_inc(loaded, 16)
            sp.wait_ge(loaded, 16 * len(pairs))


def to_features(nc, ident, src, width, dst):
    with Scope(nc) as sc:
        bank = sc.ps("bank", [128, GROUPS, 512])
        turned = sc.sem("turned")
        block = sc.block()

        @block.tensor
        def _(pe):
            for g in range(GROUPS):
                for w in windows(g):
                    ins = pe.transpose(bank[0:width, g, (w % 4) * P:(w % 4 + 1) * P], src[:, w, 0:width], ident[0:P, 0:P])
                ins.then_inc(turned, 1)

        @block.scalar
        def _(act):
            for g in range(GROUPS):
                act.wait_ge(turned, g + 1)
                act.copy(dst[0:width, 4 * g * P:4 * g * P + span(g)], bank[0:width, g, 0:span(g)])


def to_nodes(nc, ident, src, dst):
    with Scope(nc) as sc:
        bank = sc.ps("bank", [128, GROUPS, 512])
        turned = sc.sem("turned")
        block = sc.block()

        @block.tensor
        def _(pe):
            for g in range(GROUPS):
                for w in windows(g):
                    ins = pe.transpose(bank[0:P, g, (w % 4) * D:(w % 4 + 1) * D], src[:, w * P:(w + 1) * P], ident[:, :])
                ins.then_inc(turned, 1)

        @block.scalar
        def _(act):
            for g in range(GROUPS):
                n = len(windows(g))
                act.wait_ge(turned, g + 1)
                act.copy(dst[:, 4 * g:4 * g + n, 0:D], bank[0:P, g, 0:n * D].rearrange("p (w f) -> p w f", f=D))


def linear_nodes(nc, terms, bias, dst):
    with Scope(nc) as sc:
        bank = sc.ps("bank", [128, GROUPS, 512])
        summed = sc.sem("summed")
        block = sc.block()

        @block.tensor
        def _(pe):
            for g in range(GROUPS):
                for w in windows(g):
                    for n, (x, m) in enumerate(terms):
                        ins = pe.matmul(bank[0:P, g, (w % 4) * D:(w % 4 + 1) * D], x[:, w * P:(w + 1) * P], m,
                                        start=n == 0, stop=n == len(terms) - 1)
                ins.then_inc(summed, 1)

        @block.vector
        def _(dve):
            for g in range(GROUPS):
                n = len(windows(g))
                dve.wait_ge(summed, g + 1)
                got = bank[0:P, g, 0:n * D].rearrange("p (w f) -> p w f", f=D)
                if bias is None:
                    dve.tensor_copy(dst[:, 4 * g:4 * g + n, 0:D], got)
                else:
                    dve.tensor_tensor(dst[:, 4 * g:4 * g + n, 0:D], got, rows_of(bias, n), ALU.add)


def linear_features(nc, x, w, func, bias, dst):
    m = w.shape[1]
    with Scope(nc) as sc:
        bank = sc.ps("bank", [128, GROUPS, 512])
        summed = sc.sem("summed")
        block = sc.block()

        @block.tensor
        def _(pe):
            for g in range(GROUPS):
                pe.matmul(bank[0:m, g, 0:span(g)], w, x[:, 4 * g * P:4 * g * P + span(g)],
                          start=True, stop=True).then_inc(summed, 1)

        @block.scalar
        def _(act):
            for g in range(GROUPS):
                act.wait_ge(summed, g + 1)
                act.activation(dst[0:m, 4 * g * P:4 * g * P + span(g)], bank[0:m, g, 0:span(g)], func, bias=bias)


def normalize(nc, y, eps, before=None, gain=None, shift=None, func=None, after=None):
    with Scope(nc) as sc:
        stats = sc.sb("stats", [P, WIN, 6])
        moments = sc.sb("moments", [P, WIN, 2])
        std = sc.sb("std", [P, WIN])
        rstd = sc.sb("rstd", [P, WIN])
        names = ("step", "stats_ready", "moments_ready", "std_ready", "centered", "scaled", "activated")
        step, stats_ready, moments_ready, std_ready, centered, scaled, activated = (sc.sem(x) for x in names)
        block = sc.block()

        @block.vector
        def _(dve):
            link = Link(dve, step)
            if before:
                before(dve, link)
            for w in range(WIN):
                dve.bn_stats(stats[:, w, :], y[:, w, :]).then_inc(stats_ready, 1)
            dve.wait_ge(stats_ready, WIN)
            for w in range(WIN):
                dve.bn_aggr(moments[:, w, :], stats[:, w, :]).then_inc(moments_ready, 1)
            dve.wait_ge(moments_ready, WIN)
            dve.wait_ge(std_ready, 1)
            link(dve.reciprocal(rstd[:, :], std[:, :]))
            if gain is not None:
                for w in range(WIN):
                    dve.scalar_tensor_tensor(out=y[:, w, :], in0=y[:, w, :], scalar=moments[:, w, 0:1], in1=gain,
                                             op0=ALU.subtract, op1=ALU.mult).then_inc(centered, 1)
                dve.wait_ge(centered, WIN)
            for w in range(WIN):
                if gain is None:
                    dve.tensor_scalar(y[:, w, :], y[:, w, :], moments[:, w, 0:1], rstd[:, w:w + 1], ALU.subtract, ALU.mult).then_inc(scaled, 1)
                else:
                    dve.scalar_tensor_tensor(out=y[:, w, :], in0=y[:, w, :], scalar=rstd[:, w:w + 1], in1=shift,
                                             op0=ALU.mult, op1=ALU.add).then_inc(scaled, 1)
            dve.wait_ge(scaled, WIN)
            if func is not None:
                dve.wait_ge(activated, WIN // FIVE)
            if after:
                after(dve, link)

        @block.scalar
        def _(act):
            act.wait_ge(moments_ready, WIN)
            act.activation(std[:, :], moments[:, :, 1], ACT.Sqrt, bias=eps[0:P, :]).then_inc(std_ready, 1)
            if func is not None:
                for w in range(0, WIN, FIVE):
                    act.wait_ge(scaled, w + FIVE)
                    act.activation(y[:, w:w + FIVE, :], y[:, w:w + FIVE, :], func).then_inc(activated, 1)


def vector_steps(nc, steps):
    with Scope(nc) as sc:
        step = sc.sem("step")
        block = sc.block()

        @block.vector
        def _(dve):
            steps(dve, Link(dve, step))




def prime(eng, *pairs):
    for pair in pairs:
        for sem in pair:
            eng.sem_inc(sem, 1)


def before(i, unit=1):
    return unit * i + 1


def done(i, unit=1):
    return unit * (i + 1) + 1


def landed(i, dmas=1):
    return 16 * dmas * (i + 1)


def hold(eng, sem, value, held_up):
    eng.wait_ge(sem, value)
    eng.sem_inc(held_up, 1)


def gather_rows(pool, i, p, table, rows, now, idx, held_up, freed, staged, rows_in):
    for sem in freed:
        hold(pool, sem[p], before(i), held_up)
    pool.tensor_copy(now[:, p, :], idx[:, bass.ds(PAIR * i + HALF * p, HALF)]).then_inc(staged[p], 1)
    hold(pool, staged[p], done(i), held_up)
    for j in range(HALF):
        pool.indirect_dma_start(rows[:, p, j, 0:D], None, table,
                                bass.IndirectOffsetOnAxis(ap=now[:, p, j:j + 1], axis=0)).then_inc(rows_in[p], 16)


def window_of(eng, g, k):
    return eng.value_load(g.team_win[0:1, bass.ds(k + 1, 1)], min_val=0, max_val=WIN - 1)


def windows_of(nc, eng, g, k):
    return nc.values_load_multi_w_load_instructions(g.team_win[0:1, bass.ds(k + 1, AHEAD)], engines=(eng.engine,), min_val=0, max_val=WIN - 1,
                                                    skip_runtime_bounds_check_because="prepare counts them up from 0, one for each later window")[1]


def one_hot(eng, g, out, i, p):
    return eng.tensor_tensor(out, rows_of(g.iota[0:P, 0:P], HALF),
                             each(g.slot[:, bass.ds(PAIR * i + HALF * p, HALF)], P), ALU.is_equal)


def add_sums(dve, g, i, p, sums, width, summed, added):
    w = window_of(dve, g, 2 * i + p)
    dve.wait_ge(summed[p], done(i))
    dve.wait_ge(added[1 - p], before(i + p))
    row = g.acc[:, bass.ds(w, 1), 0:width]
    dve.tensor_tensor(row, row, sums[:, p:p + 1, 0:width], ALU.add).then_inc(added[p], 1)


def sum_steps(pe, i, p, onehot, values, sums, width, made, values_ready, summed, added):
    pe.wait_ge(made[p], done(i))
    for sem, count in values_ready:
        pe.wait_ge(sem[p], count)
    pe.wait_ge(added[p], before(i))
    for j in range(HALF):
        ins = pe.matmul(sums[:, p, 0:width], onehot[:, p, j, :], values[:, p, j, 0:width], start=j == 0, stop=j == HALF - 1)
    ins.then_inc(summed[p], 1)


def many_pairs(eng, g):
    return eng.value_load(g.many[0:1, 0:1], min_val=0, max_val=1) > 0


def neighbour_sums(nc, g, table, y):
    width = D + 1
    with Scope(nc) as sc:
        rows = sc.sb("rows", [P, 2, HALF, width])
        now = sc.sb("now", [P, 2, HALF], I32)
        held_up = sc.sem("held_up")
        onehot = sc.sb("onehot", [P, 2, HALF, P])
        sums = sc.ps("sums", [P, 2, 512])
        ones_set, acc_clear, tabled = sc.sem("ones_set"), sc.sem("acc_clear"), sc.sem("tabled")
        staged, rows_in, made, summed, added = (sc.sems(x) for x in ("staged", "rows_in", "made", "summed", "added"))
        block = sc.block()

        @block.sync
        def _(sp):
            with sp.If(many_pairs(sp, g)):
                sp.dma_start(by_window(table), y[:, :, :]).then_inc(tabled, 16)
                sp.wait_ge(tabled, 16)

        @block.gpsimd
        def _(pool):
            with pool.If(many_pairs(pool, g)):
                prime(pool, staged)
                pool.wait_ge(tabled, 16)
                with pool.Fori(0, LOOPS) as i:
                    for p in range(2):
                        gather_rows(pool, i, p, table, rows, now, g.idx, held_up, [summed], staged, rows_in)

        @block.vector
        def _(dve):
            with dve.If(many_pairs(dve, g)):
                prime(dve, made, added)
                dve.memset(rows[:, :, :, D:width], 1.0).then_inc(ones_set, 1)
                dve.memset(g.acc[:, :, :], 0.0).then_inc(acc_clear, 1)
                dve.wait_ge(acc_clear, 1)
                for p in range(2):
                    one_hot(dve, g, onehot[:, p, :, :], 0, p).then_inc(made[p], 1)
                with dve.Fori(0, LOOPS) as i:
                    for p in range(2):
                        add_sums(dve, g, i, p, sums, width, summed, added)
                        one_hot(dve, g, onehot[:, p, :, :], i + 1, p).then_inc(made[p], 1)

        @block.tensor
        def _(pe):
            with pe.If(many_pairs(pe, g)):
                prime(pe, summed)
                pe.wait_ge(ones_set, 1)
                with pe.Fori(0, LOOPS) as i:
                    for p in range(2):
                        sum_steps(pe, i, p, onehot, rows, sums, width, made, [(rows_in, landed(i, HALF))], summed, added)



def begin(eng, *sems):
    for sem in sems:
        eng.sem_inc(sem, AHEAD)


def after(k, lag=0):
    return k - lag + 1 + AHEAD


def gather_teams(pool, table, rows, now, held_up, staged, kept, rows_in):
    with pool.Fori(0, TEAMS // AHEAD) as i:
        for q in range(AHEAD):
            k = AHEAD * i + q
            hold(pool, staged, after(k), held_up)
            if kept is not None:
                hold(pool, kept, after(k, AHEAD), held_up)
            for j in range(HALF):
                pool.indirect_dma_start(rows[:, q, j, :], None, table,
                                        bass.IndirectOffsetOnAxis(ap=now[:, q, j:j + 1], axis=0)).then_inc(rows_in[q], 16)


def hot_rows(dve, g, k, out):
    return dve.tensor_tensor(out, rows_of(g.iota[0:P, 0:P], HALF), each(g.slot[:, bass.ds(HALF * k, HALF)], P), ALU.is_equal)


def attention_logits(nc, g, table, xl, xr, att, spill, own_logit, logit, capped):
    with Scope(nc) as sc:
        rows = sc.sb("rows", [P, AHEAD, HALF, D])
        now = sc.sb("now", [P, AHEAD, HALF], I32)
        onehot = sc.sb("onehot", [P, AHEAD, HALF, P])
        onehot_t = sc.sb("onehot_t", [P, 2, HALF * P])
        z = sc.sb("z", [P, 2, HALF, D])
        warmed = sc.sb("warmed", [P, 1])
        turn = sc.ps("turn", [P, 2, 512])
        zp = sc.ps("zp", [P, 2, HALF, 256])
        zs = sc.sb("zs", [P, WIN, D])
        step, own_ready = sc.sem("step"), sc.sem("own_ready")
        names = ("held_up", "warm", "staged", "made", "turned", "copied", "spread", "added", "leaky", "scaled", "summed", "taken", "kept")
        held_up, warm, staged, made, turned, copied, spread, added, leaky, scaled, summed, taken, kept = (sc.sem(x) for x in names)
        rows_in = [sc.sem(f"rows_in{q}") for q in range(AHEAD)]
        spilled = [sc.sem(f"spilled{q}") for q in range(AHEAD)]
        block = sc.block()

        @block.gpsimd
        def _(pool):
            gather_teams(pool, table, rows, now, held_up, staged, kept, rows_in)

        @block.sync
        def _(sp):
            begin(sp, kept)
            with sp.Fori(0, TEAMS // AHEAD) as i:
                for q in range(AHEAD):
                    sp.wait_ge(rows_in[q], landed(i, HALF))
                    sp.dma_start(spill[bass.ds(AHEAD * i + q, 1), :, :].rearrange("a p f -> (a p) f"),
                                 rows[:, q, :, :].rearrange("p j f -> p (j f)")).then_inc(spilled[q], 16)
                    sp.wait_ge(spilled[q], landed(i))
                    sp.sem_inc(kept, 1)

        @block.scalar
        def _(act):
            begin(act, copied)
            act.copy(warmed[:, :], g.eps[0:P, :]).then_inc(warm, 1)
            with act.Fori(0, LOOPS) as i:
                for p in range(2):
                    k = 2 * i + p
                    act.wait_ge(turned, after(k))
                    act.wait_ge(spread, after(k, 2))
                    act.copy(onehot_t[:, p, :], turn[:, p, 0:HALF * P]).then_inc(copied, 1)

        @block.tensor
        def _(pe):
            begin(pe, turned, spread)

            def turn_rows(k, q):
                pe.wait_ge(made, after(k))
                pe.wait_ge(copied, after(k, 2))
                for j in range(HALF):
                    ins = pe.transpose(turn[:, q % 2, j * P:(j + 1) * P], onehot[:, q, j, :], g.ident[0:P, 0:P])
                ins.then_inc(turned, 1)

            for p in range(2):
                turn_rows(p, p)
            pe.wait_ge(own_ready, 1)
            with pe.Fori(0, TEAMS // AHEAD) as i:
                for q in range(AHEAD):
                    k, p = AHEAD * i + q, q % 2
                    w = window_of(pe, g, k)
                    own = xl[:, bass.ds(w, 1), :].rearrange("p w f -> p (w f)")
                    pe.wait_ge(copied, after(k))
                    pe.wait_ge(added, after(k, 2))
                    pe.wait_ge(taken, after(k, 2))
                    for j in range(HALF):
                        ins = pe.matmul(zp[:, p, j, 0:D + HEADS], onehot_t[:, p, j * P:(j + 1) * P], own, start=True, stop=True)
                    ins.then_inc(spread, 1)
                    turn_rows(k + 2, (q + 2) % AHEAD)

        @block.vector
        def _(dve):
            begin(dve, staged, made, added, leaky, scaled, summed, taken)
            for q in range(AHEAD):
                dve.tensor_copy(now[:, q, :], g.idx[:, HALF * q:HALF * q + HALF]).then_inc(staged, 1)
            link = Link(dve, step)
            link(dve.tensor_tensor(zs[:, :, :], xl[:, :, 0:D], xr[:, :, :], ALU.add))
            link(dve.scalar_tensor_tensor(out=zs[:, :, :], in0=zs[:, :, :], scalar=0.2, in1=zs[:, :, :], op0=ALU.mult, op1=ALU.max))
            link(dve.tensor_tensor(zs[:, :, :], zs[:, :, :], rows_of(att, WIN), ALU.mult))
            link(dve.tensor_reduce(own_logit[:, :, :], zs[:, :, :].rearrange("p w (h c) -> p w h c", h=HEADS), AX_X, ALU.add))
            dve.tensor_copy(xl[:, :, D:D + HEADS], own_logit[:, :, :]).then_inc(own_ready, 1)
            for q in range(AHEAD - 1):
                hot_rows(dve, g, q, onehot[:, q, :, :]).then_inc(made, 1)
            with dve.Fori(0, TEAMS // AHEAD) as i:
                for q in range(AHEAD):
                    k, p = AHEAD * i + q, q % 2
                    s = bass.ds(HALF * k, HALF)
                    zz = z[:, p, :, :]
                    dve.wait_ge(rows_in[q], landed(i, HALF))
                    dve.wait_ge(spread, after(k))
                    dve.wait_ge(summed, after(k, 2))
                    dve.tensor_tensor(zz, zp[:, p, :, 0:D], rows[:, q, :, :], ALU.add).then_inc(added, 1)
                    dve.wait_ge(turned, after(k, 1))
                    hot_rows(dve, g, k + 3, onehot[:, (q + 3) % AHEAD, :, :]).then_inc(made, 1)
                    dve.wait_ge(added, after(k))
                    dve.scalar_tensor_tensor(out=zz, in0=zz, scalar=0.2, in1=zz, op0=ALU.mult, op1=ALU.max).then_inc(leaky, 1)
                    dve.tensor_copy(now[:, q, :], g.idx[:, bass.ds(HALF * k + AHEAD * HALF, HALF)]).then_inc(staged, 1)
                    dve.wait_ge(leaky, after(k))
                    dve.tensor_tensor(zz, zz, rows_of(att, HALF), ALU.mult).then_inc(scaled, 1)
                    dve.wait_ge(scaled, after(k))
                    dve.tensor_reduce(logit[:, s, :], zz.rearrange("p j (h c) -> p j h c", h=HEADS), AX_X, ALU.add).then_inc(summed, 1)
                    dve.wait_ge(summed, after(k))
                    dve.tensor_tensor(capped[:, s, :], logit[:, s, :], zp[:, p, :, D:D + HEADS], ALU.max).then_inc(taken, 1)


def softmax_weights(nc, g, logit, capped, first_max):
    lanes = PAIR * P
    with Scope(nc) as sc:
        lrow = sc.sb("lrow", [LOOPS, HEADS, lanes])
        crow = sc.sb("crow", [LOOPS, HEADS, lanes])
        fwd = sc.sb("fwd", [LOOPS, lanes])
        mx = sc.sb("mx", [LOOPS, HEADS, lanes])
        ends = sc.sb("ends", [LOOPS, 2, HEADS])
        ends_t = sc.sb("ends_t", [HEADS, 2, LOOPS])
        run = sc.sb("run", [HEADS, 2, LOOPS])
        carry_t = sc.sb("carry_t", [HEADS, 2, LOOPS])
        carry = sc.sb("carry", [LOOPS, 2, HEADS])
        bank = sc.ps("bank", [128, 8, 512])

        with Scope(nc) as s1:
            turned, copied = s1.sem("turned"), s1.sem("copied")
            block = s1.block()
            jobs = [(a, b, h, q) for a, b in ((logit, lrow), (capped, crow)) for h in range(HEADS) for q in range(2)]

            @block.tensor
            def _(pe):
                for n, (a, b, h, q) in enumerate(jobs):
                    if n >= 8:
                        pe.wait_ge(copied, n - 7)
                    av = a[:, :, h].rearrange("p (c b) -> p c b", b=PAIR)
                    for k in range(4):
                        ins = pe.transpose(bank[0:LOOPS, n % 8, k * P:(k + 1) * P], av[:, :, 4 * q + k], g.ident[0:P, 0:P])
                    ins.then_inc(turned, 1)

            @block.scalar
            def _(act):
                for n, (a, b, h, q) in enumerate(jobs):
                    act.wait_ge(turned, n + 1)
                    act.copy(b[:, h, 4 * q * P:(4 * q + 4) * P], bank[0:LOOPS, n % 8, 0:4 * P]).then_inc(copied, 1)

        with Scope(nc) as s2:
            step, ends_ready, ends_turned, carry_ready, carry_turned = (s2.sem(x) for x in (
                "step", "ends_ready", "ends_turned", "carry_ready", "carry_turned"))
            block = s2.block()

            @block.vector
            def _(dve):
                link = Link(dve, step)
                for h in range(HEADS):
                    link(dve.tensor_tensor_scan(fwd[:, :], g.brk[:, 0:lanes], crow[:, h, :], -BIG, ALU.add, ALU.max))
                    link(dve.tensor_tensor_scan(mx[:, h, ::-1], g.brk[:, 1:lanes + 1][:, ::-1], crow[:, h, ::-1], -BIG, ALU.add, ALU.max))
                    link(dve.tensor_copy(ends[:, 0, h:h + 1], fwd[:, lanes - 1:lanes]))
                    link(dve.tensor_copy(ends[:, 1, h:h + 1], mx[:, h, 0:1]))
                    link(dve.tensor_tensor(mx[:, h, :], mx[:, h, :], fwd[:, :], ALU.max))
                dve.sem_inc(ends_ready, 1)
                dve.wait_ge(ends_turned, 1)
                for k in range(2):
                    link(dve.tensor_copy(ends_t[:, k, :], bank[0:HEADS, k, 0:LOOPS]))
                link(dve.tensor_tensor_scan(run[:, 0, :], g.whole_up[:, :], ends_t[:, 0, :], -BIG, ALU.add, ALU.max))
                link(dve.tensor_tensor_scan(run[:, 1, ::-1], g.whole_down[:, ::-1], ends_t[:, 1, ::-1], -BIG, ALU.add, ALU.max))
                link(dve.memset(carry_t[:, :, :], -BIG))
                link(dve.tensor_tensor(carry_t[:, 0, 1:LOOPS], run[:, 0, 0:LOOPS - 1], g.joint[:, 1:LOOPS], ALU.add))
                link(dve.tensor_tensor(carry_t[:, 1, 0:LOOPS - 1], run[:, 1, 1:LOOPS], g.joint[:, 1:LOOPS], ALU.add))
                dve.sem_inc(carry_ready, 1)
                dve.wait_ge(carry_turned, 1)
                for k in range(2):
                    link(dve.tensor_copy(carry[:, k, :], bank[0:LOOPS, 2 + k, 0:HEADS]))
                for h in range(HEADS):
                    link(dve.scalar_tensor_tensor(out=mx[:, h, :], in0=g.head_run[:, :], scalar=carry[:, 0, h:h + 1], in1=mx[:, h, :], op0=ALU.add, op1=ALU.max))
                    link(dve.scalar_tensor_tensor(out=mx[:, h, :], in0=g.tail_run[:, :], scalar=carry[:, 1, h:h + 1], in1=mx[:, h, :], op0=ALU.add, op1=ALU.max))
                    link(dve.tensor_tensor(lrow[:, h, :], lrow[:, h, :], mx[:, h, :], ALU.subtract))

            @block.tensor
            def _(pe):
                pe.wait_ge(ends_ready, 1)
                for k in range(2):
                    ins = pe.transpose(bank[0:HEADS, k, 0:LOOPS], ends[:, k, :], g.ident[0:LOOPS, 0:LOOPS])
                ins.then_inc(ends_turned, 1)
                pe.wait_ge(carry_ready, 1)
                for k in range(2):
                    ins = pe.transpose(bank[0:LOOPS, 2 + k, 0:HEADS], carry_t[:, k, :], g.ident[0:HEADS, 0:HEADS])
                ins.then_inc(carry_turned, 1)

        with Scope(nc) as s3:
            exped, turned, copied = s3.sem("exped"), s3.sem("turned"), s3.sem("copied")
            block = s3.block()
            jobs = [(a, b, h, q) for h in range(HEADS) for a, b in ((lrow, logit), (mx, first_max)) for q in range(2)]

            @block.scalar
            def _(act):
                for h in range(HEADS):
                    act.activation(lrow[:, h, :], lrow[:, h, :], ACT.Exp).then_inc(exped, 1)

            @block.tensor
            def _(pe):
                for n, (a, b, h, q) in enumerate(jobs):
                    pe.wait_ge(exped, h + 1)
                    if n >= 8:
                        pe.wait_ge(copied, n - 7)
                    for k in range(4):
                        ins = pe.transpose(bank[0:P, n % 8, k * LOOPS:(k + 1) * LOOPS], a[:, h, (4 * q + k) * P:(4 * q + k + 1) * P],
                                           g.ident[0:LOOPS, 0:LOOPS])
                    ins.then_inc(turned, 1)

            @block.vector
            def _(dve):
                for n, (a, b, h, q) in enumerate(jobs):
                    dve.wait_ge(turned, n + 1)
                    out = b[:, :, h].rearrange("p (c b) -> p b c", b=PAIR)[:, 4 * q:4 * q + 4, :]
                    got = bank[0:P, n % 8, 0:4 * LOOPS].rearrange("p (k c) -> p k c", k=4)
                    if b is first_max:
                        flag = g.first[:, 0:STEPS].rearrange("p (c b) -> p b c", b=PAIR)[:, 4 * q:4 * q + 4, :]
                        dve.tensor_tensor(out, got, flag, ALU.mult).then_inc(copied, 1)
                    else:
                        dve.tensor_copy(out, got).then_inc(copied, 1)


def attention_sums(nc, g, spill, weight, first_max):
    width = ACCW
    with Scope(nc) as sc:
        rows = sc.sb("rows", [P, AHEAD, HALF, D])
        values = sc.sb("values", [P, AHEAD, HALF, width])
        onehot = sc.sb("onehot", [P, AHEAD, HALF, P])
        warmed = sc.sb("warmed", [P, 1])
        sums = sc.ps("sums", [P, AHEAD, 512])
        names = ("held_up", "warm", "acc_clear", "made", "weighted", "tailed", "maxed", "marked", "summed", "accd")
        held_up, warm, acc_clear, made, weighted, tailed, maxed, marked, summed, accd = (sc.sem(x) for x in names)
        rows_in = [sc.sem(f"rows_in{q}") for q in range(AHEAD)]
        block = sc.block()

        @block.sync
        def _(sp):
            with sp.Fori(0, TEAMS // AHEAD) as i:
                for q in range(AHEAD):
                    k = AHEAD * i + q
                    sp.wait_ge(weighted, after(k, AHEAD))
                    sp.dma_start(rows[:, q, :, :].rearrange("p j f -> p (j f)"),
                                 spill[bass.ds(k, 1), :, :].rearrange("a p f -> (a p) f")).then_inc(rows_in[q], 16)

        @block.scalar
        def _(act):
            begin(act, tailed, maxed, marked)
            act.copy(warmed[:, :], g.eps[0:P, :]).then_inc(warm, 1)
            with act.Fori(0, TEAMS // AHEAD) as i:
                for q in range(AHEAD):
                    k = AHEAD * i + q
                    s = bass.ds(HALF * k, HALF)
                    act.wait_ge(summed, after(k, AHEAD))
                    act.copy(values[:, q, :, D:D + HEADS], weight[:, s, :]).then_inc(tailed, 1)
                    act.copy(values[:, q, :, D + HEADS:width - 1], first_max[:, s, :]).then_inc(maxed, 1)
                    act.copy(values[:, q, :, width - 1:width], g.first[:, s].unsqueeze(2)).then_inc(marked, 1)

        @block.gpsimd
        def _(pool):
            begin(pool, weighted)
            with pool.Fori(0, TEAMS // AHEAD) as i:
                for q in range(AHEAD):
                    k = AHEAD * i + q
                    pool.wait_ge(rows_in[q], landed(i))
                    hold(pool, summed, after(k, AHEAD), held_up)
                    pool.tensor_tensor(values[:, q, :, 0:D].rearrange("p j (h c) -> p j h c", h=HEADS),
                                       rows[:, q, :, :].rearrange("p j (h c) -> p j h c", h=HEADS),
                                       weight[:, bass.ds(HALF * k, HALF), :].unsqueeze(3).broadcast_to([P, HALF, HEADS, HID]), ALU.mult).then_inc(weighted, 1)

        @block.vector
        def _(dve):
            begin(dve, made, accd)
            dve.memset(g.acc[:, :, :], 0.0).then_inc(acc_clear, 1)
            dve.wait_ge(acc_clear, 1)

            def add_team(k, q, w):
                dve.wait_ge(summed, after(k))
                dve.wait_ge(accd, after(k, 1))
                row = g.acc[:, bass.ds(w, 1), 0:width]
                dve.tensor_tensor(row, row, sums[:, q:q + 1, 0:width], ALU.add).then_inc(accd, 1)

            def teams(i):
                ws = windows_of(nc, dve, g, AHEAD * i - 1)
                for q in range(AHEAD):
                    team(AHEAD * i + q, q, ws[q])

            def team(k, q, w):
                if not (isinstance(k, int) and k == 0):
                    add_team(k - 1, (q - 1) % AHEAD, w)
                dve.wait_ge(summed, after(k, 1))
                hot_rows(dve, g, k + 3, onehot[:, (q + 3) % AHEAD, :, :]).then_inc(made, 1)

            for q in range(AHEAD - 1):
                hot_rows(dve, g, q, onehot[:, q, :, :]).then_inc(made, 1)
            teams(0)
            with dve.Fori(1, TEAMS // AHEAD) as i:
                teams(i)
            add_team(TEAMS - 1, AHEAD - 1, window_of(dve, g, TEAMS - 1))

        @block.tensor
        def _(pe):
            begin(pe, summed)
            with pe.Fori(0, TEAMS // AHEAD) as i:
                for q in range(AHEAD):
                    k = AHEAD * i + q
                    pe.wait_ge(made, after(k))
                    pe.wait_ge(tailed, after(k))
                    pe.wait_ge(maxed, after(k))
                    pe.wait_ge(marked, after(k))
                    pe.wait_ge(weighted, after(k))
                    pe.wait_ge(accd, after(k, AHEAD))
                    for j in range(HALF):
                        ins = pe.matmul(sums[:, q, 0:width], onehot[:, q, j, :], values[:, q, j, :], start=j == 0, stop=j == HALF - 1)
                    ins.then_inc(summed, 1)


def message_sums(nc, g, table, own):
    width = D + 1
    with Scope(nc) as sc:
        rows = sc.sb("rows", [P, AHEAD, HALF, D])
        now = sc.sb("now", [P, AHEAD, HALF], I32)
        onehot = sc.sb("onehot", [P, AHEAD, HALF, P + 1])
        onehot_t = sc.sb("onehot_t", [P + 1, 2, HALF * P])
        z = sc.sb("z", [P, 2, HALF, D])
        hidden = sc.sb("hidden", [P, 2, HALF, D])
        values = sc.sb("values", [P, 2, HALF, width])
        turn = sc.ps("turn", [P + 1, 2, 512])
        zp = sc.ps("zp", [P, 2, HALF, D])
        sums = sc.ps("sums", [P, 2, 512])
        held_up_too = sc.sem("held_up_too")
        names = ("held_up", "acc_clear", "staged", "made", "weighed", "turned", "copied", "spread", "added", "active", "tailed", "weighted", "summed", "accd")
        held_up, acc_clear, staged, made, weighed, turned, copied, spread, added, active, tailed, weighted, summed, accd = (sc.sem(x) for x in names)
        rows_in = [sc.sem(f"rows_in{q}") for q in range(AHEAD)]
        block = sc.block()

        @block.gpsimd
        def _(pool):
            gather_teams(pool, table, rows, now, held_up, staged, None, rows_in)

        @block.scalar
        def _(act):
            begin(act, copied, active)

            def copy_turned(k, p):
                act.wait_ge(turned, after(k))
                act.wait_ge(spread, after(k, 2))
                act.activation(onehot_t[:, p, :], turn[:, p, 0:HALF * P], ACT.Identity).then_inc(copied, 1)

            copy_turned(0, 0)
            with act.Fori(0, LOOPS) as i:
                for p in range(2):
                    k = 2 * i + p
                    copy_turned(k + 1, 1 - p)
                    act.wait_ge(added, after(k))
                    act.wait_ge(weighted, after(k, 2))
                    act.activation(hidden[:, p, :, :], z[:, p, :, :], ACT.Silu).then_inc(active, 1)

        @block.tensor
        def _(pe):
            begin(pe, turned, spread, summed)

            def turn_rows(k, q):
                pe.wait_ge(made, after(k))
                pe.wait_ge(weighed, after(k))
                pe.wait_ge(copied, after(k, 2))
                for j in range(HALF):
                    ins = pe.transpose(turn[:, q % 2, j * P:(j + 1) * P], onehot[:, q, j, :], g.ident[0:P, 0:P])
                ins.then_inc(turned, 1)

            def spread_rows(k, p):
                w = window_of(pe, g, k)
                pe.wait_ge(copied, after(k))
                pe.wait_ge(added, after(k, 2))
                for j in range(HALF):
                    ins = pe.matmul(zp[:, p, j, :], onehot_t[:, p, j * P:(j + 1) * P],
                                    own[:, bass.ds(w, 1), :].rearrange("p w f -> p (w f)"), start=True, stop=True)
                ins.then_inc(spread, 1)

            def sum_team(k, q):
                pe.wait_ge(tailed, after(k))
                pe.wait_ge(weighted, after(k))
                pe.wait_ge(accd, after(k, 2))
                for j in range(HALF):
                    ins = pe.matmul(sums[:, q % 2, 0:width], onehot[:, q, j, 0:P], values[:, q % 2, j, :], start=j == 0, stop=j == HALF - 1)
                ins.then_inc(summed, 1)

            def team(k, q):
                spread_rows(k, q % 2)
                turn_rows(k + 2, (q + 2) % AHEAD)
                if not (isinstance(k, int) and k == 0):
                    sum_team(k - 1, (q - 1) % AHEAD)

            turn_rows(0, 0)
            turn_rows(1, 1)
            for q in range(AHEAD):
                team(q, q)
            with pe.Fori(1, TEAMS // AHEAD) as i:
                for q in range(AHEAD):
                    team(AHEAD * i + q, q)
            sum_team(TEAMS - 1, AHEAD - 1)

        @block.vector
        def _(dve):
            begin(dve, staged, made, weighed, added, tailed, weighted, accd)
            dve.memset(g.acc[:, :, :], 0.0).then_inc(acc_clear, 1)
            dve.wait_ge(acc_clear, 1)

            def make_rows(k, q):
                dve.wait_ge(summed, after(k, AHEAD))
                hot_rows(dve, g, k, onehot[:, q, :, 0:P]).then_inc(made, 1)
                dve.tensor_copy(onehot[:, q, :, P:P + 1], g.ew[:, bass.ds(HALF * k, HALF)].unsqueeze(2)).then_inc(weighed, 1)

            def weigh(k, p):
                s = bass.ds(HALF * k, HALF)
                dve.wait_ge(summed, after(k, 2))
                dve.wait_ge(active, after(k))
                dve.tensor_tensor(values[:, p, :, 0:D], hidden[:, p, :, :], each(g.ew[:, s], D), ALU.mult).then_inc(weighted, 1)
                dve.tensor_copy(values[:, p, :, D:width], g.ew[:, s].unsqueeze(2)).then_inc(tailed, 1)

            def add_team(k, p):
                w = window_of(dve, g, k)
                dve.wait_ge(summed, after(k))
                dve.wait_ge(accd, after(k, 1))
                row = g.acc[:, bass.ds(w, 1), 0:width]
                dve.tensor_tensor(row, row, sums[:, p:p + 1, 0:width], ALU.add).then_inc(accd, 1)

            def team(i, q):
                k, p = AHEAD * i + q, q % 2
                first = isinstance(k, int)
                if not (first and k < 1):
                    weigh(k - 1, 1 - p)
                dve.wait_ge(rows_in[q], landed(i, HALF))
                dve.wait_ge(spread, after(k))
                dve.wait_ge(active, after(k, 2))
                dve.tensor_tensor(z[:, p, :, :], zp[:, p, :, :], rows[:, q, :, :], ALU.add).then_inc(added, 1)
                make_rows(k + 2, (q + 2) % AHEAD)
                hold(dve, added, after(k), held_up_too)
                dve.tensor_copy(now[:, q, :], g.idx[:, bass.ds(HALF * k + AHEAD * HALF, HALF)]).then_inc(staged, 1)
                if not (first and k < 2):
                    add_team(k - 2, p)

            for q in range(AHEAD):
                dve.tensor_copy(now[:, q, :], g.idx[:, HALF * q:HALF * q + HALF]).then_inc(staged, 1)
            make_rows(0, 0)
            make_rows(1, 1)
            for q in range(AHEAD):
                team(0, q)
            with dve.Fori(1, TEAMS // AHEAD) as i:
                for q in range(AHEAD):
                    team(i, q)
            weigh(TEAMS - 1, 1)
            add_team(TEAMS - 2, 0)
            add_team(TEAMS - 1, 1)


def take_sums(dve, bank, chunks, plus, out):
    for k, n in chunks:
        at = slice(512 * k, 512 * k + n)
        if plus is None:
            dve.tensor_copy(out[:, at], bank[:, k, 0:n])
        else:
            dve.tensor_tensor(out[:, at], bank[:, k, 0:n], plus[:, at], ALU.add)


def scatter_to_sources(nc, g, table, y, out, plus):
    wide = N + 1
    chunks = [(k, min(512, N - 512 * k)) for k in range((N + 511) // 512)]
    with Scope(nc) as sc:
        rows = sc.sb("rows", [P, 2, HALF, D])
        now = sc.sb("now", [P, 2, HALF], I32)
        held_up = sc.sem("held_up")
        parts = [sc.sb(f"part{k}", [P, 2, HALF, D], BF16) for k in range(3)]
        nodes = sc.sb("nodes", [P, wide], F16)
        hot = sc.sb("hot", [P, 2, wide], BF16)
        zero = sc.sb("zero", [P, 512], BF16)
        bank = sc.ps("bank", [128, len(chunks), 512])
        cleared, finished, noded = sc.sem("cleared"), sc.sem("finished"), sc.sem("noded")
        tabled = sc.sem("tabled")
        staged, rows_in, hot_made, hot_used = (sc.sems(x) for x in ("staged", "rows_in", "hot_made", "hot_used"))
        cut = [sc.sems(f"cut{k}") for k in range(3)]
        left = [sc.sems(f"left{k}") for k in range(2)]
        block = sc.block()

        @block.sync
        def _(sp):
            with sp.If(many_pairs(sp, g)):
                sp.dma_start(by_window(table), y[:, :, :]).then_inc(tabled, 16)
                sp.wait_ge(tabled, 16)

        @block.gpsimd
        def _(pool):
            with pool.If(many_pairs(pool, g)):
                prime(pool, staged)
                pool.iota(nodes[:, :], pattern=[[1, wide]], base=-(N // 2), channel_multiplier=0,
                          allow_small_or_imprecise_dtypes=True).then_inc(noded, 1)
                pool.wait_ge(tabled, 16)
                with pool.Fori(0, LOOPS) as i:
                    for p in range(2):
                        gather_rows(pool, i, p, table, rows, now, g.key, held_up, [cut[2]], staged, rows_in)

        @block.vector
        def _(dve):
            with dve.If(many_pairs(dve, g)):
                prime(dve, hot_made, *cut, *left)
                dve.memset(zero[:, :], 0.0).then_inc(cleared, 1)
                dve.wait_ge(noded, 1)
                with dve.Fori(0, LOOPS) as i:
                    for p in range(2):
                        row = rows[:, p, :, :]
                        dve.wait_ge(rows_in[p], landed(i, HALF))
                        for b in range(2):
                            dve.wait_ge(hot_used[b], HALF * i + 2 * p + 1)
                        for k in range(3):
                            dve.tensor_copy(parts[k][:, p, :, :], row).then_inc(cut[k][p], 1)
                            if k < 2:
                                dve.wait_ge(cut[k][p], done(i))
                                dve.tensor_tensor(row, row, parts[k][:, p, :, :], ALU.subtract).then_inc(left[k][p], 1)
                                dve.wait_ge(left[k][p], done(i))
                        for j in range(HALF):
                            b, use = j % 2, HALF * i + 2 * p + j // 2
                            dve.wait_ge(hot_used[b], use + 3)
                            dve.tensor_scalar(hot[:, b, :], nodes[:, :], g.src_key[:, bass.ds(PAIR * i + HALF * p + j, 1)], None,
                                              ALU.is_equal).then_inc(hot_made[b], 1)
                dve.wait_ge(finished, 1)
                take_sums(dve, bank, chunks, plus, out)

        @block.tensor
        def _(pe):
            with pe.If(many_pairs(pe, g)):
                for sem in hot_used:
                    pe.sem_inc(sem, 3)
                pe.wait_ge(cleared, 1)
                for k, n in chunks:
                    pe.matmul(bank[:, k, 0:n], zero[:, 0:D], zero[:, 0:n], start=True, stop=False, skip_group_check=True)
                with pe.Fori(0, LOOPS) as i:
                    for p in range(2):
                        pe.wait_ge(cut[2][p], done(i))
                        for j in range(HALF):
                            b, use = j % 2, HALF * i + 2 * p + j // 2
                            pe.wait_ge(hot_made[b], use + 2)
                            for part in parts:
                                for k, n in chunks:
                                    ins = pe.matmul(bank[:, k, 0:n], part[:, p, j, :], hot[:, b, 512 * k:512 * k + n],
                                                    start=False, stop=False, skip_group_check=True)
                            ins.then_inc(hot_used[b], 1)
                for k, n in chunks:
                    ins = pe.matmul(bank[:, k, 0:n], zero[:, 0:D], zero[:, 0:n], start=False, stop=True, skip_group_check=True)
                ins.then_inc(finished, 1)



def count_pairs(nc, g, pairs, weight, source_weight):
    low = HYPER // P
    part = SIDE // 2
    with Scope(nc) as sc:
        counts = sc.sb("counts", [P, WIN, SIDE])
        with Scope(nc) as s1:
            nodes = s1.sb("nodes", [P, SIDE], F16)
            lanes = s1.sb("lanes", [P, P], BF16)
            hot = s1.sb("hot", [P, 2, HALF, SIDE], BF16)
            hot_dst = s1.sb("hot_dst", [P, 2, HALF, P], BF16)
            zero = s1.sb("zero", [P, CHUNK], BF16)
            warmed = s1.sb("warmed", [P, 1])
            bank = s1.ps("bank", [128, 4, 512])
            names = ("noded", "laned", "cleared", "made", "warm", "hot_made")
            noded, laned, cleared, made, warm, hot_made = (s1.sem(x) for x in names)
            hot_used, copied = (s1.sems(x) for x in ("hot_used", "copied"))
            block = s1.block()

            @block.gpsimd
            def _(pool):
                pool.iota(nodes[:, :], pattern=[[1, SIDE]], base=0, channel_multiplier=0,
                          allow_small_or_imprecise_dtypes=True).then_inc(noded, 1)

            @block.vector
            def _(dve):
                dve.memset(zero[:, :], 0.0).then_inc(cleared, 1)
                dve.tensor_copy(lanes[:, :], g.iota[0:P, :]).then_inc(laned, 1)
                dve.wait_ge(laned, 1)
                dve.wait_ge(noded, 1)
                with dve.Fori(0, LOOPS) as i:
                    for p in range(2):
                        k = 2 * i + p
                        dve.wait_ge(hot_used[1], after(k, 2))
                        dve.tensor_tensor(hot_dst[:, p, :, :], rows_of(lanes[:, :], HALF),
                                          each(g.slot[:, bass.ds(HALF * k, HALF)], P), ALU.is_equal).then_inc(made, 1)
                        for j in range(HALF):
                            s = bass.ds(HALF * k + j, 1)
                            dve.tensor_scalar(hot[:, p, j, :], nodes[:, :], g.src_lo[:, s], g.src_unit[:, s],
                                              ALU.is_equal, ALU.mult).then_inc(hot_made, 1)

            @block.tensor
            def _(pe):
                begin(pe, *hot_used)
                pe.wait_ge(cleared, 1)
                for b in range(4):
                    pe.matmul(bank[0:P, b, 0:CHUNK], zero[:, 0:P], zero[:, :], start=True, stop=False, skip_group_check=True)
                with pe.Fori(0, LOOPS) as i:
                    for p in range(2):
                        k = 2 * i + p
                        pe.wait_ge(made, k + 1)
                        for h in range(2):
                            pe.wait_ge(copied[h], after(k, 1))
                            for j in range(HALF):
                                pe.wait_ge(hot_made, HALF * k + j + 1)
                                for c in range(2):
                                    ins = pe.matmul(bank[0:P, 2 * h + c, 0:CHUNK], hot_dst[:, p, j, :], hot[:, p, j, (2 * h + c) * CHUNK:(2 * h + c + 1) * CHUNK],
                                                    start=False, stop=False, skip_group_check=True)
                            ins.then_inc(hot_used[h], 1)
                for h in range(2):
                    pe.wait_ge(copied[h], after(TEAMS, 1))
                for b in range(4):
                    pe.matmul(bank[0:P, b, 0:CHUNK], zero[:, 0:P], zero[:, :], start=False, stop=True, skip_group_check=True)

            @block.scalar
            def _(act):
                begin(act, *copied)
                act.copy(warmed[:, :], g.eps[0:P, :]).then_inc(warm, 1)
                with act.Fori(0, LOOPS) as i:
                    for p in range(2):
                        k = 2 * i + p
                        w = window_of(act, g, k)
                        for h in range(2):
                            act.wait_ge(hot_used[h], after(k))
                            act.wait_ge(copied[h], after(k, 1))
                            act.copy(counts[:, bass.ds(w, 1), h * part:(h + 1) * part].rearrange("p w (c n) -> p (w c) n", n=CHUNK),
                                     bank[0:P, 2 * h:2 * h + 2, 0:CHUNK]).then_inc(copied[h], 1)

        check_counts(nc, g, counts)
        with Scope(nc) as s3:
            weighed = s3.ps("weighed", [4, 8, 512])
            with Scope(nc) as s1:
                ring, items = 3, 2 * WIN
                own = s1.sb("own", [P, ring, part])
                high = s1.sb("high", [P, ring, part])
                out = s1.sb("out", [P, ring, 2, part], BF16)
                bias = s1.sb("bias", [P, 2])
                hw = s1.sb("hw", [P, WIN, 1])
                left = s1.sb("left", [P, WIN, 1])
                hw_parts = s1.sb("hw_parts", [P, WIN, 4], BF16)
                step, hw_in, hw_cut, used = (s1.sem(x) for x in ("step", "hw_in", "hw_cut", "used"))
                biased, own_made, high_made, rounded, upper, lower = (s1.sem(x) for x in ("biased", "own_made", "high_made", "rounded", "upper", "lower"))
                stored = [s1.sem(f"stored{r}") for r in range(ring)]
                block = s1.block()

                def columns(u, before=0):
                    return counts[:, u // 2 - before, (u % 2) * part:(u % 2 + 1) * part]

                @block.gpsimd
                def _(pool):
                    for u in range(items):
                        if u >= ring:
                            pool.wait_ge(lower, u - ring + 1)
                        if u < 2:
                            pool.tensor_copy(own[:, u % ring, :], columns(u)).then_inc(own_made, 1)
                        else:
                            pool.tensor_tensor(own[:, u % ring, :], columns(u), columns(u, 1), ALU.subtract).then_inc(own_made, 1)

                @block.scalar
                def _(act):
                    act.wait_ge(biased, 2)
                    for u in range(items + 1):
                        if u < items:
                            act.wait_ge(own_made, u + 1)
                            if u >= ring:
                                act.wait_ge(upper, u - ring + 1)
                            act.activation(high[:, u % ring, :], own[:, u % ring, :], ACT.Identity, bias=bias[:, 0:1], scale=1.0 / UNIT).then_inc(high_made, 1)
                        if u >= 1:
                            v = u - 1
                            act.wait_ge(rounded, v + 1)
                            if v >= ring:
                                act.wait_ge(stored[v % ring], 16 * (v // ring))
                                act.wait_ge(used, v - ring + 1)
                                act.wait_ge(lower, v - ring + 1)
                            act.activation(out[:, v % ring, 1, :], high[:, v % ring, :], ACT.Identity, bias=bias[:, 1:2]).then_inc(upper, 1)

                @block.vector
                def _(dve):
                    link = Link(dve, step)
                    dve.wait_ge(hw_in, 16 * 2)
                    link(dve.tensor_copy(hw[:, low + 1:WIN, :], hw[:, low:low + 1, :].broadcast_to([P, WIN - low - 1, 1])))
                    rows = hw
                    for k in range(3):
                        link(dve.tensor_copy(hw_parts[:, :, k:k + 1], rows[:, :, :]))
                        if k < 2:
                            link(dve.tensor_tensor(left[:, :, :], rows[:, :, :], hw_parts[:, :, k:k + 1], ALU.subtract))
                        rows = left
                    dve.sem_inc(hw_cut, 1)
                    dve.memset(bias[:, 0:1], -0.5 + 0.5 / UNIT).then_inc(biased, 1)
                    dve.memset(bias[:, 1:2], -ROUND).then_inc(biased, 1)
                    for u in range(items + 1):
                        if u < items:
                            dve.wait_ge(high_made, u + 1)
                            dve.tensor_scalar(high[:, u % ring, :], high[:, u % ring, :], ROUND, None, ALU.add).then_inc(rounded, 1)
                        if u >= 1:
                            v = u - 1
                            if v >= ring:
                                dve.wait_ge(stored[v % ring], 16 * (v // ring))
                                dve.wait_ge(used, v - ring + 1)
                            dve.wait_ge(upper, v + 1)
                            dve.wait_ge(own_made, v + 1)
                            dve.scalar_tensor_tensor(out=out[:, v % ring, 0, :], in0=out[:, v % ring, 1, :], scalar=-float(UNIT), in1=own[:, v % ring, :],
                                                     op0=ALU.mult, op1=ALU.add).then_inc(lower, 1)

                @block.tensor
                def _(pe):
                    pe.wait_ge(hw_cut, 1)
                    for u in range(items):
                        w, h, r = u // 2, u % 2, u % ring
                        pe.wait_ge(lower, u + 1)
                        pe.wait_ge(upper, u + 1)
                        for s in range(2):
                            for c in range(2):
                                ins = pe.matmul(weighed[0:3, 4 * s + 2 * h + c, 0:CHUNK], hw_parts[:, w, 0:3], out[:, r, s, c * CHUNK:(c + 1) * CHUNK],
                                                start=w == 0, stop=w == WIN - 1)
                        ins.then_inc(used, 1)

                @block.sync
                def _(sp):
                    sp.dma_start(hw[:, 0:low, :], weight.rearrange("(w p a) -> p w a", p=P, a=1), allow_slow_non_contiguous=True).then_inc(hw_in, 16)
                    sp.dma_start(hw[:, low, :], weight[HYPER - 1:HYPER].partition_broadcast(P), allow_slow_non_contiguous=True).then_inc(hw_in, 16)
                    for u in range(items):
                        r = u % ring
                        sp.wait_ge(lower, u + 1)
                        sp.wait_ge(upper, u + 1)
                        sp.dma_start(pairs[u // 2, :, :].rearrange("p (s h n) -> p s h n", s=2, h=2)[:, :, u % 2, :], out[:, r, :, :]).then_inc(stored[r], 16)
                    for r in range(ring):
                        sp.wait_ge(stored[r], 16 * len(range(r, items, ring)))
            with Scope(nc) as s1:
                rows = s1.sb("rows", [4, 8, CHUNK])
                taken, stored = s1.sem("taken"), s1.sem("stored")
                block = s1.block()

                @block.vector
                def _(dve):
                    dve.tensor_copy(rows[0:3, :, :], weighed[0:3, :, 0:CHUNK]).then_inc(taken, 1)

                @block.sync
                def _(sp):
                    sp.wait_ge(taken, 1)
                    sp.dma_start(source_weight, rows[0:3, :, :].rearrange("p c n -> p (c n)")).then_inc(stored, 16)
                    sp.wait_ge(stored, 16)


def check_counts(nc, g, counts):
    with Scope(nc) as sc:
        high = sc.sb("high", [P, SIDE])
        low = sc.sb("low", [P, SIDE])
        most = sc.sb("most", [P, 4])
        flag = sc.sb("flag", [P, 2])
        ones = sc.sb("ones", [P, P])
        total = sc.ps("total", [P, 512])
        step, ready, summed = sc.sem("step"), sc.sem("ready"), sc.sem("summed")
        block = sc.block()

        @block.vector
        def _(dve):
            link = Link(dve, step)
            link(dve.memset(ones[:, :], 1.0))
            link(dve.tensor_scalar(high[:, :], counts[:, WIN - 1, :], 1.0 / UNIT, -0.5 + 0.5 / UNIT, ALU.mult, ALU.add))
            link(dve.tensor_scalar(high[:, :], high[:, :], ROUND, None, ALU.add))
            link(dve.tensor_scalar(high[:, :], high[:, :], -ROUND, None, ALU.add))
            link(dve.scalar_tensor_tensor(out=low[:, :], in0=high[:, :], scalar=-float(UNIT), in1=counts[:, WIN - 1, :], op0=ALU.mult, op1=ALU.add))
            link(dve.tensor_reduce(most[:, 0:1], high[:, :], AX_X, ALU.max))
            link(dve.tensor_reduce(most[:, 1:2], low[:, :], AX_X, ALU.max))
            link(dve.tensor_reduce(most[:, 2:3], high[:, :], AX_X, ALU.add))
            link(dve.tensor_reduce(most[:, 3:4], low[:, :], AX_X, ALU.add))
            link(dve.tensor_tensor(flag[:, 0:1], most[:, 0:1], most[:, 1:2], ALU.max))
            link(dve.tensor_scalar(flag[:, 0:1], flag[:, 0:1], float(FEW), None, ALU.is_gt))
            link(dve.tensor_tensor(flag[:, 1:2], most[:, 2:3], most[:, 3:4], ALU.add))
            dve.sem_inc(ready, 1)
            dve.wait_ge(summed, 1)
            link(dve.tensor_scalar(flag[:, 0:1], total[:, 0:1], 1.0, None, ALU.min))
            link(dve.tensor_scalar(flag[:, 1:2], total[:, 1:2], float(E), None, ALU.not_equal))
            link(dve.tensor_tensor(flag[:, 0:1], flag[:, 0:1], flag[:, 1:2], ALU.max))
            link(dve.tensor_copy(g.many[:, :], flag[0:1, 0:1]))

        @block.tensor
        def _(pe):
            pe.wait_ge(ready, 1)
            pe.matmul(total[:, 0:2], ones[:, :], flag[:, :], start=True, stop=True).then_inc(summed, 1)


def cut_rows(dve, link, y, rest, parts, cut):
    for w in range(0, WIN, FIVE):
        rows, left = y[:, w:w + FIVE, :], rest[:, w:w + FIVE, :]
        for k in range(3):
            link(dve.tensor_copy(parts[:, k, w:w + FIVE, :], rows))
            if k < 2:
                link(dve.tensor_tensor(left, rows, parts[:, k, w:w + FIVE, :], ALU.subtract))
            rows = left
        dve.sem_inc(cut, 1)


def sums_to_sources(nc, g, table, pairs, y, out, plus=None):
    chunks = [(k, min(512, N - 512 * k)) for k in range((N + 511) // 512)]
    with Scope(nc) as sc:
        rest = sc.sb("rest", [P, WIN, D])
        parts = sc.sb("parts", [P, 3, WIN, D], BF16)
        counts = sc.sb("counts", [P, FIVE, 2 * SIDE], BF16)
        zero = sc.sb("zero", [P, 512], BF16)
        bank = sc.ps("bank", [128, len(chunks), 512])
        step, cleared, cut, finished = (sc.sem(x) for x in ("step", "cleared", "cut", "finished"))
        counts_in = [sc.sem(f"counts_in{b}") for b in range(FIVE)]
        counts_used = [sc.sem(f"counts_used{b}") for b in range(FIVE)]
        block = sc.block()

        @block.sync
        def _(sp):
            with sp.Fori(0, WIN // FIVE) as i:
                for b in range(FIVE):
                    sp.wait_ge(counts_used[b], before(i))
                    sp.dma_start(counts[:, b, :], pairs[bass.ds(FIVE * i + b, 1), :, :].rearrange("w p n -> (w p) n")).then_inc(counts_in[b], 16)

        @block.vector
        def _(dve):
            link = Link(dve, step)
            dve.memset(zero[:, :], 0.0).then_inc(cleared, 1)
            cut_rows(dve, link, y, rest, parts, cut)
            dve.wait_ge(finished, 1)
            take_sums(dve, bank, chunks, plus, out)

        @block.tensor
        def _(pe):
            prime(pe, counts_used)
            pe.wait_ge(cleared, 1)
            for k, n in chunks:
                pe.matmul(bank[:, k, 0:n], zero[:, 0:D], zero[:, 0:n], start=True, stop=False, skip_group_check=True)
            with pe.Fori(0, WIN // FIVE) as i:
                pe.wait_ge(cut, i + 1)
                for b in range(FIVE):
                    pe.wait_ge(counts_in[b], landed(i))
                    for part in range(3):
                        rows = parts[:, part, bass.ds(FIVE * i + b, 1), :].rearrange("p w f -> p (w f)")
                        for k, n in chunks:
                            ins = pe.matmul(bank[:, k, 0:n], rows, counts[:, b, 512 * k:512 * k + n], start=False, stop=False, skip_group_check=True)
                    ins.then_inc(counts_used[b], 1)
            for k, n in chunks:
                ins = pe.matmul(bank[:, k, 0:n], zero[:, 0:D], zero[:, 0:n], start=False, stop=True, skip_group_check=True)
            ins.then_inc(finished, 1)

    scatter_to_sources(nc, g, table, y, out, plus)


def sums_to_hyperedges(nc, g, table, pairs, y):
    low = HYPER // P
    with Scope(nc) as sc:
        rest = sc.sb("rest", [P, WIN, D])
        parts = sc.sb("parts", [P, 3, WIN, D], BF16)
        counts = sc.sb("counts", [P, low, 2 * SIDE], BF16)
        counts_t = sc.sb("counts_t", [P, FIVE, HYPER], BF16)
        ident = sc.sb("ident", [P, P], BF16)
        zero = sc.sb("zero", [P, 512], BF16)
        turn = sc.ps("turn", [P, FIVE, 8, D], BF16)
        sums = sc.ps("sums", [P, 2, 512])
        step, cleared, cut, finished, counts_in = (sc.sem(x) for x in ("step", "cleared", "cut", "finished", "counts_in"))
        turned, copied, used = ([sc.sem(f"{x}{b}") for b in range(FIVE)] for x in ("turned", "copied", "used"))
        block = sc.block()
        at = lambda w: sums[:, w // 4, (w % 4) * D:(w % 4 + 1) * D]

        @block.sync
        def _(sp):
            sp.dma_start(counts[:, :, :], pairs[0:low, :, :].rearrange("w p n -> p w n")).then_inc(counts_in, 16)

        @block.vector
        def _(dve):
            link = Link(dve, step)
            link(dve.tensor_copy(ident[:, :], g.ident[0:P, 0:P]))
            dve.memset(zero[:, :], 0.0).then_inc(cleared, 1)
            dve.wait_ge(cleared, 1)
            dve.sem_inc(cleared, 1)
            cut_rows(dve, link, y, rest, parts, cut)
            dve.wait_ge(counts_in, 16)
            dve.tensor_reduce(g.acc[:, 0:low, D], counts[:, :, :], AX_X, ALU.add)
            dve.wait_ge(finished, 1)
            dve.tensor_copy(g.acc[:, 0:4, 0:D], sums[:, 0, :].rearrange("p (w f) -> p w f", f=D))
            dve.tensor_copy(g.acc[:, 4, 0:D], at(4))

        @block.tensor
        def _(pe):
            prime(pe, used)
            pe.wait_ge(cleared, 2)
            pe.matmul(sums[:, 0, :], zero[:, 0:P], zero[:, :], start=True, stop=False, skip_group_check=True)
            pe.matmul(at(4), zero[:, 0:P], zero[:, 0:D], start=True, stop=False, skip_group_check=True)
            pe.wait_ge(counts_in, 16)
            with pe.Fori(0, WIN // FIVE) as i:
                pe.wait_ge(cut, i + 1)
                for b in range(FIVE):
                    pe.wait_ge(copied[b], before(i))
                    for w in range(low):
                        ins = pe.transpose(turn[:, b, w, 0:P], counts[:, w, bass.ds(P * (FIVE * i + b), P)], ident[:, :])
                    ins.then_inc(turned[b], 1)
                for b in range(FIVE):
                    pe.wait_ge(copied[b], done(i))
                    for w in range(low):
                        for part in range(3):
                            ins = pe.matmul(at(w), counts_t[:, b, w * P:(w + 1) * P], parts[:, part, bass.ds(FIVE * i + b, 1), :].rearrange("p w f -> p (w f)"),
                                            start=False, stop=False, skip_group_check=True)
                    ins.then_inc(used[b], 1)
            pe.matmul(sums[:, 0, :], zero[:, 0:P], zero[:, :], start=False, stop=True, skip_group_check=True)
            pe.matmul(at(4), zero[:, 0:P], zero[:, 0:D], start=False, stop=True, skip_group_check=True).then_inc(finished, 1)

        @block.scalar
        def _(act):
            prime(act, copied)
            with act.Fori(0, WIN // FIVE) as i:
                for b in range(FIVE):
                    act.wait_ge(turned[b], i + 1)
                    act.wait_ge(used[b], before(i))
                    act.copy(counts_t[:, b, :].rearrange("p (w n) -> p w n", n=P), turn[:, b, 0:low, 0:P]).then_inc(copied[b], 1)
    neighbour_sums(nc, g, table, y)



class Graph:
    pass


def prepare(nc, g, sc, src, dst, edge_weight):
    lanes = PAIR * P
    g.ident = sc.sb("ident", [128, 128])
    g.iota = sc.sb("iota", [128, P])
    g.eps = sc.sb("eps", [128, 1])
    g.many = sc.sb("many", [1, 1], I32)
    g.slot = sc.sb("slot", [P, PAD])
    g.first = sc.sb("first", [P, PAD])
    g.ew = sc.sb("ew", [P, PAD])
    g.key = sc.sb("key", [P, PAD])
    g.src_lo = sc.sb("src_lo", [P, PAD])
    g.src_unit = sc.sb("src_unit", [P, PAD])
    g.team_win = sc.sb("team_win", [1, TEAMS + 1], I32)

    with Scope(nc) as s1:
        rlen = E // RROWS
        src_i = s1.sb("src_i", [RROWS, rlen], I32)
        dst_i = s1.sb("dst_i", [RROWS, rlen], I32)
        pre_i = s1.sb("pre_i", [RROWS, rlen], I32)
        row = [s1.sb(f"row{k}", [RROWS, rlen]) for k in range(4)]
        pre = s1.sb("pre", [RROWS, rlen])
        ones = s1.sb("ones", [RROWS, rlen])
        junk = s1.sb("junk", [RROWS, rlen])
        below = s1.sb("below", [RROWS, WIN - 1])
        eight = s1.sb("eight", [P, 1])
        pick = s1.sb("pick", [RROWS, TPR, STEPS])
        got = s1.sb("got", [P, STEPS])
        from_ = s1.sb("from", [P, STEPS])
        valid = s1.sb("valid", [P, STEPS])
        half = STEPS // 2
        teams = s1.sb("teams", [P, TEAMS])
        tile = s1.sb("tile", [P, STEPS])
        win = [s1.sb(f"win{k}", [P, TEAMS]) for k in range(2)]
        offset = s1.sb("offset", [P, TEAMS])
        move = s1.sb("move", [P, TEAMS])
        low = s1.sb("low", [P, WIN])
        span_ = s1.sb("span", [P, WIN])
        upto = s1.sb("upto", [P, WIN])
        none = s1.sb("none", [P, WIN])
        start = s1.sb("start", [P, WIN])

        with Scope(nc) as s2:
            loaded, pre_set, zeroed, drawn = (s2.sem(x) for x in ("loaded", "pre_set", "zeroed", "drawn"))
            step, counted, totals = s2.sem("step"), s2.sem("counted"), s2.sem("totals")
            total = s2.ps("total", [P, 512])
            block = s2.block()

            @block.sync
            def _(sp):
                sp.dma_start(src_i[:, :], src.rearrange("(r l) -> r l", l=rlen)).then_inc(loaded, 16)
                sp.dma_start(dst_i[:, :], dst.rearrange("(r l) -> r l", l=rlen)).then_inc(loaded, 16)
                sp.dma_start(row[2][:, :], edge_weight.rearrange("(r l) -> r l", l=rlen)).then_inc(loaded, 16)
                sp.dma_start(pre_i[1:RROWS, :], dst[rlen - 1:E - 1].rearrange("(r l) -> r l", l=rlen)).then_inc(loaded, 16)
                sp.dma_start(pre_i[0:1, 1:rlen], dst[0:rlen - 1].rearrange("(r l) -> r l", r=1)).then_inc(loaded, 16)

            @block.gpsimd
            def _(pool):
                pool.memset(pre_i[0:1, 0:1], -1).then_inc(pre_set, 1)
                pool.memset(g.ident[:, :], 0.0).then_inc(zeroed, 1)
                pool.wait_ge(zeroed, 1)
                pool.affine_select(out=g.ident[:, :], in_=g.ident[:, :], compare_op=ALU.not_equal, fill=1.0, base=0,
                                   pattern=[[-1, 128]], channel_multiplier=1).then_inc(drawn, 1)
                for out, pattern, base, by in ((g.iota, [[1, P]], 0, 0), (eight, [[0, 1]], 0, TPR), (teams, [[1, TEAMS]], 0, 0), (tile, [[1, STEPS]], 0, 0)):
                    pool.iota(out[:, :], pattern=pattern, base=base, channel_multiplier=by,
                              allow_small_or_imprecise_dtypes=True).then_inc(drawn, 1)

            @block.vector
            def _(dve):
                link = Link(dve, step)
                link(dve.memset(g.eps[:, :], EPS))
                link(dve.memset(ones[:, :], 1.0))
                for t, v in ((g.slot, -1.0), (g.first, 0.0), (g.ew, 0.0), (g.key, -1.0), (g.src_lo, -2000.0), (g.src_unit, 1.0)):
                    link(dve.memset(t[:, STEPS:PAD], v))
                dve.wait_ge(loaded, 16 * 5)
                dve.wait_ge(pre_set, 1)
                link(dve.tensor_copy(row[0][:, :], src_i[:, :]))
                link(dve.tensor_copy(row[1][:, :], dst_i[:, :]))
                link(dve.tensor_copy(pre[:, :], pre_i[:, :]))
                link(dve.tensor_tensor(row[3][:, :], row[1][:, :], pre[:, :], ALU.not_equal))
                for w in range(1, WIN):
                    link(dve.scalar_tensor_tensor(out=junk[:, :], in0=row[1][:, :], scalar=float(P * w), in1=ones[:, :],
                                                  op0=ALU.is_lt, op1=ALU.mult, accum_out=below[:, w - 1:w]))
                dve.sem_inc(counted, 1)
                dve.wait_ge(totals, 1)
                link(dve.memset(low[:, :], 0.0))
                link(dve.tensor_scalar(low[:, 1:WIN], total[:, 0:WIN - 1], -float(P // 2), 1.0 / P, ALU.add, ALU.mult))
                link(dve.tensor_scalar(low[:, 1:WIN], low[:, 1:WIN], ROUND, None, ALU.add))
                link(dve.tensor_scalar(low[:, 1:WIN], low[:, 1:WIN], -ROUND, None, ALU.add))
                link(dve.memset(span_[:, :], float(TILES)))
                link(dve.tensor_scalar(span_[:, 0:WIN - 1], total[:, 0:WIN - 1], float(P // 2), 1.0 / P, ALU.add, ALU.mult))
                link(dve.tensor_scalar(span_[:, 0:WIN - 1], span_[:, 0:WIN - 1], ROUND, None, ALU.add))
                link(dve.tensor_scalar(span_[:, 0:WIN - 1], span_[:, 0:WIN - 1], -ROUND, None, ALU.add))
                link(dve.tensor_tensor(span_[:, :], span_[:, :], low[:, :], ALU.subtract))
                link(dve.tensor_scalar(span_[:, :], span_[:, :], 1.0, None, ALU.max))
                link(dve.tensor_scalar(span_[:, :], span_[:, :], (HALF - 1) / 2, 1.0 / HALF, ALU.add, ALU.mult))
                link(dve.tensor_scalar(span_[:, :], span_[:, :], ROUND, None, ALU.add))
                link(dve.tensor_scalar(span_[:, :], span_[:, :], -ROUND, None, ALU.add))
                link(dve.memset(none[:, :], 0.0))
                link(dve.tensor_tensor_scan(upto[:, :], none[:, :], span_[:, :], 0.0, ALU.add, ALU.add))
                link(dve.memset(start[:, :], 0.0))
                link(dve.scalar_tensor_tensor(out=start[:, 1:WIN], in0=upto[:, 0:WIN - 1], scalar=-float(HALF), in1=low[:, 1:WIN], op0=ALU.mult, op1=ALU.add))
                link(dve.tensor_tensor(none[:, 1:WIN], start[:, 1:WIN], start[:, 0:WIN - 1], ALU.subtract))
                link(dve.memset(win[0][:, :], 0.0))
                link(dve.memset(offset[:, :], 0.0))
                dve.wait_ge(drawn, 5)
                for w in range(1, WIN):
                    link(dve.scalar_tensor_tensor(out=win[w % 2][:, :], in0=teams[:, :], scalar=upto[:, w - 1:w], in1=win[1 - w % 2][:, :],
                                                  op0=ALU.is_ge, op1=ALU.add))
                    link(dve.tensor_scalar(move[:, :], teams[:, :], upto[:, w - 1:w], none[:, w:w + 1], ALU.is_ge, ALU.mult))
                    link(dve.tensor_tensor(offset[:, :], offset[:, :], move[:, :], ALU.add))
                link(dve.memset(g.team_win[:, :], 0))
                link(dve.tensor_copy(g.team_win[:, 1:TEAMS + 1], win[0][0:1, :]))
                by_team = tile[:, :].rearrange("p (t j) -> p t j", j=HALF)
                link(dve.tensor_tensor(by_team, by_team, each(offset[:, :], HALF), ALU.add))
                link(dve.tensor_scalar(tile[:, :], tile[:, :], eight[:, :], None, ALU.subtract))
                for b8 in range(TPR):
                    link(dve.tensor_scalar(pick[:, b8, :], tile[0:RROWS, :], float(b8), None, ALU.is_equal))

            @block.tensor
            def _(pe):
                pe.wait_ge(counted, 1)
                pe.matmul(total[:, 0:WIN - 1], ones[:, 0:P], below[:, :], start=True, stop=True).then_inc(totals, 1)
        assert (WIN - 1) % 2 == 0

        with Scope(nc) as s2:
            bank = s2.ps("bank", [P, 8, 512])
            step, picked = s2.sem("step"), s2.sem("picked")
            block = s2.block()

            @block.tensor
            def _(pe):
                for k in range(4):
                    for h in range(2):
                        for b8 in range(TPR):
                            ins = pe.matmul(bank[:, 2 * k + h, 0:half], row[k][:, b8 * P:(b8 + 1) * P],
                                            pick[:, b8, h * half:(h + 1) * half], start=b8 == 0, stop=b8 == TPR - 1)
                    ins.then_inc(picked, 1)

            @block.vector
            def _(dve):
                link = Link(dve, step)

                def two(t):
                    return t.rearrange("p (h s) -> p h s", h=2)

                dve.wait_ge(picked, 2)
                link(dve.tensor_copy(two(from_[:, :]), bank[:, 0:2, 0:half]))
                link(dve.tensor_copy(two(got[:, :]), bank[:, 2:4, 0:half]))
                link(dve.scalar_tensor_tensor(out=g.slot[:, 0:STEPS].rearrange("p (t j) -> p t j", j=HALF), in0=each(win[0][:, :], HALF), scalar=-float(P),
                                              in1=got[:, :].rearrange("p (t j) -> p t j", j=HALF), op0=ALU.mult, op1=ALU.add))
                link(dve.tensor_scalar(valid[:, :], g.slot[:, 0:STEPS], 0.0, None, ALU.is_ge))
                link(dve.scalar_tensor_tensor(out=valid[:, :], in0=g.slot[:, 0:STEPS], scalar=float(P), in1=valid[:, :], op0=ALU.is_lt, op1=ALU.mult))
                link(dve.scalar_tensor_tensor(out=g.key[:, 0:STEPS], in0=got[:, :], scalar=1.0, in1=valid[:, :], op0=ALU.add, op1=ALU.mult))
                link(dve.tensor_scalar(g.key[:, 0:STEPS], g.key[:, 0:STEPS], -1.0, None, ALU.add))
                lo, unit = g.src_lo[:, 0:STEPS], g.src_unit[:, 0:STEPS]
                link(dve.tensor_scalar(lo, from_[:, :], float(SIDE), -float(SIDE), ALU.is_ge, ALU.mult))
                link(dve.tensor_tensor(lo, lo, from_[:, :], ALU.add))
                link(dve.scalar_tensor_tensor(out=lo, in0=lo, scalar=2000.0, in1=valid[:, :], op0=ALU.add, op1=ALU.mult))
                link(dve.tensor_scalar(lo, lo, -2000.0, None, ALU.add))
                link(dve.tensor_scalar(unit, from_[:, :], float(SIDE), UNIT - 1.0, ALU.is_ge, ALU.mult))
                link(dve.tensor_scalar(unit, unit, 1.0, None, ALU.add))
                dve.wait_ge(picked, 4)
                link(dve.tensor_copy(two(g.ew[:, 0:STEPS]), bank[:, 4:6, 0:half]))
                link(dve.tensor_copy(two(g.first[:, 0:STEPS]), bank[:, 6:8, 0:half]))


def prepare_runs(nc, g, sc):
    lanes = PAIR * P
    g.src_key = sc.sb("src_key", [P, PAD])
    g.idx = sc.sb("idx", [P, PAD], I32)
    g.brk = sc.sb("brk", [LOOPS, lanes + 1])
    g.head_run = sc.sb("head_run", [LOOPS, lanes])
    g.tail_run = sc.sb("tail_run", [LOOPS, lanes])
    g.whole_up = sc.sb("whole_up", [HEADS, LOOPS])
    g.whole_down = sc.sb("whole_down", [HEADS, LOOPS])
    g.joint = sc.sb("joint", [HEADS, LOOPS])
    g.acc = sc.sb("acc", [P, WIN, ACCW])
    with Scope(nc) as s1:
        krow = s1.sb("krow", [LOOPS, lanes])
        row_of = s1.sb("row_of", [P, PAD])
        cols = s1.sb("cols", [LOOPS, 3, HEADS])
        edge = s1.sb("edge", [HEADS, 3, LOOPS])
        bank = s1.ps("bank", [128, 8, 512])
        step, turned, cols_ready, cols_turned = (s1.sem(x) for x in ("step", "turned", "cols_ready", "cols_turned"))
        block = s1.block()

        @block.tensor
        def _(pe):
            kv = g.key[:, 0:STEPS].rearrange("p (c b) -> p c b", b=PAIR)
            for b in range(PAIR):
                ins = pe.transpose(bank[0:LOOPS, b // 4, (b % 4) * P:(b % 4 + 1) * P], kv[:, :, b], g.ident[0:P, 0:P])
            ins.then_inc(turned, 1)
            pe.wait_ge(cols_ready, 1)
            for k in range(3):
                ins = pe.transpose(bank[0:HEADS, 2 + k, 0:LOOPS], cols[:, k, :], g.ident[0:LOOPS, 0:LOOPS])
            ins.then_inc(cols_turned, 1)

        @block.vector
        def _(dve):
            link = Link(dve, step)
            link(dve.tensor_scalar(row_of[:, :], g.src_unit[:, :], 1.0, float(SIDE), ALU.is_gt, ALU.mult))
            link(dve.tensor_tensor(row_of[:, :], row_of[:, :], g.src_lo[:, :], ALU.add))
            link(dve.tensor_scalar(g.src_key[:, :], row_of[:, :], -float(N // 2), None, ALU.add))
            link(dve.tensor_scalar(row_of[:, :], row_of[:, :], 0.0, None, ALU.max))
            link(dve.tensor_copy(g.idx[:, :], row_of[:, :]))
            dve.wait_ge(turned, 1)
            link(dve.tensor_scalar(g.key[:, :], g.key[:, :], 0.0, None, ALU.max))
            link(dve.tensor_copy(krow[:, :].rearrange("p (a l) -> p a l", a=2), bank[0:LOOPS, 0:2, 0:4 * P]))
            link(dve.memset(g.brk[:, :], 0.0))
            link(dve.tensor_tensor(g.brk[:, 1:lanes], krow[:, 1:lanes], krow[:, 0:lanes - 1], ALU.not_equal))
            link(dve.tensor_scalar(g.brk[:, 1:lanes], g.brk[:, 1:lanes], -BIG, None, ALU.mult))
            link(dve.tensor_tensor_scan(g.head_run[:, :], g.brk[:, 0:lanes], g.brk[:, 0:lanes], 0.0, ALU.min, ALU.min))
            back = g.brk[:, 1:lanes + 1][:, ::-1]
            link(dve.tensor_tensor_scan(g.tail_run[:, ::-1], back, back, 0.0, ALU.min, ALU.min))
            for k, c in enumerate((krow[:, 0:1], krow[:, lanes - 1:lanes], g.head_run[:, lanes - 1:lanes])):
                link(dve.tensor_copy(cols[:, k, :], c.to_broadcast([LOOPS, HEADS])))
            dve.sem_inc(cols_ready, 1)
            dve.wait_ge(cols_turned, 1)
            link(dve.tensor_copy(edge[:, :, :], bank[0:HEADS, 2:5, 0:LOOPS]))
            link(dve.memset(g.joint[:, :], -BIG))
            link(dve.tensor_tensor(g.joint[:, 1:LOOPS], edge[:, 0, 1:LOOPS], edge[:, 1, 0:LOOPS - 1], ALU.not_equal))
            link(dve.tensor_scalar(g.joint[:, 1:LOOPS], g.joint[:, 1:LOOPS], -BIG, None, ALU.mult))
            link(dve.tensor_tensor(g.whole_up[:, :], g.joint[:, :], edge[:, 2, :], ALU.add))
            link(dve.memset(g.whole_down[:, :], -BIG))
            link(dve.tensor_tensor(g.whole_down[:, 0:LOOPS - 1], g.joint[:, 1:LOOPS], edge[:, 2, 0:LOOPS - 1], ALU.add))



def by_window(table):
    return table.rearrange("(w p) f -> p w f", p=P)


def column(v):
    return v.rearrange("(f a) -> f a", a=1)


def layer0(nc, g, a, x, table, pairs):
    with Scope(nc) as sc:
        cur = sc.sb("cur", [P, WIN, D])
        ft = sc.sb("ft", [128, N])
        ht = sc.sb("ht", [128, N])
        w1 = sc.sb("w1", [128, 3, D])
        w2 = sc.sb("w2", [128, 3, D])
        cols = sc.sb("cols", [128, 3, 4])
        loads = [(w1[:, :, :], a["L0_gnn_W1"].rearrange("l i o -> i l o")), (w2[:, :, :], a["L0_gnn_W2"].rearrange("l i o -> i l o"))]
        for i in range(3):
            for k, n in enumerate(("b1", "b2", "gamma", "beta")):
                loads.append((cols[:, i, k:k + 1], column(a[f"L0_gnn_{n}"][i, :])))
        load(nc, loads)
        to_features(nc, g.ident, x, D, ht)
        for i in range(3):
            sums_to_sources(nc, g, table, pairs, x if i == 0 else cur, ft, plus=ht)
            linear_features(nc, ft[:, :], w1[:, i, :], ACT.Relu, cols[:, i, 0:1], ht)
            linear_features(nc, ht[:, :], w2[:, i, :], ACT.Identity, cols[:, i, 1:2], ft)
            with Scope(nc) as s1:
                std, gain = s1.sb("std", [128, 1]), s1.sb("gain", [128, 1])
                stats = s1.sb("stats", [128, GROUPS, 6])
                moments = s1.sb("moments", [128, 2])
                step, stats_ready, var_ready, std_ready = (s1.sem(k) for k in ("step", "stats_ready", "var_ready", "std_ready"))
                block = s1.block()

                @block.vector
                def _(dve):
                    link = Link(dve, step)
                    for k in range(GROUPS):
                        dve.bn_stats(stats[:, k, :], ft[:, 4 * k * P:4 * k * P + span(k)]).then_inc(stats_ready, 1)
                    dve.wait_ge(stats_ready, GROUPS)
                    dve.bn_aggr(moments[:, :], stats[:, :, :].rearrange("p k s -> p (k s)")).then_inc(var_ready, 1)
                    dve.wait_ge(var_ready, 1)
                    link(dve.tensor_scalar(ht[:, :], ft[:, :], moments[:, 0:1], None, ALU.subtract))
                    dve.wait_ge(std_ready, 1)
                    link(dve.reciprocal(gain[:, :], std[:, :]))
                    link(dve.tensor_tensor(gain[:, :], gain[:, :], cols[:, i, 2:3], ALU.mult))
                    link(dve.tensor_scalar(ht[:, :], ht[:, :], gain[:, :], cols[:, i, 3:4], ALU.mult, ALU.add))

                @block.scalar
                def _(act):
                    act.wait_ge(var_ready, 1)
                    act.activation(std[:, :], moments[:, 1:2], ACT.Sqrt, bias=g.eps[:, :]).then_inc(std_ready, 1)
            to_nodes(nc, g.ident, ht, cur)
        normalize(nc, x[:, :, :], g.eps, before=lambda dve, link: link(dve.tensor_tensor(x[:, :, :], x[:, :, :], cur[:, :, :], ALU.add)))


def layer1(nc, g, a, x, table, spill):
    with Scope(nc) as sc:
        h = sc.sb("h", [P, WIN, D])
        ft = sc.sb("ft", [128, N])
        xr = sc.sb("xr", [P, WIN, D])
        xl = sc.sb("xl", [P, WIN, D + HEADS])
        win = sc.sb("win", [128, HID])
        wout = sc.sb("wout", [128, D])
        bin_ = sc.sb("bin", [HID, 1])
        bout = sc.sb("bout", [P, D])
        load(nc, [(win[:, :], a["L1_gnn_W_in"]), (wout[:, :], a["L1_gnn_W_out"]), (bin_[:, :], column(a["L1_gnn_b_in"])),
                  (bout[:, :], a["L1_gnn_b_out"].partition_broadcast(P))])
        to_features(nc, g.ident, x, D, ft)
        with Scope(nc) as s1:
            f0 = s1.sb("f0", [HID, N])
            linear_features(nc, ft[:, :], win[:, :], ACT.Gelu, bin_[:, :], f0)
            vector_steps(nc, lambda dve, link: link(dve.tensor_copy(ft[0:HID, :], f0[:, :])))
        for i in range(3):
            k = HID if i == 0 else D
            with Scope(nc) as s1:
                wl = s1.sb("wl", [k, D])
                wr = s1.sb("wr", [k, D])
                row = s1.sb("row", [P, 6, D])
                logit = s1.sb("logit", [P, STEPS, HEADS])
                capped = s1.sb("capped", [P, STEPS, HEADS])
                ls = s1.sb("ls", [P, WIN, HEADS])
                names = [a[f"L1_gnn_{n}{i}"] for n in ("bl", "br", "att", "bo", "g", "be")]
                names[2] = names[2].rearrange("h c -> (h c)")
                load(nc, [(wl[:, :], a[f"L1_gnn_Wl{i}"]), (wr[:, :], a[f"L1_gnn_Wr{i}"])]
                     + [(row[:, n, :], v.partition_broadcast(P)) for n, v in enumerate(names)])
                bl, br, att, bo, gain, shift = (row[:, n, :] for n in range(6))
                linear_nodes(nc, [(ft[0:k, :], wl[:, :])], bl, xl)
                linear_nodes(nc, [(ft[0:k, :], wr[:, :])], br, xr)
                load(nc, [(by_window(table), xr[:, :, :])])
                attention_logits(nc, g, table, xl, xr, att, spill, ls, logit, capped)
                softmax_weights(nc, g, logit, capped, capped)
                attention_sums(nc, g, spill, logit, capped)
                with Scope(nc) as s2:
                    m = s2.sb("m", [P, WIN, HEADS])
                    some = s2.sb("some", [P, WIN])
                    es = s2.sb("es", [P, WIN, HEADS])
                    step, shifted, exped = s2.sem("step"), s2.sem("shifted"), s2.sem("exped")
                    block = s2.block()
                    heads = lambda t: t.rearrange("p w (h c) -> p w h c", h=HEADS)
                    over = lambda t: t.unsqueeze(3).broadcast_to([P, WIN, HEADS, HID])

                    @block.vector
                    def _(dve):
                        link = Link(dve, step)
                        link(dve.tensor_scalar(some[:, :].unsqueeze(2), g.acc[:, :, ACCW - 1:ACCW], 0.0, -BIG, ALU.is_equal, ALU.mult))
                        link(dve.tensor_tensor(m[:, :, :], g.acc[:, :, D + HEADS:ACCW - 1], each(some[:, :], HEADS), ALU.add))
                        link(dve.tensor_tensor(m[:, :, :], m[:, :, :], ls[:, :, :], ALU.max))
                        dve.tensor_tensor(m[:, :, :], ls[:, :, :], m[:, :, :], ALU.subtract).then_inc(shifted, 1)
                        dve.wait_ge(exped, 1)
                        link(dve.tensor_tensor(heads(xr[:, :, :]), heads(xr[:, :, :]), over(es[:, :, :]), ALU.mult))
                        link(dve.tensor_tensor(xr[:, :, :], xr[:, :, :], g.acc[:, :, 0:D], ALU.add))
                        link(dve.tensor_tensor(m[:, :, :], es[:, :, :], g.acc[:, :, D:D + HEADS], ALU.add))
                        link(dve.tensor_scalar(m[:, :, :], m[:, :, :], 1e-16, None, ALU.add))
                        link(dve.reciprocal(m[:, :, :], m[:, :, :]))
                        link(dve.tensor_tensor(heads(xr[:, :, :]), heads(xr[:, :, :]), over(m[:, :, :]), ALU.mult))
                        link(dve.tensor_tensor(xr[:, :, :], xr[:, :, :], rows_of(bo, WIN), ALU.add))

                    @block.scalar
                    def _(act):
                        act.wait_ge(shifted, 1)
                        act.activation(es[:, :, :], m[:, :, :], ACT.Exp).then_inc(exped, 1)
                def keep(dve, link):
                    if i == 0:
                        link(dve.tensor_copy(h[:, :, :], xr[:, :, :]))
                    else:
                        link(dve.tensor_tensor(h[:, :, :], h[:, :, :], xr[:, :, :], ALU.add))

                normalize(nc, xr[:, :, :], g.eps, gain=gain, shift=shift, func=ACT.Gelu, after=keep)
                to_features(nc, g.ident, h, D, ft)
        linear_nodes(nc, [(ft[:, :], wout[:, :])], bout[:, :], h)
        with Scope(nc) as s1:
            sq = s1.sb("sq", [P, WIN, D])
            length = s1.sb("length", [P, WIN])
            root = s1.sb("root", [P, WIN])
            step, summed, rooted = s1.sem("step"), s1.sem("summed"), s1.sem("rooted")
            block = s1.block()

            @block.vector
            def _(dve):
                link = Link(dve, step)
                link(dve.tensor_tensor(sq[:, :, :], h[:, :, :], h[:, :, :], ALU.mult))
                dve.tensor_reduce(length[:, :], sq[:, :, :], AX_X, ALU.add).then_inc(summed, 1)
                dve.wait_ge(rooted, 1)
                link(dve.tensor_scalar(root[:, :], root[:, :], 1e-12, None, ALU.max))
                link(dve.reciprocal(root[:, :], root[:, :]))
                link(dve.tensor_tensor(h[:, :, :], h[:, :, :], each(root[:, :], D), ALU.mult))

            @block.scalar
            def _(act):
                act.wait_ge(summed, 1)
                act.activation(root[:, :], length[:, :], ACT.Sqrt).then_inc(rooted, 1)
        normalize(nc, x[:, :, :], g.eps, before=lambda dve, link: link(dve.tensor_tensor(x[:, :, :], x[:, :, :], h[:, :, :], ALU.add)))


def layer2(nc, g, a, x, table, pairs, source_weight):
    low = HYPER // P
    with Scope(nc) as sc:
        dv = sc.sb("dv", [P, WIN])
        y = sc.sb("y", [P, WIN, D])
        he = sc.sb("he", [P, WIN, D])
        hw = sc.sb("hw", [P, low + 1])
        de = sc.sb("de", [P, low])
        ft = sc.sb("ft", [128, N])
        w = sc.sb("w", [128, D])
        wt = sc.sb("wt", [128, D])
        last = sc.sb("last", [P, P])
        bias = sc.sb("bias", [P, D])
        load(nc, [(hw[:, 0:low], a["L2_gnn_hyperedge_weight"].rearrange("(w p) -> p w", p=P)), (w[:, :], a["L2_gnn_W"]),
                  (hw[:, low:low + 1], a["L2_gnn_hyperedge_weight"][HYPER - 1:HYPER].partition_broadcast(P)),
                  (bias[:, :], a["L2_gnn_b"].partition_broadcast(P)), (ft[0:3, :], source_weight[:, 0:N])])

        def look_up(dve, link):
            link(dve.memset(he[:, :, :], 0.0))
            link(dve.tensor_copy(he[:, 0:low, 0:1], hw[:, 0:low].unsqueeze(2)))
            link(dve.tensor_copy(he[:, low:WIN, 0:1], rows_of(hw[:, low:low + 1], WIN - low)))

        vector_steps(nc, look_up)
        scatter_to_sources(nc, g, table, he, ft, None)
        with Scope(nc) as s1:
            root = s1.sb("root", [P, WIN])
            turn = s1.ps("turn", [128, 512])
            parts = s1.ps("parts", [P, WIN, 4])
            step, parted, clipped, rooted, turned = (s1.sem(k) for k in ("step", "parted", "clipped", "rooted", "turned"))
            block = s1.block()

            @block.tensor
            def _(pe):
                for v in range(WIN):
                    ins = pe.transpose(parts[:, v, 0:3], ft[0:3, v * P:(v + 1) * P], g.ident[0:3, 0:3])
                ins.then_inc(parted, 1)
                pe.transpose(turn[:, 0:D], w[:, :], g.ident[:, :]).then_inc(turned, 1)

            @block.vector
            def _(dve):
                link = Link(dve, step)
                dve.wait_ge(parted, 1)
                link(dve.tensor_reduce(dv[:, :], parts[:, :, 0:3], AX_X, ALU.add))
                dve.tensor_scalar(dv[:, :], dv[:, :], 1.0, None, ALU.max).then_inc(clipped, 1)
                dve.wait_ge(rooted, 1)
                link(dve.reciprocal(dv[:, :], root[:, :]))
                link(dve.tensor_tensor(y[:, :, :], x[:, :, :], each(dv[:, :], D), ALU.mult))
                link(dve.tensor_copy(last[:, :], g.ident[0:P, P - 1:P].to_broadcast([P, P])))
                dve.wait_ge(turned, 1)
                link(dve.tensor_copy(wt[:, :], turn[:, 0:D]))

            @block.scalar
            def _(act):
                act.wait_ge(clipped, 1)
                act.activation(root[:, :], dv[:, :], ACT.Sqrt).then_inc(rooted, 1)
        sums_to_hyperedges(nc, g, table, pairs, y)

        def hyperedges(dve, link):
            link(dve.tensor_scalar(de[:, :].unsqueeze(2), g.acc[:, 0:low, D:D + 1], 1.0, None, ALU.max))
            link(dve.reciprocal(de[:, :], de[:, :]))
            link(dve.tensor_tensor(de[:, :], de[:, :], hw[:, 0:low], ALU.mult))
            link(dve.tensor_tensor(he[:, 0:low, :], g.acc[:, 0:low, 0:D], each(de[:, :], D), ALU.mult))

        vector_steps(nc, hyperedges)
        with Scope(nc) as s1:
            row = s1.ps("row", [P, 512])
            taken = s1.sem("taken")
            block = s1.block()

            @block.tensor
            def _(pe):
                pe.matmul(row[:, 0:D], last[:, :], he[:, low - 1, :], start=True, stop=True).then_inc(taken, 1)

            @block.vector
            def _(dve):
                dve.wait_ge(taken, 1)
                dve.tensor_copy(he[:, low:WIN, :], rows_of(row[:, 0:D], WIN - low))

        sums_to_sources(nc, g, table, pairs, he, ft)
        linear_nodes(nc, [(ft[:, :], wt[:, :])], None, y)

        def scale(dve, link):
            link(dve.tensor_tensor(y[:, :, :], y[:, :, :], each(dv[:, :], D), ALU.mult))
            link(dve.tensor_tensor(y[:, :, :], y[:, :, :], rows_of(bias[:, :], WIN), ALU.add))
            link(dve.tensor_tensor(x[:, :, :], x[:, :, :], y[:, :, :], ALU.add))

        normalize(nc, x[:, :, :], g.eps, before=scale)


def layer3(nc, g, a, x, table):
    with Scope(nc) as sc:
        ft = sc.sb("ft", [128, N])
        at = sc.sb("at", [128, N])
        pa = sc.sb("pa", [P, WIN, D])
        pb = sc.sb("pb", [P + 1, WIN, D])
        m1 = sc.sb("m1", [128, 2, D])
        u1 = sc.sb("u1", [128, 2, D])
        m2 = sc.sb("m2", [128, D])
        u2 = sc.sb("u2", [128, D])
        row = sc.sb("row", [P, 6, D])
        n3 = lambda n: a[f"L3_gnn_{n}"]
        rows = [n3("mb1"), n3("mb2"), n3("ub1"), n3("ln_g"), n3("ln_b"), n3("ub2")]
        load(nc, [(m1[:, :, :], n3("mW1")[0:2 * D, :].rearrange("(b i) o -> i b o", b=2)),
                  (u1[:, :, :], n3("uW1").rearrange("(b i) o -> i b o", b=2)), (m2[:, :], n3("mW2")), (u2[:, :], n3("uW2"))]
             + [(row[:, n, :], v.partition_broadcast(P)) for n, v in enumerate(rows)])
        mb1, mb2, ub1, ln_g, ln_b, ub2 = (row[:, n, :] for n in range(6))
        to_features(nc, g.ident, x, D, ft)
        linear_nodes(nc, [(ft[:, :], m1[:, 0, :])], None, pa)
        linear_nodes(nc, [(ft[:, :], m1[:, 1, :])], mb1, pb[0:P, :, :])
        load(nc, [(by_window(table), pa[:, :, :])] 
             + [(pb[P:P + 1, :, :], n3("mW1")[2 * D:2 * D + 1, :].unsqueeze(1).broadcast_to([1, WIN, D]))])
        message_sums(nc, g, table, pb)
        to_features(nc, g.ident, g.acc, D, at)
        linear_nodes(nc, [(at[:, :], m2[:, :])], None, pa)

        def bias(dve, link):
            link(dve.tensor_tensor(pb[0:P, :, :], rows_of(mb2, WIN), g.acc[:, :, D:D + 1].broadcast_to([P, WIN, D]), ALU.mult))
            link(dve.tensor_tensor(pa[:, :, :], pa[:, :, :], pb[0:P, :, :], ALU.add))

        vector_steps(nc, bias)
        to_features(nc, g.ident, pa, D, at)
        linear_nodes(nc, [(ft[:, :], u1[:, 0, :]), (at[:, :], u1[:, 1, :])], ub1, pa)
        normalize(nc, pa[:, :, :], g.eps, gain=ln_g, shift=ln_b, func=ACT.Silu)
        to_features(nc, g.ident, pa, D, at)
        linear_nodes(nc, [(at[:, :], u2[:, :])], ub2, pa)

        def residual(dve, link):
            link(dve.scalar_tensor_tensor(out=x[:, :, :], in0=x[:, :, :], scalar=2.0, in1=pa[:, :, :], op0=ALU.mult, op1=ALU.add))

        normalize(nc, x[:, :, :], g.eps, before=residual)


def program(nc, a, out, upto=4):
    table = nc.dram_tensor("node_table", (N, D), F32, kind="Internal").ap()
    spill = nc.dram_tensor("gathered", (2 * LOOPS, P, HALF * D), F32, kind="Internal").ap()
    pairs = nc.dram_tensor("pairs", (WIN, P, 2 * SIDE), BF16, kind="Internal").ap()
    source_weight = nc.dram_tensor("source_weight", (3, 2 * SIDE), F32, kind="Internal").ap()
    g = Graph()
    with Scope(nc) as sc:
        prepare(nc, g, sc, a["src"], a["dst"], a["edge_weight"])
        count_pairs(nc, g, pairs, a["L2_gnn_hyperedge_weight"], source_weight)
        prepare_runs(nc, g, sc)
        x = sc.sb("x", [P, WIN, D])
        load(nc, [(x[:, :, :], by_window(a["x"]))])
        with Scope(nc) as s1:
            layer0(nc, g, a, x, table, pairs)
        if upto >= 2:
            layer1(nc, g, a, x, table, spill)
        if upto >= 3:
            layer2(nc, g, a, x, table, pairs, source_weight)
        if upto >= 4:
            layer3(nc, g, a, x, table)
        load(nc, [(by_window(out), x[:, :, :])])


_INS = ['x', 'src', 'dst', 'edge_weight'] + [f'L0_gnn_{n}' for n in ('W1', 'b1', 'W2', 'b2', 'gamma', 'beta')] + [
    'L1_gnn_W_in', 'L1_gnn_b_in'] + [f'L1_gnn_{n}{i}' for i in range(3) for n in ('Wl', 'bl', 'Wr', 'br', 'att', 'bo', 'g', 'be')] + [
    'L1_gnn_W_out', 'L1_gnn_b_out', 'L2_gnn_hyperedge_weight', 'L2_gnn_W', 'L2_gnn_b'] + [
    f'L3_gnn_{n}' for n in ('mW1', 'mb1', 'mW2', 'mb2', 'uW1', 'ub1', 'ln_g', 'ln_b', 'uW2', 'ub2')]


def kernel(**inputs):
    import numpy as _np
    import concourse.bacc as _bacc
    from concourse.bass_utils import run_bass_kernel_spmd as _run

    nc = _bacc.Bacc("TRN2", target_bir_lowering=False, num_devices=1)
    arrays, args = {}, {}
    for name in _INS:
        v = _np.ascontiguousarray(inputs[name])
        arrays[f"in_{name}"] = v
        args[name] = nc.dram_tensor(f"in_{name}", v.shape, mybir.dt.from_np(v.dtype), kind="ExternalInput").ap()
    out = nc.dram_tensor("out", (N, D), F32, kind="ExternalOutput").ap()
    program(nc, args, out)
    r = _run(nc, [arrays], core_ids=[0])
    return r.results[0]["out"]
```
